# Optimizing a Trainium2 kernel written in Bass

```python
import numpy as np
import jax
import jax.numpy as jnp

def _softmax(x, axis=-1):
    return jax.nn.softmax(x, axis=axis)

def _gelu(x):
    return jax.nn.gelu(x, approximate=True)

def _silu(x):
    return jax.nn.silu(x)

def _sigmoid(x):
    return jax.nn.sigmoid(x)

def _layernorm(x, axis=-1, eps=1e-05):
    m = jnp.mean(x, axis=axis, keepdims=True)
    v = jnp.var(x, axis=axis, keepdims=True)
    return (x - m) / jnp.sqrt(v + eps)

def _scatter_add(tgt, idx, src, axis=0):
    return tgt.at[idx].add(src)

def _segment_sum(src, seg, n):
    return jax.ops.segment_sum(src, seg, n)
kernel_name = 'mk_gnn_ffn_d4_gnn_r32_854a38'

def setup_inputs(seed: int=0):
    np.random.seed(seed)
    _w = jnp.asarray

    def _rec_inputs():
        import jax
        import jax.numpy as jnp
        _gk = jax.random.key(seed)
        x = -0.0003713 + 1 * jax.random.normal(jax.random.fold_in(_gk, 1), (3125, 256), jnp.float32)
        _s = jax.random.randint(jax.random.fold_in(_gk, 2), (25000,), 0, 3125, jnp.int32)
        _d = jax.random.randint(jax.random.fold_in(_gk, 3), (25000,), 0, 3125, jnp.int32)
        _loop = jnp.arange(3125, dtype=jnp.int32)
        src = jnp.concatenate([_s, _d, _loop])
        dst = jnp.concatenate([_d, _s, _loop])
        _o = jnp.argsort(dst, stable=True)
        src = src[_o]
        dst = dst[_o]
        edge_attr_2 = -0.000414295 + 0.999828 * jax.random.normal(jax.random.fold_in(_gk, 13), (53125, 2), jnp.float32)
        node_vec1 = jax.random.uniform(jax.random.fold_in(_gk, 15), (3125, 1), jnp.float32, 0.0, 0.999957)
        return (x, src, dst, edge_attr_2, node_vec1)
    x, src, dst, edge_attr_2, node_vec1 = _rec_inputs()

    def _L0_gnn_setup():
        import jax, jax.numpy as jnp
        import numpy as np
        N = 50000
        E = 12500
        D_IN = 256
        D_HID = 256
        D_OUT = 256

        def _sage_conv(x, edge_index, W_l, W_r, b):
            src, dst = (edge_index[0], edge_index[1])
            msgs = x[src]
            agg_sum = jax.ops.segment_sum(msgs, dst, num_segments=x.shape[0])
            deg = jax.ops.segment_sum(jnp.ones((edge_index.shape[1],), x.dtype), dst, num_segments=x.shape[0])
            agg = agg_sum / jnp.maximum(deg, 1.0)[:, None]
            return agg @ W_l + x @ W_r + b
        key = jax.random.key(seed)
        ks = jax.random.split(key, 8)
        x = jax.random.normal(ks[0], (N, D_IN), dtype=jnp.float32)
        edge_index = jax.random.randint(ks[1], (2, E), 0, N, dtype=jnp.int64)

        def glorot(k, fan_in, fan_out):
            lim = float(np.sqrt(6.0 / (fan_in + fan_out)))
            return jax.random.uniform(k, (fan_in, fan_out), jnp.float32, -lim, lim)
        return {'x': x, 'edge_index': edge_index, 'W1_l': glorot(ks[2], D_IN, D_HID), 'W1_r': glorot(ks[3], D_IN, D_HID), 'b1': jnp.zeros((D_HID,), jnp.float32), 'W2_l': glorot(ks[4], D_HID, D_OUT), 'W2_r': glorot(ks[5], D_HID, D_OUT), 'b2': jnp.zeros((D_OUT,), jnp.float32)}
    _L0_gnn_all = _L0_gnn_setup()
    _L0_gnn_in = {k: v for k, v in _L0_gnn_all.items() if k in ('W1_l', 'W1_r', 'b1', 'W2_l', 'W2_r', 'b2')}
    del _L0_gnn_all

    def _L0_ffn_setup():
        import jax, jax.numpy as jnp
        import numpy as np
        DIM = 256
        H = 8
        D = 64
        G = 64
        INNER = H * D
        SCALE = D ** (-0.5)
        key = jax.random.key(seed)
        ks = jax.random.split(key, 12)
        B, N = (4, 512)
        x = jax.random.normal(ks[0], (B, N, DIM), dtype=jnp.float32)
        s = lambda fan_in: 1.0 / np.sqrt(fan_in)
        W_fx = jax.random.normal(ks[1], (DIM, INNER), dtype=jnp.float32) * s(DIM)
        b_fx = jnp.zeros((INNER,), dtype=jnp.float32)
        W_x = jax.random.normal(ks[2], (DIM, INNER), dtype=jnp.float32) * s(DIM)
        b_x = jnp.zeros((INNER,), dtype=jnp.float32)
        A = jax.random.normal(ks[3], (G, D), dtype=jnp.float32)
        Q, _ = jnp.linalg.qr(A.T)
        W_slice = Q[:, :G].astype(jnp.float32)
        b_slice = jnp.zeros((G,), dtype=jnp.float32)
        W_q = jax.random.normal(ks[4], (D, D), dtype=jnp.float32) * s(D)
        W_k = jax.random.normal(ks[5], (D, D), dtype=jnp.float32) * s(D)
        W_v = jax.random.normal(ks[6], (D, D), dtype=jnp.float32) * s(D)
        W_out = jax.random.normal(ks[7], (INNER, DIM), dtype=jnp.float32) * s(INNER)
        b_out = jnp.zeros((DIM,), dtype=jnp.float32)
        temperature = jnp.ones((1, H, 1, 1), dtype=jnp.float32) * 0.5
        return {'x': x, 'W_fx': W_fx, 'b_fx': b_fx, 'W_x': W_x, 'b_x': b_x, 'W_slice': W_slice, 'b_slice': b_slice, 'W_q': W_q, 'W_k': W_k, 'W_v': W_v, 'W_out': W_out, 'b_out': b_out, 'temperature': temperature}
    _L0_ffn_all = _L0_ffn_setup()
    _L0_ffn_in = {k: v for k, v in _L0_ffn_all.items() if k in ('W_fx', 'b_fx', 'W_x', 'b_x', 'W_slice', 'b_slice', 'W_q', 'W_k', 'W_v', 'W_out', 'b_out', 'temperature')}
    del _L0_ffn_all

    def _L1_gnn_setup():
        import jax, jax.numpy as jnp
        import numpy as np
        N, E = (50000, 25000)
        IN_C, HID_C, OUT_C = (256, 256, 256)

        def _gcn_prep(edge_index, n_nodes):
            src = jnp.concatenate([edge_index[0], jnp.arange(n_nodes, dtype=edge_index.dtype)])
            dst = jnp.concatenate([edge_index[1], jnp.arange(n_nodes, dtype=edge_index.dtype)])
            deg = jax.ops.segment_sum(jnp.ones_like(dst, dtype=jnp.float32), dst, num_segments=n_nodes)
            deg_inv_sqrt = jnp.where(deg > 0, jax.lax.rsqrt(jnp.maximum(deg, 1.0)), 0.0)
            norm = deg_inv_sqrt[src] * deg_inv_sqrt[dst]
            return (src, dst, norm)

        def _gcn_layer(x, src, dst, norm, W, b, n_nodes):
            h = x @ W
            msg = h[src] * norm[:, None]
            out = jax.ops.segment_sum(msg, dst, num_segments=n_nodes)
            return out + b
        key = jax.random.key(seed)
        ks = jax.random.split(key, 8)
        x_piece = jax.random.normal(ks[0], (N, IN_C), dtype=jnp.float32)
        edge_index_piece = jax.random.randint(ks[1], (2, E), 0, N, dtype=jnp.int64)
        batch = jnp.zeros((N,), dtype=jnp.int64)

        def glorot(k, fan_in, fan_out):
            s = jnp.sqrt(6.0 / (fan_in + fan_out)).astype(jnp.float32)
            return jax.random.uniform(k, (fan_in, fan_out), jnp.float32, -s, s)
        return {'x_piece': x_piece, 'edge_index_piece': edge_index_piece, 'batch': batch, 'W1': glorot(ks[2], IN_C, HID_C), 'b1': jnp.zeros((HID_C,), jnp.float32), 'W2': glorot(ks[3], HID_C, HID_C), 'b2': jnp.zeros((HID_C,), jnp.float32), 'W3': glorot(ks[4], HID_C, OUT_C), 'b3': jnp.zeros((OUT_C,), jnp.float32)}
    _L1_gnn_all = _L1_gnn_setup()
    _L1_gnn_in = {k: v for k, v in _L1_gnn_all.items() if k in ('W1', 'b1', 'W2', 'b2', 'W3', 'b3')}
    del _L1_gnn_all

    def _L1_ffn_setup():
        import jax, jax.numpy as jnp
        import numpy as np
        E = 8
        K = 2
        D = 256
        H = 512
        DOUT = 256
        EPS = 1e-05
        key = jax.random.key(seed)
        ks = jax.random.split(key, 9)
        s = 0.02
        return {'x': jax.random.normal(ks[0], (4, 256, D), jnp.float32), 'gamma': 1.0 + 0.05 * jax.random.normal(ks[1], (D,), jnp.float32), 'beta': 0.05 * jax.random.normal(ks[2], (D,), jnp.float32), 'Wr': 0.01 * jax.random.normal(ks[3], (D, E), jnp.float32), 'br': jnp.zeros((E,), jnp.float32), 'W1': s * jax.random.normal(ks[4], (E, D, H), jnp.float32), 'b1': s * jax.random.normal(ks[5], (E, H), jnp.float32), 'W2': s * jax.random.normal(ks[6], (E, H, DOUT), jnp.float32), 'b2': s * jax.random.normal(ks[7], (E, DOUT), jnp.float32)}
    _L1_ffn_all = _L1_ffn_setup()
    _L1_ffn_in = {k: v for k, v in _L1_ffn_all.items() if k in ('gamma', 'beta', 'Wr', 'br', 'W1', 'b1', 'W2', 'b2')}
    del _L1_ffn_all

    def _L2_gnn_setup():
        import jax, jax.numpy as jnp
        import numpy as np
        N_NODES = 50000
        N_EDGES = 25000
        D = 256
        EPS = 1e-08
        BN_EPS = 1e-05
        key = jax.random.key(seed)
        ks = jax.random.split(key, 11)
        return {'h': jax.random.normal(ks[0], (N_NODES, D), jnp.float32), 'eig': jax.random.normal(ks[1], (N_EDGES, 2), jnp.float32), 'snorm_n': jax.random.uniform(ks[2], (N_NODES, 1), jnp.float32), 'W1': jax.random.normal(ks[3], (2 * D, D), jnp.float32) * (1.0 / np.sqrt(2 * D)), 'b1': jnp.zeros((D,), jnp.float32), 'W2': jax.random.normal(ks[4], (4 * D, D), jnp.float32) * (1.0 / np.sqrt(4 * D)), 'b2': jnp.zeros((D,), jnp.float32), 'gamma': jnp.ones((D,), jnp.float32), 'beta': jnp.zeros((D,), jnp.float32), 'src': jax.random.randint(ks[5], (N_EDGES,), 0, N_NODES, jnp.int64 if jax.config.jax_enable_x64 else jnp.int32), 'dst': jax.random.randint(ks[6], (N_EDGES,), 0, N_NODES, jnp.int64 if jax.config.jax_enable_x64 else jnp.int32)}
    _L2_gnn_all = _L2_gnn_setup()
    _L2_gnn_in = {k: v for k, v in _L2_gnn_all.items() if k in ('W1', 'b1', 'W2', 'b2', 'gamma', 'beta')}
    del _L2_gnn_all

    def _L2_ffn_setup():
        import math
        import jax, jax.numpy as jnp
        import numpy as np
        CAPACITY_FACTOR = 1.25
        TOP_K = 2
        LN_EPS = 1e-05

        def _layer_norm(x, gamma, beta):
            mu = jnp.mean(x, axis=-1, keepdims=True)
            var = jnp.var(x, axis=-1, keepdims=True)
            return (x - mu) * jax.lax.rsqrt(var + LN_EPS) * gamma + beta
        key = jax.random.key(seed)
        ks = jax.random.split(key, 4)
        B, S, D, F, E = (8, 128, 256, 512, 8)
        x = jax.random.normal(ks[0], (B, S, D), dtype=jnp.float32)
        Wr = jax.random.normal(ks[1], (D, E), dtype=jnp.float32) / np.sqrt(D)
        br = jnp.zeros((E,), jnp.float32)
        W1 = jax.random.normal(ks[2], (E, D, F), dtype=jnp.float32) / np.sqrt(D)
        b1 = jnp.zeros((E, F), jnp.float32)
        W2 = jax.random.normal(ks[3], (E, F, D), dtype=jnp.float32) / np.sqrt(F)
        b2 = jnp.zeros((E, D), jnp.float32)
        gamma = jnp.ones((D,), jnp.float32)
        beta = jnp.zeros((D,), jnp.float32)
        return {'x': x, 'Wr': Wr, 'br': br, 'W1': W1, 'b1': b1, 'W2': W2, 'b2': b2, 'gamma': gamma, 'beta': beta}
    _L2_ffn_all = _L2_ffn_setup()
    _L2_ffn_in = {k: v for k, v in _L2_ffn_all.items() if k in ('Wr', 'br', 'W1', 'b1', 'W2', 'b2', 'gamma', 'beta')}
    del _L2_ffn_all

    def _L3_gnn_setup():
        import jax, jax.numpy as jnp
        import numpy as np
        NUM_NODES = 3125
        HIDDEN = 256
        NUM_EDGES = 50000

        def _sage_conv(x, edge_index, w_l, w_r, b):
            src, dst = (edge_index[0], edge_index[1])
            n = x.shape[0]
            nbr_sum = jax.ops.segment_sum(x[src], dst, num_segments=n)
            deg = jax.ops.segment_sum(jnp.ones((src.shape[0],), x.dtype), dst, num_segments=n)
            nbr_mean = nbr_sum / jnp.maximum(deg, 1.0)[:, None]
            return nbr_mean @ w_l.T + x @ w_r.T + b
        key = jax.random.key(seed)
        ks = jax.random.split(key, 8)

        def glorot(k, shape):
            lim = float(np.sqrt(6.0 / (shape[0] + shape[1])))
            return jax.random.uniform(k, shape, jnp.float32, -lim, lim)
        return {'node_features': jax.random.normal(ks[0], (NUM_NODES, HIDDEN), jnp.float32), 'w1_l': glorot(ks[1], (HIDDEN, HIDDEN)), 'w1_r': glorot(ks[2], (HIDDEN, HIDDEN)), 'b1': jnp.zeros((HIDDEN,), jnp.float32), 'w2_l': glorot(ks[3], (HIDDEN, HIDDEN)), 'w2_r': glorot(ks[4], (HIDDEN, HIDDEN)), 'b2': jnp.zeros((HIDDEN,), jnp.float32), 'edge_index': jax.random.randint(ks[5], (2, NUM_EDGES), 0, NUM_NODES, jnp.int64)}
    _L3_gnn_all = _L3_gnn_setup()
    _L3_gnn_in = {k: v for k, v in _L3_gnn_all.items() if k in ('w1_l', 'w1_r', 'b1', 'w2_l', 'w2_r', 'b2')}
    del _L3_gnn_all

    def _L3_ffn_setup():
        import jax, jax.numpy as jnp
        import numpy as np
        BN_EPS = 0.001

        def _bn(h, g, b, m, v):
            return g * (h - m) * jax.lax.rsqrt(v + BN_EPS) + b
        key = jax.random.key(seed)
        ks = jax.random.split(key, 8)
        B, F, Df = (256, 64, 256)
        E, H, D = (8, 256, 256)
        s1 = 1.0 / np.sqrt(Df)
        s2 = 1.0 / np.sqrt(H)
        return {'x': jax.random.normal(ks[0], (B, F, Df), jnp.float32), 'Wr': jax.random.normal(ks[1], (Df, E), jnp.float32) * s1, 'br': jnp.zeros((E,), jnp.float32), 'W1': jax.random.normal(ks[2], (E, Df, H), jnp.float32) * s1, 'b1': jnp.zeros((E, H), jnp.float32), 'g1': jnp.ones((E, H), jnp.float32), 'be1': jnp.zeros((E, H), jnp.float32), 'm1': jnp.zeros((E, H), jnp.float32), 'v1': jnp.ones((E, H), jnp.float32), 'W2': jax.random.normal(ks[3], (E, H, H), jnp.float32) * s2, 'b2': jnp.zeros((E, H), jnp.float32), 'g2': jnp.ones((E, H), jnp.float32), 'be2': jnp.zeros((E, H), jnp.float32), 'm2': jnp.zeros((E, H), jnp.float32), 'v2': jnp.ones((E, H), jnp.float32), 'Wo': jax.random.normal(ks[4], (E, H, D), jnp.float32) * s2, 'bo': jnp.zeros((E, D), jnp.float32)}
    _L3_ffn_all = _L3_ffn_setup()
    _L3_ffn_in = {k: v for k, v in _L3_ffn_all.items() if k in ('Wr', 'br', 'W1', 'b1', 'g1', 'be1', 'm1', 'v1', 'W2', 'b2', 'g2', 'be2', 'm2', 'v2', 'Wo', 'bo')}
    del _L3_ffn_all
    return {'x': x, 'src': src, 'dst': dst, 'edge_attr_2': edge_attr_2, 'node_vec1': node_vec1, 'L0_gnn_W1_l': _L0_gnn_in['W1_l'], 'L0_gnn_W1_r': _L0_gnn_in['W1_r'], 'L0_gnn_b1': _L0_gnn_in['b1'], 'L0_gnn_W2_l': _L0_gnn_in['W2_l'], 'L0_gnn_W2_r': _L0_gnn_in['W2_r'], 'L0_gnn_b2': _L0_gnn_in['b2'], 'L0_ffn_W_fx': _L0_ffn_in['W_fx'], 'L0_ffn_b_fx': _L0_ffn_in['b_fx'], 'L0_ffn_W_x': _L0_ffn_in['W_x'], 'L0_ffn_b_x': _L0_ffn_in['b_x'], 'L0_ffn_W_slice': _L0_ffn_in['W_slice'], 'L0_ffn_b_slice': _L0_ffn_in['b_slice'], 'L0_ffn_W_q': _L0_ffn_in['W_q'], 'L0_ffn_W_k': _L0_ffn_in['W_k'], 'L0_ffn_W_v': _L0_ffn_in['W_v'], 'L0_ffn_W_out': _L0_ffn_in['W_out'], 'L0_ffn_b_out': _L0_ffn_in['b_out'], 'L0_ffn_temperature': _L0_ffn_in['temperature'], 'L1_gnn_W1': _L1_gnn_in['W1'], 'L1_gnn_b1': _L1_gnn_in['b1'], 'L1_gnn_W2': _L1_gnn_in['W2'], 'L1_gnn_b2': _L1_gnn_in['b2'], 'L1_gnn_W3': _L1_gnn_in['W3'], 'L1_gnn_b3': _L1_gnn_in['b3'], 'L1_ffn_gamma': _L1_ffn_in['gamma'], 'L1_ffn_beta': _L1_ffn_in['beta'], 'L1_ffn_Wr': _L1_ffn_in['Wr'], 'L1_ffn_br': _L1_ffn_in['br'], 'L1_ffn_W1': _L1_ffn_in['W1'], 'L1_ffn_b1': _L1_ffn_in['b1'], 'L1_ffn_W2': _L1_ffn_in['W2'], 'L1_ffn_b2': _L1_ffn_in['b2'], 'L2_gnn_W1': _L2_gnn_in['W1'], 'L2_gnn_b1': _L2_gnn_in['b1'], 'L2_gnn_W2': _L2_gnn_in['W2'], 'L2_gnn_b2': _L2_gnn_in['b2'], 'L2_gnn_gamma': _L2_gnn_in['gamma'], 'L2_gnn_beta': _L2_gnn_in['beta'], 'L2_ffn_Wr': _L2_ffn_in['Wr'], 'L2_ffn_br': _L2_ffn_in['br'], 'L2_ffn_W1': _L2_ffn_in['W1'], 'L2_ffn_b1': _L2_ffn_in['b1'], 'L2_ffn_W2': _L2_ffn_in['W2'], 'L2_ffn_b2': _L2_ffn_in['b2'], 'L2_ffn_gamma': _L2_ffn_in['gamma'], 'L2_ffn_beta': _L2_ffn_in['beta'], 'L3_gnn_w1_l': _L3_gnn_in['w1_l'], 'L3_gnn_w1_r': _L3_gnn_in['w1_r'], 'L3_gnn_b1': _L3_gnn_in['b1'], 'L3_gnn_w2_l': _L3_gnn_in['w2_l'], 'L3_gnn_w2_r': _L3_gnn_in['w2_r'], 'L3_gnn_b2': _L3_gnn_in['b2'], 'L3_ffn_Wr': _L3_ffn_in['Wr'], 'L3_ffn_br': _L3_ffn_in['br'], 'L3_ffn_W1': _L3_ffn_in['W1'], 'L3_ffn_b1': _L3_ffn_in['b1'], 'L3_ffn_g1': _L3_ffn_in['g1'], 'L3_ffn_be1': _L3_ffn_in['be1'], 'L3_ffn_m1': _L3_ffn_in['m1'], 'L3_ffn_v1': _L3_ffn_in['v1'], 'L3_ffn_W2': _L3_ffn_in['W2'], 'L3_ffn_b2': _L3_ffn_in['b2'], 'L3_ffn_g2': _L3_ffn_in['g2'], 'L3_ffn_be2': _L3_ffn_in['be2'], 'L3_ffn_m2': _L3_ffn_in['m2'], 'L3_ffn_v2': _L3_ffn_in['v2'], 'L3_ffn_Wo': _L3_ffn_in['Wo'], 'L3_ffn_bo': _L3_ffn_in['bo']}

def reference(x, src, dst, edge_attr_2, node_vec1, L0_gnn_W1_l, L0_gnn_W1_r, L0_gnn_b1, L0_gnn_W2_l, L0_gnn_W2_r, L0_gnn_b2, L0_ffn_W_fx, L0_ffn_b_fx, L0_ffn_W_x, L0_ffn_b_x, L0_ffn_W_slice, L0_ffn_b_slice, L0_ffn_W_q, L0_ffn_W_k, L0_ffn_W_v, L0_ffn_W_out, L0_ffn_b_out, L0_ffn_temperature, L1_gnn_W1, L1_gnn_b1, L1_gnn_W2, L1_gnn_b2, L1_gnn_W3, L1_gnn_b3, L1_ffn_gamma, L1_ffn_beta, L1_ffn_Wr, L1_ffn_br, L1_ffn_W1, L1_ffn_b1, L1_ffn_W2, L1_ffn_b2, L2_gnn_W1, L2_gnn_b1, L2_gnn_W2, L2_gnn_b2, L2_gnn_gamma, L2_gnn_beta, L2_ffn_Wr, L2_ffn_br, L2_ffn_W1, L2_ffn_b1, L2_ffn_W2, L2_ffn_b2, L2_ffn_gamma, L2_ffn_beta, L3_gnn_w1_l, L3_gnn_w1_r, L3_gnn_b1, L3_gnn_w2_l, L3_gnn_w2_r, L3_gnn_b2, L3_ffn_Wr, L3_ffn_br, L3_ffn_W1, L3_ffn_b1, L3_ffn_g1, L3_ffn_be1, L3_ffn_m1, L3_ffn_v1, L3_ffn_W2, L3_ffn_b2, L3_ffn_g2, L3_ffn_be2, L3_ffn_m2, L3_ffn_v2, L3_ffn_Wo, L3_ffn_bo):
    import jax
    import jax.numpy as jnp

    def _L0_gnn_ref(x, edge_index, W1_l, W1_r, b1, W2_l, W2_r, b2):
        import jax, jax.numpy as jnp
        import numpy as np
        N = 50000
        E = 12500
        D_IN = 256
        D_HID = 256
        D_OUT = 256

        def _sage_conv(x, edge_index, W_l, W_r, b):
            src, dst = (edge_index[0], edge_index[1])
            msgs = x[src]
            agg_sum = jax.ops.segment_sum(msgs, dst, num_segments=x.shape[0])
            deg = jax.ops.segment_sum(jnp.ones((edge_index.shape[1],), x.dtype), dst, num_segments=x.shape[0])
            agg = agg_sum / jnp.maximum(deg, 1.0)[:, None]
            return agg @ W_l + x @ W_r + b
        h = _sage_conv(x, edge_index, W1_l, W1_r, b1)
        h = jax.nn.relu(h)
        out = _sage_conv(h, edge_index, W2_l, W2_r, b2)
        return out

    def _L0_ffn_ref(x, W_fx, b_fx, W_x, b_x, W_slice, b_slice, W_q, W_k, W_v, W_out, b_out, temperature):
        import jax, jax.numpy as jnp
        import numpy as np
        DIM = 256
        H = 8
        D = 64
        G = 64
        INNER = H * D
        SCALE = D ** (-0.5)
        B, N, _ = x.shape
        fx_mid = (x @ W_fx + b_fx).reshape(B, N, H, D).transpose(0, 2, 1, 3)
        x_mid = (x @ W_x + b_x).reshape(B, N, H, D).transpose(0, 2, 1, 3)
        temp = jnp.clip(temperature, 0.1, 5.0)
        slice_weights = jax.nn.softmax((x_mid @ W_slice + b_slice) / temp, axis=-1)
        slice_norm = slice_weights.sum(axis=2)
        slice_token = jnp.einsum('bhnc,bhng->bhgc', fx_mid, slice_weights)
        slice_token = slice_token / (slice_norm[..., None] + 1e-05)
        q = slice_token @ W_q
        k = slice_token @ W_k
        v = slice_token @ W_v
        attn = jax.nn.softmax(jnp.einsum('bhgc,bhkc->bhgk', q, k) * SCALE, axis=-1)
        out_slice = jnp.einsum('bhgk,bhkc->bhgc', attn, v)
        out_x = jnp.einsum('bhgc,bhng->bhnc', out_slice, slice_weights)
        out_x = out_x.transpose(0, 2, 1, 3).reshape(B, N, INNER)
        return out_x @ W_out + b_out

    def _L1_gnn_ref(x_piece, edge_index_piece, batch, W1, b1, W2, b2, W3, b3):
        import jax, jax.numpy as jnp
        import numpy as np
        N, E = (50000, 25000)
        IN_C, HID_C, OUT_C = (256, 256, 256)

        def _gcn_prep(edge_index, n_nodes):
            src = jnp.concatenate([edge_index[0], jnp.arange(n_nodes, dtype=edge_index.dtype)])
            dst = jnp.concatenate([edge_index[1], jnp.arange(n_nodes, dtype=edge_index.dtype)])
            deg = jax.ops.segment_sum(jnp.ones_like(dst, dtype=jnp.float32), dst, num_segments=n_nodes)
            deg_inv_sqrt = jnp.where(deg > 0, jax.lax.rsqrt(jnp.maximum(deg, 1.0)), 0.0)
            norm = deg_inv_sqrt[src] * deg_inv_sqrt[dst]
            return (src, dst, norm)

        def _gcn_layer(x, src, dst, norm, W, b, n_nodes):
            h = x @ W
            msg = h[src] * norm[:, None]
            out = jax.ops.segment_sum(msg, dst, num_segments=n_nodes)
            return out + b
        n_nodes = x_piece.shape[0]
        src, dst, norm = _gcn_prep(edge_index_piece, n_nodes)
        x = _gcn_layer(x_piece, src, dst, norm, W1, b1, n_nodes)
        x = jax.nn.gelu(x)
        x = _gcn_layer(x, src, dst, norm, W2, b2, n_nodes)
        x = jax.nn.gelu(x)
        x = _gcn_layer(x, src, dst, norm, W3, b3, n_nodes)
        return x

    def _L1_ffn_ref(x, gamma, beta, Wr, br, W1, b1, W2, b2):
        import jax, jax.numpy as jnp
        import numpy as np
        E = 8
        K = 2
        D = 256
        H = 512
        DOUT = 256
        EPS = 1e-05
        mu = jnp.mean(x, axis=-1, keepdims=True)
        var = jnp.mean(jnp.square(x - mu), axis=-1, keepdims=True)
        xn = (x - mu) * jax.lax.rsqrt(var + EPS) * gamma + beta
        logits = jnp.einsum('bsd,de->bse', xn, Wr) + br
        top_vals, top_idx = jax.lax.top_k(logits, K)
        w = jax.nn.softmax(top_vals, axis=-1)
        w_full = jnp.einsum('bsk,bske->bse', w, jax.nn.one_hot(top_idx, E, dtype=w.dtype))
        y = jnp.zeros(x.shape[:-1] + (DOUT,), x.dtype)
        for e in range(E):
            h = jax.nn.gelu(jnp.einsum('bsd,dh->bsh', xn, W1[e]) + b1[e], approximate=False)
            y_e = jnp.einsum('bsh,hd->bsd', h, W2[e]) + b2[e]
            y = y + y_e * w_full[..., e, None]
        return y

    def _L2_gnn_ref(h, eig, snorm_n, W1, b1, W2, b2, gamma, beta, src, dst):
        import jax, jax.numpy as jnp
        import numpy as np
        N_NODES = 50000
        N_EDGES = 25000
        D = 256
        EPS = 1e-08
        BN_EPS = 1e-05
        n = h.shape[0]
        seg = lambda x: jax.ops.segment_sum(x, dst, num_segments=n)
        z2 = jnp.concatenate([h[src], h[dst]], axis=1)
        e = z2 @ W1 + b1
        deg = seg(jnp.ones((dst.shape[0],), h.dtype))
        mean_agg = seg(e) / jnp.maximum(deg, 1.0)[:, None]
        w = eig[:, 0]
        s = seg(jnp.abs(w)) + EPS
        wn = w / s[dst]
        dir_av = seg(e * jnp.abs(wn)[:, None])
        dir_dx = jnp.abs(seg(e * wn[:, None]) - h)
        hc = jnp.concatenate([h, mean_agg, dir_av, dir_dx], axis=1)
        out = hc @ W2 + b2
        out = out * snorm_n
        mu = out.mean(axis=0)
        var = jnp.mean((out - mu) ** 2, axis=0)
        out = (out - mu) / jnp.sqrt(var + BN_EPS) * gamma + beta
        out = jax.nn.relu(out)
        out = h + out
        return out

    def _L2_ffn_ref(x, Wr, br, W1, b1, W2, b2, gamma, beta):
        import math
        import jax, jax.numpy as jnp
        import numpy as np
        CAPACITY_FACTOR = 1.25
        TOP_K = 2
        LN_EPS = 1e-05

        def _layer_norm(x, gamma, beta):
            mu = jnp.mean(x, axis=-1, keepdims=True)
            var = jnp.var(x, axis=-1, keepdims=True)
            return (x - mu) * jax.lax.rsqrt(var + LN_EPS) * gamma + beta
        B, S, D = x.shape
        E = Wr.shape[1]
        N = B * S
        K = TOP_K
        logits = jnp.mean(x, axis=1) @ Wr + br
        routing_weights = jax.nn.softmax(logits, axis=-1)
        capacity = float(math.ceil(N * CAPACITY_FACTOR / E))
        expected_loads = routing_weights.sum(axis=0) * (N / B)
        scale = jnp.where(expected_loads > capacity, capacity / expected_loads, 1.0)
        routing_weights = jax.nn.softmax(routing_weights * scale, axis=-1)
        rw_tok = jnp.broadcast_to(routing_weights[:, None, :], (B, S, E)).reshape(N, E)
        top_w, top_i = jax.lax.top_k(rw_tok, K)
        top_w = jax.nn.softmax(top_w, axis=-1)
        xf = x.reshape(N, D)
        h = jax.nn.gelu(jnp.einsum('nd,edf->enf', xf, W1) + b1[:, None, :], approximate=False)
        y = jnp.einsum('enf,efd->end', h, W2) + b2[:, None, :]
        w_dense = jnp.zeros((N, E), x.dtype).at[jnp.arange(N)[:, None], top_i].add(top_w)
        out = jnp.einsum('ne,end->nd', w_dense, y).reshape(B, S, D)
        out = _layer_norm(out + x, gamma, beta)
        return out

    def _L3_gnn_ref(node_features, w1_l, w1_r, b1, w2_l, w2_r, b2, edge_index):
        import jax, jax.numpy as jnp
        import numpy as np
        NUM_NODES = 3125
        HIDDEN = 256
        NUM_EDGES = 50000

        def _sage_conv(x, edge_index, w_l, w_r, b):
            src, dst = (edge_index[0], edge_index[1])
            n = x.shape[0]
            nbr_sum = jax.ops.segment_sum(x[src], dst, num_segments=n)
            deg = jax.ops.segment_sum(jnp.ones((src.shape[0],), x.dtype), dst, num_segments=n)
            nbr_mean = nbr_sum / jnp.maximum(deg, 1.0)[:, None]
            return nbr_mean @ w_l.T + x @ w_r.T + b
        h = _sage_conv(node_features, edge_index, w1_l, w1_r, b1)
        h = jax.nn.relu(h)
        out = _sage_conv(h, edge_index, w2_l, w2_r, b2)
        return out

    def _L3_ffn_ref(x, Wr, br, W1, b1, g1, be1, m1, v1, W2, b2, g2, be2, m2, v2, Wo, bo):
        import jax, jax.numpy as jnp
        import numpy as np
        BN_EPS = 0.001

        def _bn(h, g, b, m, v):
            return g * (h - m) * jax.lax.rsqrt(v + BN_EPS) + b
        feat = jnp.mean(x, axis=0)
        w = jax.nn.softmax(feat @ Wr + br, axis=-1)
        h = jnp.einsum('bfd,edh->bfeh', x, W1) + b1
        h = jax.nn.relu(_bn(h, g1, be1, m1, v1))
        h = jnp.einsum('bfeh,ehk->bfek', h, W2) + b2
        h = jax.nn.relu(_bn(h, g2, be2, m2, v2))
        y = jnp.einsum('bfeh,ehd->bfed', h, Wo) + bo
        return jnp.einsum('bfed,fe->bfd', y, w)
    edge_index = jnp.stack([src, dst])
    batch0 = jnp.zeros((3125,), jnp.int32)
    x = x + _L0_gnn_ref(_layernorm(x, axis=-1), edge_index, L0_gnn_W1_l, L0_gnn_W1_r, L0_gnn_b1, L0_gnn_W2_l, L0_gnn_W2_r, L0_gnn_b2)
    x = x + _L0_ffn_ref(_layernorm(x, axis=-1)[None], L0_ffn_W_fx, L0_ffn_b_fx, L0_ffn_W_x, L0_ffn_b_x, L0_ffn_W_slice, L0_ffn_b_slice, L0_ffn_W_q, L0_ffn_W_k, L0_ffn_W_v, L0_ffn_W_out, L0_ffn_b_out, L0_ffn_temperature)[0]
    x = x + _L1_gnn_ref(_layernorm(x, axis=-1), edge_index, batch0, L1_gnn_W1, L1_gnn_b1, L1_gnn_W2, L1_gnn_b2, L1_gnn_W3, L1_gnn_b3)
    x = x + _L1_ffn_ref(_layernorm(x, axis=-1)[None], L1_ffn_gamma, L1_ffn_beta, L1_ffn_Wr, L1_ffn_br, L1_ffn_W1, L1_ffn_b1, L1_ffn_W2, L1_ffn_b2)[0]
    x = x + _L2_gnn_ref(_layernorm(x, axis=-1), edge_attr_2, node_vec1, L2_gnn_W1, L2_gnn_b1, L2_gnn_W2, L2_gnn_b2, L2_gnn_gamma, L2_gnn_beta, src, dst)
    x = x + _L2_ffn_ref(_layernorm(x, axis=-1)[None], L2_ffn_Wr, L2_ffn_br, L2_ffn_W1, L2_ffn_b1, L2_ffn_W2, L2_ffn_b2, L2_ffn_gamma, L2_ffn_beta)[0]
    x = x + _L3_gnn_ref(_layernorm(x, axis=-1), L3_gnn_w1_l, L3_gnn_w1_r, L3_gnn_b1, L3_gnn_w2_l, L3_gnn_w2_r, L3_gnn_b2, edge_index)
    x = x + _L3_ffn_ref(_layernorm(x, axis=-1)[None], L3_ffn_Wr, L3_ffn_br, L3_ffn_W1, L3_ffn_b1, L3_ffn_g1, L3_ffn_be1, L3_ffn_m1, L3_ffn_v1, L3_ffn_W2, L3_ffn_b2, L3_ffn_g2, L3_ffn_be2, L3_ffn_m2, L3_ffn_v2, L3_ffn_Wo, L3_ffn_bo)[0]
    return x

_drawn_inputs = setup_inputs


def setup_inputs(seed=0):
    import zlib

    import numpy as np

    out = dict(_drawn_inputs(seed))
    spreads = {'L0_gnn_b1': (0.0, 0.1),
     'L0_gnn_b2': (0.0, 0.1),
     'L0_ffn_b_fx': (0.0, 0.1),
     'L0_ffn_b_x': (0.0, 0.8),
     'L0_ffn_b_slice': (0.0, 0.8),
     'L0_ffn_b_out': (0.0, 0.1),
     'L0_ffn_temperature': (0.5, 0.6),
     'L1_gnn_b1': (0.0, 0.323),
     'L1_gnn_b2': (0.0, 0.1),
     'L1_gnn_b3': (0.0, 0.1),
     'L1_ffn_br': (0.0, 0.305),
     'L2_gnn_b1': (0.0, 0.545),
     'L2_gnn_b2': (0.0, 0.485),
     'L2_gnn_gamma': (1.0, 0.2),
     'L2_gnn_beta': (0.0, 0.274),
     'L2_ffn_br': (0.0, 0.1),
     'L2_ffn_b1': (0.0, 0.628),
     'L2_ffn_b2': (0.0, 0.409),
     'L2_ffn_gamma': (1.0, 0.2),
     'L2_ffn_beta': (0.0, 0.271),
     'L3_gnn_b1': (0.0, 0.318),
     'L3_gnn_b2': (0.0, 0.288),
     'L3_ffn_br': (0.0, 0.8),
     'L3_ffn_b1': (0.0, 0.8),
     'L3_ffn_g1': (1.0, 0.6),
     'L3_ffn_be1': (0.0, 0.8),
     'L3_ffn_m1': (0.0, 0.8),
     'L3_ffn_v1': (1.0, 0.6),
     'L3_ffn_b2': (0.0, 0.774),
     'L3_ffn_g2': (1.0, 0.6),
     'L3_ffn_be2': (0.0, 0.8),
     'L3_ffn_m2': (0.0, 0.741),
     'L3_ffn_v2': (1.0, 0.6),
     'L3_ffn_bo': (0.0, 0.564)}
    factors = {'L0_ffn_W_x': 5.416,
     'L0_ffn_W_slice': 6.8,
     'L0_ffn_W_q': 8.0,
     'L0_ffn_W_k': 8.0,
     'L1_ffn_gamma': 8.0,
     'L1_ffn_beta': 6.712,
     'L1_ffn_b1': 8.0,
     'L1_ffn_b2': 5.737}
    for name, (base, spread) in spreads.items():
        noise = np.random.default_rng([zlib.crc32(name.encode()), seed]).standard_normal(out[name].shape)
        drawn = base * np.exp(spread * noise) if base else spread * noise
        out[name] = jnp.asarray(drawn.astype(out[name].dtype))
    for name, factor in factors.items():
        out[name] = (out[name] * factor).astype(out[name].dtype)
    return out
```

```python
from contextlib import ExitStack, contextmanager
from math import ceil

import numpy as np

import concourse.bass as bass
from concourse import mybir

F32 = mybir.dt.float32
I32 = mybir.dt.int32
U32 = mybir.dt.uint32
ALU = mybir.AluOpType
ACT = mybir.ActivationFunctionType
AX = mybir.AxisListType.X
RMAX = bass.bass_isa.ReduceOp.max
ds = bass.ds

N = 3125
D = 256
P = 128
KD = D // P
TP = 125
NT = N // TP
TU = 5
CH = 392
NCH = 8
NP = CH * NCH
WIN = 128
AW = 3264
E = 53125
EG = 416
EU = 16
SLOTS = 8
BANKS = 4
PAD_DST = 1 << 20
NE = 8
H1 = 512
HEADS = 8
G = 64
HG = HEADS * G

LN_EPS = 1e-5

VECS = {}
_at = 0
for _name, _n in [
    ("L0_gnn_b1", 2), ("L0_gnn_b2", 2), ("L0_ffn_b_out", 2), ("L0_ffn_b_x", 4),
    ("L1_gnn_b1", 2), ("L1_gnn_b2", 2), ("L1_gnn_b3", 2),
    ("L1_ffn_gamma", 2), ("L1_ffn_beta", 2), ("L1_ffn_b1", 32),
    ("L2_gnn_b1", 2), ("L2_gnn_b2", 2), ("L2_gnn_gamma", 2), ("L2_gnn_beta", 2),
    ("L2_ffn_gamma", 2), ("L2_ffn_beta", 2),
    ("L3_gnn_b1", 2), ("L3_gnn_b2", 2),
    ("L3_ffn_b1", 16), ("L3_ffn_g1", 16), ("L3_ffn_be1", 16), ("L3_ffn_m1", 16), ("L3_ffn_v1", 16),
    ("L3_ffn_b2", 16), ("L3_ffn_g2", 16), ("L3_ffn_be2", 16), ("L3_ffn_m2", 16), ("L3_ffn_v2", 16),
]:
    VECS[_name] = (_at, _n)
    _at += _n
NVEC = _at


class Machine:

    def __init__(self, nc, stack, ins, out):
        self.nc, self.stack, self.ins, self.out = nc, stack, ins, out
        self.stale = []
        sb = self.sb
        self.xT = sb("residual", [P, KD, NP])
        self.yT = sb("activations", [P, KD, NP])
        self.big = sb("big", [P, 4 * AW + 16384])
        self.degree = sb("degree", [P, AW])
        self.gathered = sb("gathered", [P, SLOTS, D])
        self.onehot = sb("onehot", [P, SLOTS * WIN + 4 * WIN])
        self.src = sb("src", [P, EG], I32)
        self.dst_rel = sb("dst_rel", [P, EG + SLOTS])
        self.edge_w = sb("edge_w", [P, EG + SLOTS])
        self.edge_abs = sb("edge_abs", [P, EG + SLOTS])
        self.base = sb("base", [1, EG], I32)
        self.src_cols = sb("src_cols", [P, 2, SLOTS], I32)
        self.ident = sb("ident", [P, P])
        self.ones = sb("ones", [P, P])
        self.mean_of = sb("mean_of", [P, P])
        self.count = sb("count", [P, WIN])
        self.pick = sb("pick", [NE, NE, P])
        self.vecs = sb("vecs", [P, NVEC])
        self.eps = sb("eps", [P, 2])
        self.small = sb("small", [P, 320])
        self.banks = [stack.enter_context(nc.psum_tensor(f"bank{i}", [P, 512], F32)) for i in range(8)]
        self.fetched = [stack.enter_context(nc.semaphore(f"fetched{s}")) for s in range(SLOTS)]
        self.fetched_before = 0
        self.table = nc.dram_tensor("table", [N, D], F32, kind="Internal").ap()

    def sb(self, name, shape, dt=F32):
        return self.stack.enter_context(self.nc.sbuf_tensor(name, shape, dt))

    def vec(self, name, i=None):
        at, n = VECS[name]
        return self.vecs[:, at:at + n] if i is None else self.vecs[:, at + i:at + i + 1]

    def part(self, at, *shape):
        n = int(np.prod(shape))
        v = self.big[:, at:at + n]
        if len(shape) == 2:
            v = v.rearrange("p (a b) -> p a b", a=shape[0])
        if len(shape) == 3:
            v = v.rearrange("p (a b c) -> p a b c", a=shape[0], b=shape[1])
        return v

    @property
    def sums(self):
        return self.part(0, 6, AW)

    REG = 4 * AW


@contextmanager
def phase(m, *names):
    with ExitStack() as stack:
        sems = [stack.enter_context(m.nc.semaphore(n)) for n in names]
        stale, m.stale = m.stale, sems
        block = stack.enter_context(m.nc.Block())

        @block.sync
        def _(sp):
            for s in stale:
                sp.sem_clear(s)

        yield block, *sems


class Steps:

    def __init__(self, eng, sem):
        self.eng, self.sem, self.n = eng, sem, 0

    def __call__(self, ins):
        ins.then_inc(self.sem, 1)
        self.n += 1
        self.eng.wait_ge(self.sem, self.n)


def tile_at(i, u, width, per):
    return ds(i * (width * per) + u * width, width)


def setup(m):
    nc, ins = m.nc, m.ins
    dst = m.part(0, EG).bitcast(I32)
    neg = m.part(EG, EG)
    neg_base = m.part(2 * EG, EG)
    dst_f = m.part(3 * EG, EG)
    iota_i = m.part(4 * EG, WIN).bitcast(I32)
    base_f = m.part(5 * EG, EG)
    with phase(m, "loaded", "pool_step", "dst_ready", "base_ready", "dve_step") as \
            (block, loaded, pool_step, dst_ready, base_ready, dve_step):

        @block.sync
        def _(sp):
            sp.dma_start(dst, ins["dst"]).then_inc(loaded, 16)
            sp.dma_start(m.src[:, :], ins["src"]).then_inc(loaded, 16)
            sp.dma_start(m.edge_w[:, 0:EG], ins["edge_w"]).then_inc(loaded, 16)
            sp.dma_start(m.vecs[:, :], ins["vecs"]).then_inc(loaded, 16)
            sp.wait_ge(loaded, 64)

        @block.gpsimd
        def _(pool):
            step = Steps(pool, pool_step)
            nc.gpsimd.memset(m.ones[:, :], 1.0)
            nc.gpsimd.memset(m.mean_of[:, :], 1.0 / D)
            nc.gpsimd.memset(m.eps[:, 0:1], LN_EPS)
            nc.gpsimd.memset(m.eps[:, 1:2], 1e-3)
            nc.gpsimd.memset(m.pick[:, :, :], 1.0)
            nc.gpsimd.memset(m.xT[:, :, N:NP], 0.0)
            nc.gpsimd.memset(m.dst_rel[:, EG:], 0.0)
            nc.gpsimd.memset(m.edge_w[:, EG:], 0.0)
            step(nc.gpsimd.iota(iota_i, [[1, WIN]], base=0, channel_multiplier=0))
            nc.gpsimd.tensor_copy(m.count[:, :], iota_i)
            nc.gpsimd.affine_select(m.ident[:, :], m.ones[:, :], [[1, P]], ALU.is_equal, 0.0,
                                    base=0, channel_multiplier=-1)
            step(nc.gpsimd.affine_select(m.pick[:, :, :], m.pick[:, :, :], [[1, NE], [0, P]],
                                         ALU.is_equal, 0.0, base=0, channel_multiplier=-1))
            pool.wait_ge(dst_ready, 1)
            nc.gpsimd.partition_all_reduce(neg_base, neg, P, RMAX).then_inc(base_ready, 1)

        @block.scalar
        def _(act):
            act.wait_ge(loaded, 64)
            act.wait_ge(pool_step, 1)
            nc.scalar.activation(m.edge_abs[:, :], m.edge_w[:, :], ACT.Abs)

        @block.vector
        def _(dve):
            step = Steps(dve, dve_step)
            dve.wait_ge(loaded, 64)
            step(nc.vector.tensor_copy(dst_f, dst))
            dve.wait_ge(pool_step, 1)
            nc.vector.tensor_scalar(neg, dst_f, -1.0, None, ALU.mult).then_inc(dst_ready, 1)
            dve.wait_ge(base_ready, 1)
            nc.vector.tensor_tensor(m.dst_rel[:, 0:EG], dst_f, neg_base, ALU.add)
            step(nc.vector.tensor_scalar(base_f[0:1, :], neg_base[0:1, :], -1.0, None, ALU.mult))
            step(nc.vector.tensor_copy(m.base[:, :], base_f[0:1, :]))


def load_rows(m, rows, to):
    nc = m.nc
    stage = m.part(0, TU, D)
    with phase(m, "row_free", "transposed", *[f"row_loaded{u}" for u in range(TU)], "evacuated") as \
            (block, row_free, transposed, *row_loaded, evacuated):

        @block.sync
        def _(sp):
            with sp.Fori(0, NT // TU) as i:
                for u in range(TU):
                    sp.wait_ge(transposed, i * TU + u + 1)
                    sp.dma_start(stage[0:TP, u, :], rows[ds(i * (TU * TP) + u * TP, TP), :])\
                        .then_inc(row_loaded[u], 16)

        @block.tensor
        def _(pe):
            pe.sem_inc(transposed, TU)
            with pe.Fori(0, NT // TU) as i:
                for u in range(TU):
                    pe.wait_ge(row_loaded[u], i * 16 + 16)
                    pe.wait_ge(evacuated, i * TU + u + 1)
                    for k in range(KD):
                        last = nc.tensor.transpose(m.banks[u][:, k * TP:(k + 1) * TP],
                                                   stage[0:TP, u, k * P:(k + 1) * P], m.ident[0:TP, 0:TP])
                    last.then_inc(transposed, 1)

        @block.vector
        def _(dve):
            dve.sem_inc(evacuated, TU)
            with dve.Fori(0, NT // TU) as i:
                for u in range(TU):
                    dve.wait_ge(transposed, i * TU + u + 1 + TU)
                    nc.vector.tensor_copy(to[:, :, tile_at(i, u, TP, TU)],
                                          m.banks[u][:, 0:KD * TP].rearrange("p (k n) -> p k n", k=KD))\
                        .then_inc(evacuated, 1)


def store_rows(m, of, rows):
    nc = m.nc
    cols = m.part(0, TU, KD, TP)
    tile = m.part(TU * KD * TP, TU, D)
    with phase(m, "staged", "transposed", *[f"row_stored{u}" for u in range(TU)], "evacuated") as \
            (block, staged, transposed, *row_stored, evacuated):

        @block.scalar
        def _(act):
            with act.Fori(0, NT // TU) as i:
                for u in range(TU):
                    act.wait_ge(transposed, i * TU + u + 1)
                    nc.scalar.copy(cols[:, u, :, :], of[:, :, tile_at(i, u, TP, TU)]).then_inc(staged, 1)

        @block.tensor
        def _(pe):
            pe.sem_inc(transposed, TU)
            with pe.Fori(0, NT // TU) as i:
                for u in range(TU):
                    pe.wait_ge(staged, i * TU + u + 1)
                    pe.wait_ge(evacuated, i * TU + u + 1)
                    for k in range(KD):
                        last = nc.tensor.transpose(m.banks[u][0:TP, k * P:(k + 1) * P],
                                                   cols[:, u, k, :], m.ident[:, :])
                    last.then_inc(transposed, 1)

        @block.vector
        def _(dve):
            dve.sem_inc(evacuated, TU)
            with dve.Fori(0, NT // TU) as i:
                for u in range(TU):
                    dve.wait_ge(transposed, i * TU + u + 1 + TU)
                    dve.wait_ge(row_stored[u], i * 16)
                    nc.vector.tensor_copy(tile[0:TP, u, :], m.banks[u][0:TP, 0:D]).then_inc(evacuated, 1)

        @block.sync
        def _(sp):
            with sp.Fori(0, NT // TU) as i:
                for u in range(TU):
                    sp.wait_ge(evacuated, i * TU + u + 1 + TU)
                    sp.dma_start(rows[ds(i * (TU * TP) + u * TP, TP), :], tile[0:TP, u, :])\
                        .then_inc(row_stored[u], 16)
            for u in range(TU):
                sp.wait_ge(row_stored[u], 16 * (NT // TU))


def layer_norm(m, of, to, gamma=None, beta=None, add_to=None):
    nc = m.nc
    LU = 4
    squares = m.part(0, LU, KD, CH)
    root = m.part(LU * KD * CH, LU, CH)
    with phase(m, "mean_ready", "centred", "squared", "var_ready", "root_ready", "normed", "scaled", "dve_step") as \
            (block, mean_ready, centred, squared, var_ready, root_ready, normed, scaled, dve_step):

        @block.tensor
        def _(pe):
            with pe.Fori(0, NCH // LU) as i:
                for u in range(LU):
                    pe.wait_ge(centred, i * LU + u + 1)
                    for k in range(KD):
                        last = nc.tensor.matmul(m.banks[u][:, 0:CH], m.mean_of[:, :],
                                                of[:, k, tile_at(i, u, CH, LU)], start=k == 0, stop=k == KD - 1)
                    last.then_inc(mean_ready, 1)
                for u in range(LU):
                    pe.wait_ge(squared, i * LU + u + 1)
                    pe.wait_ge(root_ready, i * LU + u + 1)
                    for k in range(KD):
                        last = nc.tensor.matmul(m.banks[LU + u][:, 0:CH], m.mean_of[:, :],
                                                squares[:, u, k, :], start=k == 0, stop=k == KD - 1)
                    last.then_inc(var_ready, 1)

        @block.scalar
        def _(act):
            act.sem_inc(root_ready, LU)
            with act.Fori(0, NCH // LU) as i:
                for u in range(LU):
                    act.wait_ge(centred, i * LU + u + 1 + LU)
                    act.wait_ge(var_ready, i * LU)
                    nc.scalar.activation(squares[:, u, :, :], to[:, :, tile_at(i, u, CH, LU)], ACT.Square)\
                        .then_inc(squared, 1)
                for u in range(LU):
                    act.wait_ge(var_ready, i * LU + u + 1)
                    act.wait_ge(normed, i * LU)
                    nc.scalar.activation(root[:, u, :], m.banks[LU + u][:, 0:CH], ACT.Sqrt, bias=m.eps[:, 0:1])\
                        .then_inc(root_ready, 1)

        @block.vector
        def _(dve):
            dve.sem_inc(centred, LU)
            with dve.Fori(0, NCH // LU) as i:
                for u in range(LU):
                    dve.wait_ge(mean_ready, i * LU + u + 1)
                    for k in range(KD):
                        cols = tile_at(i, u, CH, LU)
                        last = nc.vector.tensor_tensor(to[:, k, cols], of[:, k, cols], m.banks[u][:, 0:CH],
                                                       ALU.subtract)
                    last.then_inc(centred, 1)
                for u in range(LU):
                    cols = tile_at(i, u, CH, LU)
                    dve.wait_ge(root_ready, i * LU + u + 1 + LU)
                    nc.vector.reciprocal(root[:, u, :], root[:, u, :]).then_inc(dve_step, 1)
                    dve.wait_ge(dve_step, i * LU + u + 1)
                    dve.wait_ge(squared, i * LU + u + 1)
                    for k in range(KD):
                        last = nc.vector.tensor_tensor(to[:, k, cols], to[:, k, cols], root[:, u, :], ALU.mult)
                    last.then_inc(normed, 1)
                    if gamma:
                        dve.wait_ge(normed, i * LU + u + 1)
                        for k in range(KD):
                            last = nc.vector.tensor_scalar(to[:, k, cols], to[:, k, cols], m.vec(gamma, k),
                                                           m.vec(beta, k), ALU.mult, ALU.add)
                        last.then_inc(scaled, 1)
                    if add_to is not None:
                        dve.wait_ge(scaled, i * LU + u + 1)
                        for k in range(KD):
                            nc.vector.tensor_tensor(add_to[:, k, cols], add_to[:, k, cols], to[:, k, cols], ALU.add)


def aggregate(m, weighted=False, degrees=False, with_self=False):
    nc = m.nc
    sums = m.sums
    nw = 3 if weighted else 1
    ahead = 4 if weighted else SLOTS
    banks = 2 if weighted else BANKS
    onehot = m.onehot[:, 0:ahead * nw * WIN].rearrange("p (s w n) -> p s w n", s=ahead, w=nw)
    wsum = m.part(6 * AW, 2, AW)
    fetched, before = m.fetched, m.fetched_before
    m.fetched_before += EG // SLOTS * 16
    with phase(m, "staged", "made", "multiplied", "added", "cleared", "slot_claimed") as \
            (block, staged, made, multiplied, added, cleared, slot_claimed):

        @block.scalar
        def _(act):
            if with_self:
                nc.scalar.copy(sums[:, 0:KD, 0:NP], m.yT[:, :, :]).then_inc(cleared, 1)
            with act.Fori(0, EG // EU) as i:
                for h in range(2):
                    act.wait_ge(multiplied, i * EU + h * SLOTS)
                    nc.scalar.copy(m.src_cols[:, h, :], m.src[:, ds(i * EU + h * SLOTS, SLOTS)]).then_inc(staged, 1)

        @block.gpsimd
        def _(pool):
            if with_self:
                nc.gpsimd.memset(sums[:, 0:KD, NP:AW], 0.0).then_inc(cleared, 1)
            else:
                nc.gpsimd.memset(sums[:, 0:KD * nw, :], 0.0).then_inc(cleared, 1)
            if weighted:
                nc.gpsimd.memset(wsum, 0.0).then_inc(cleared, 1)
            elif degrees:
                nc.gpsimd.memset(m.degree[:, :], 0.0).then_inc(cleared, 1)
            with pool.Fori(0, EG // EU) as i:
                for k in range(EU):
                    s = k % SLOTS
                    if s == 0:
                        pool.wait_ge(staged, i * 2 + k // SLOTS + 1)
                    pool.wait_ge(multiplied, i * EU + k + 1)
                    pool.sem_inc(slot_claimed, 1)
                    nc.gpsimd.indirect_dma_start(
                        m.gathered[:, s, :], None, m.table,
                        bass.IndirectOffsetOnAxis(ap=m.src_cols[:, k // SLOTS, s:s + 1].bitcast(U32), axis=0),
                    ).then_inc(fetched[s], 16)

        @block.tensor
        def _(pe):
            pe.sem_inc(multiplied, SLOTS)
            with pe.Fori(0, EG // EU) as i:
                for k in range(EU):
                    s, b, o = k % SLOTS, k % banks, k % ahead
                    pe.wait_ge(fetched[s], (i * 2 + k // SLOTS + 1) * 16 + before)
                    pe.wait_ge(made, i * EU + k + 1)
                    pe.wait_ge(added, i * EU + k + 1)
                    for f in range(KD):
                        to = m.banks[2 * b + f][:, 0:nw * WIN] if weighted else m.banks[b][:, f * WIN:(f + 1) * WIN]
                        last = nc.tensor.matmul(to, m.gathered[:, s, f * P:(f + 1) * P], onehot[:, o, :, :],
                                                start=True, stop=True)
                    if weighted:
                        last = nc.tensor.matmul(m.banks[4 + b][:, 0:2 * WIN], m.ones[:, :], onehot[:, o, 1:3, :],
                                                start=True, stop=True)
                    if degrees:
                        last = nc.tensor.matmul(m.banks[4 + b][:, 0:WIN], m.ones[:, :], onehot[:, o, 0, :],
                                                start=True, stop=True)
                    last.then_inc(multiplied, 1)

        @block.vector
        def _(dve):
            def make(o, c):
                rel, w = m.dst_rel[:, ds(c, 1)], m.edge_w[:, ds(c, 1)]
                last = nc.vector.tensor_scalar(onehot[:, o, 0, :], m.count[:, :], rel, None, ALU.is_equal)
                if weighted:
                    nc.vector.tensor_scalar(onehot[:, o, 2, :], m.count[:, :], rel, w, ALU.is_equal, ALU.mult)
                    last = nc.vector.tensor_scalar(onehot[:, o, 1, :], m.count[:, :], rel, m.edge_abs[:, ds(c, 1)],
                                                   ALU.is_equal, ALU.mult)
                last.then_inc(made, 1)

            for k in range(ahead):
                make(k, k)
            dve.wait_ge(cleared, 2 if (weighted or degrees or with_self) else 1)
            dve.sem_inc(added, banks)
            with dve.Fori(0, EG // EU) as i:
                for k in range(EU):
                    b = k % banks
                    at = dve.value_load(m.base[0:1, ds(i * EU + k, 1)], min_val=0, max_val=N - 1)
                    dve.wait_ge(multiplied, i * EU + k + 1 + SLOTS)
                    dve.wait_ge(added, i * EU + k + banks)
                    window = ds(at, WIN)
                    if weighted:
                        for f in range(KD):
                            view = sums[:, :, window].rearrange("p (w f) n -> p f w n", f=KD)[:, f, :, :]
                            nc.vector.tensor_tensor(view, view, m.banks[2 * b + f][:, 0:nw * WIN].rearrange(
                                "p (w n) -> p w n", w=nw), ALU.add)
                        last = nc.vector.tensor_tensor(wsum[:, :, window], wsum[:, :, window],
                                                       m.banks[4 + b][:, 0:2 * WIN].rearrange("p (w n) -> p w n", w=2),
                                                       ALU.add)
                    else:
                        view = sums[:, 0:KD, window]
                        last = nc.vector.tensor_tensor(view, view, m.banks[b][:, 0:KD * WIN].rearrange(
                            "p (f n) -> p f n", f=KD), ALU.add)
                    if degrees:
                        last = nc.vector.tensor_tensor(m.degree[:, window], m.degree[:, window],
                                                       m.banks[4 + b][:, 0:WIN], ALU.add)
                    last.then_inc(added, 1)
                    make(k % ahead, i * EU + k + ahead)


def sage_update(m, w_l, w_r, b, last_layer):
    nc, ins = m.nc, m.ins
    w = m.part(m.REG, 2, KD, D)
    inverse = m.part(m.REG + 1024, NP)
    mean = m.part(m.REG + 1024 + NP, 2, KD * CH)
    sums = m.sums
    with phase(m, "loaded", "dve_step", "averaged", "multiplied", "taken") as \
            (block, loaded, dve_step, averaged, multiplied, taken):

        @block.sync
        def _(sp):
            for j, name in enumerate((w_l, w_r)):
                sp.dma_start(w[:, j, :, :], ins[name].rearrange("(k p) o -> p k o", p=P)).then_inc(loaded, 16)

        @block.tensor
        def _(pe):
            pe.wait_ge(loaded, 32)
            with pe.Fori(0, NCH // 2) as i:
                for u in range(2):
                    pe.wait_ge(averaged, i * 2 + u + 1 + 2)
                    pe.wait_ge(taken, i * 2 + u + 1)
                    mu = mean[:, u, :].rearrange("p (k n) -> p k n", k=KD)
                    for f in range(KD):
                        cols = slice(f * P, (f + 1) * P)
                        for k in range(KD):
                            nc.tensor.matmul(m.banks[2 * u + f][:, 0:CH], w[:, 1, k, cols],
                                             m.yT[:, k, tile_at(i, u, CH, 2)], start=k == 0, stop=False)
                        for k in range(KD):
                            last = nc.tensor.matmul(m.banks[2 * u + f][:, 0:CH], w[:, 0, k, cols],
                                                    mu[:, k, :], start=False, stop=k == KD - 1)
                    last.then_inc(multiplied, 1)

        @block.vector
        def _(dve):
            step = Steps(dve, dve_step)
            step(nc.vector.tensor_scalar(inverse, m.degree[:, 0:NP], 1.0, None, ALU.max))
            step(nc.vector.reciprocal(inverse, inverse))
            dve.sem_inc(averaged, 2)

            def average(i, u):
                mu = mean[:, u, :].rearrange("p (k n) -> p k n", k=KD)
                cols = tile_at(i, u, CH, 2)
                for k in range(KD):
                    last = nc.vector.tensor_tensor(mu[:, k, :], sums[:, k, cols], inverse[:, cols], ALU.mult)
                last.then_inc(averaged, 1)

            with dve.Fori(0, NCH // 2) as i:
                for u in range(2):
                    dve.wait_ge(multiplied, i * 2)
                    average(i, u)
                if last_layer:
                    for u in range(2):
                        cols = tile_at(i, u, CH, 2)
                        dve.wait_ge(multiplied, i * 2 + u + 1)
                        for f in range(KD):
                            last = nc.vector.scalar_tensor_tensor(
                                m.xT[:, f, cols], m.banks[2 * u + f][:, 0:CH], m.vec(b, f), m.xT[:, f, cols],
                                ALU.add, ALU.add)
                        last.then_inc(taken, 1)

        @block.scalar
        def _(act):
            act.sem_inc(taken, 2)
            if not last_layer:
                with act.Fori(0, NCH // 2) as i:
                    for u in range(2):
                        act.wait_ge(multiplied, i * 2 + u + 1)
                        for f in range(KD):
                            last = nc.scalar.activation(m.yT[:, f, tile_at(i, u, CH, 2)],
                                                        m.banks[2 * u + f][:, 0:CH], ACT.Relu, bias=m.vec(b, f))
                        last.then_inc(taken, 1)


def sage(m, w1_l, w1_r, b1, w2_l, w2_r, b2, degrees=False):
    store_rows(m, m.yT, m.table)
    aggregate(m, degrees=degrees)
    sage_update(m, w1_l, w1_r, b1, False)
    store_rows(m, m.yT, m.table)
    aggregate(m)
    sage_update(m, w2_l, w2_r, b2, True)


def repeat_last(ap, n):
    return ap.unsqueeze(2).broadcast_to([*ap.shape, n])


def repeat_first(ap, n):
    return ap.unsqueeze(1).broadcast_to([ap.shape[0], n, ap.shape[1]])


def slice_attention(m):
    nc, ins = m.nc, m.ins
    at = [m.REG]

    def reg(*shape):
        v = m.part(at[0], *shape)
        at[0] += int(np.prod(shape))
        return v

    HP = HG // P
    wT = m.part(0, HP, NP)
    wx_t = reg(HP, D)
    wfx = reg(KD, HG)
    wo = reg(HP, D)
    pair = reg(4, P)
    wc = reg(KD, HG)
    bc = reg(HG)
    b_fx = reg(HG)
    b_slice = reg(G)
    inv_temp = reg(HEADS)
    mixed = reg(HP, D + 1)
    mixed_t = reg(KD, HG)
    share = reg(HG)
    tok = reg(HG)
    q_t, k_t, v_s = reg(HG), reg(HG), reg(HG)
    score = reg(HP, G)
    attn, attn_t, out_t = reg(HG), reg(HG), reg(HG)
    mo = reg(HP, D)
    probs = reg(TU, HG)
    assert at[0] <= 4 * AW + 16384
    zero = attn
    y_rows = m.gathered
    y_cols = m.onehot[:, 0:TU * KD * TP].rearrange("p (u k n) -> p u k n", u=TU, k=KD)
    top = m.small[:, 0:TU * HEADS].rearrange("p (u h) -> p u h", u=TU)
    tot = m.small[:, 64:64 + TU * HEADS].rearrange("p (u h) -> p u h", u=TU)
    tiny = m.small[:, 128:160]

    def four(ap):
        return ap.rearrange("p (j n) -> p j n", j=HP)

    def diagonal(ap, b):
        return four(ap)[b * G:(b + 1) * G, :, b * G:(b + 1) * G]

    with phase(m, "cleared", "loaded", "multiplied", "dve_step") as (block, cleared, loaded, multiplied, dve_step):

        @block.gpsimd
        def _(pool):
            nc.gpsimd.memset(attn, 0.0)
            nc.gpsimd.memset(tok, 0.0)
            nc.gpsimd.memset(wT[:, :, N:NP], 0.0)
            nc.gpsimd.memset(pair, 0.0).then_inc(cleared, 1)

        @block.sync
        def _(sp):
            def load(to, of):
                sp.dma_start(to, of).then_inc(loaded, 16)

            load(wx_t, ins["L0_ffn_W_x_t"].rearrange("(j p) f -> p j f", p=P))
            load(wfx, ins["L0_ffn_W_fx"].rearrange("(k p) o -> p k o", p=P))
            load(wo, ins["L0_ffn_W_out"].rearrange("(j p) o -> p j o", p=P))
            load(b_fx[0:1, :], ins["L0_ffn_b_fx"])
            load(b_slice[0:1, :], ins["L0_ffn_b_slice"])
            load(inv_temp, ins["L0_ffn_temperature"].partition_broadcast(P))
            sp.wait_ge(cleared, 1)
            for w, name in enumerate(("W_slice", "W_q", "W_k", "W_v")):
                for b in range(2):
                    load(pair[b * G:(b + 1) * G, w, b * G:(b + 1) * G], ins["L0_ffn_" + name])
            sp.wait_ge(loaded, 16 * 14)

        @block.tensor
        def _(pe):
            pe.wait_ge(loaded, 16 * 14)
            for j in range(HP):
                for k in range(KD):
                    nc.tensor.matmul(m.banks[k][:, j * P:(j + 1) * P], wx_t[:, j, k * P:(k + 1) * P], pair[:, 0, :],
                                     start=True, stop=True)
                last = nc.tensor.matmul(m.banks[2][0:1, j * P:(j + 1) * P], m.vec("L0_ffn_b_x", j), pair[:, 0, :],
                                        start=True, stop=True)
            last.then_inc(multiplied, 1)

        @block.vector
        def _(dve):
            step = Steps(dve, dve_step)
            dve.wait_ge(loaded, 16 * 14)
            step(nc.vector.tensor_scalar(inv_temp, inv_temp, 0.1, 5.0, ALU.max, ALU.min))
            step(nc.vector.reciprocal(inv_temp, inv_temp))
            dve.wait_ge(multiplied, 1)
            heads = lambda ap: ap.rearrange("p (h g) -> p h g", h=HEADS)
            for k in range(KD):
                nc.vector.tensor_tensor(heads(wc[:, k, :]), heads(m.banks[k][:, :]), repeat_last(inv_temp, G), ALU.mult)
            step(nc.vector.tensor_tensor(heads(bc[0:1, :]), heads(m.banks[2][0:1, :]),
                                         repeat_first(b_slice[0:1, :], HEADS), ALU.add))
            step(nc.vector.tensor_tensor(heads(bc[0:1, :]), heads(bc[0:1, :]), repeat_last(inv_temp[0:1, :], G),
                                         ALU.mult))

    LOGITS, ROWS, TURNED, NORM, MIXED = (0, 1), 2, (3, 4), 5, (6, 7)
    with phase(m, "staged", "y_turned", "y_taken", "logits_ready", "centred", "exped", "normed", "mixed_in",
               "w_turned", "w_taken", "maxed", "summed", "inverted") as \
            (block, staged, y_turned, y_taken, logits_ready, centred, exped, normed, mixed_in,
             w_turned, w_taken, maxed, summed, inverted):

        @block.scalar
        def _(act):
            act.sem_inc(y_taken, 1)
            act.sem_inc(w_taken, 2)

            def front(i, u):
                act.wait_ge(mixed_in, i * TU)
                nc.scalar.copy(y_cols[:, u, :, :], m.yT[:, :, tile_at(i, u, TP, TU)]).then_inc(staged, 1)
                act.wait_ge(y_turned, i * TU + u + 1)
                nc.scalar.copy(y_rows[0:TP, u, :], m.banks[ROWS][0:TP, 0:D]).then_inc(y_taken, 1)

            def back(i, u):
                act.wait_ge(centred, i * TU + u + 1)
                nc.scalar.activation(probs[0:TP, u, :], probs[0:TP, u, :], ACT.Exp).then_inc(exped, 1)

            def last(i, u):
                act.wait_ge(w_turned, i * TU + u + 1)
                nc.scalar.copy(wT[:, :, tile_at(i, u, TP, TU)],
                               m.banks[TURNED[u % 2]][:, 0:HP * TP].rearrange("p (j n) -> p j n", j=HP))\
                    .then_inc(w_taken, 1)

            with act.Fori(0, NT // TU) as i:
                front(i, 0)
                for u in range(TU):
                    if u + 1 < TU:
                        front(i, u + 1)
                    back(i, u)
                    if u:
                        last(i, u - 1)
                last(i, TU - 1)

        @block.tensor
        def _(pe):
            for b in MIXED:
                nc.tensor.matmul(m.banks[b][:, :], zero[:, 0:P], zero, start=True, stop=False)
            nc.tensor.matmul(m.banks[NORM][:, 0:HP], zero[:, 0:P], zero[:, 0:HP], start=True, stop=False)

            def front(i, u):
                pe.wait_ge(staged, i * TU + u + 1)
                pe.wait_ge(y_taken, i * TU + u + 1)
                for k in range(KD):
                    last = nc.tensor.transpose(m.banks[ROWS][0:TP, k * P:(k + 1) * P], y_cols[:, u, k, :], m.ident[:, :])
                last.then_inc(y_turned, 1)
                pe.wait_ge(centred, i * TU + max(u - 1, 0))
                logits = m.banks[LOGITS[u % 2]][0:TP, :]
                for k in range(KD):
                    nc.tensor.matmul(logits, y_cols[:, u, k, :], wc[:, k, :], start=k == 0, stop=False)
                nc.tensor.matmul(logits, m.ones[0:1, 0:TP], bc[0:1, :], start=False, stop=True)\
                    .then_inc(logits_ready, 1)

            def back(i, u):
                pe.wait_ge(normed, i * TU + u + 1)
                pe.wait_ge(y_taken, i * TU + u + 1 + 1)
                pe.wait_ge(w_taken, i * TU + u + 1 + (u == 0))
                for j in range(HP):
                    w = probs[0:TP, u, j * P:(j + 1) * P]
                    nc.tensor.transpose(m.banks[TURNED[u % 2]][:, j * TP:(j + 1) * TP], w, m.ident[0:TP, 0:TP])\
                        .then_inc(w_turned, 1) if j == HP - 1 else \
                        nc.tensor.transpose(m.banks[TURNED[u % 2]][:, j * TP:(j + 1) * TP], w, m.ident[0:TP, 0:TP])
                for j in range(HP):
                    w = probs[0:TP, u, j * P:(j + 1) * P]
                    nc.tensor.matmul(m.banks[MIXED[j // 2]][:, (j % 2) * D:(j % 2 + 1) * D], w, y_rows[0:TP, u, :],
                                     start=False, stop=False, skip_group_check=True)
                    last = nc.tensor.matmul(m.banks[NORM][:, j:j + 1], w, m.ones[0:TP, 0:1], start=False, stop=False,
                                            skip_group_check=True)
                last.then_inc(mixed_in, 1)

            with pe.Fori(0, NT // TU) as i:
                front(i, 0)
                for u in range(TU):
                    if u + 1 < TU:
                        front(i, u + 1)
                    back(i, u)
            for b in MIXED:
                nc.tensor.matmul(m.banks[b][:, :], zero[:, 0:P], zero, start=False, stop=True)
            nc.tensor.matmul(m.banks[NORM][:, 0:HP], zero[:, 0:P], zero[:, 0:HP], start=False, stop=True)

        @block.vector
        def _(dve):
            heads = lambda ap: ap.rearrange("p (h g) -> p h g", h=HEADS)

            def centre(i, u):
                logits = heads(m.banks[LOGITS[u % 2]][0:TP, :])
                dve.wait_ge(logits_ready, i * TU + u + 1)
                nc.vector.tensor_reduce(top[0:TP, u, :], logits, AX, ALU.max).then_inc(maxed, 1)
                dve.wait_ge(maxed, i * TU + u + 1)
                dve.wait_ge(mixed_in, i * TU)
                nc.vector.tensor_tensor(heads(probs[0:TP, u, :]), logits, repeat_last(top[0:TP, u, :], G),
                                        ALU.subtract).then_inc(centred, 1)

            def norm(i, u):
                p = heads(probs[0:TP, u, :])
                dve.wait_ge(exped, i * TU + u + 1)
                nc.vector.tensor_reduce(tot[0:TP, u, :], p, AX, ALU.add).then_inc(summed, 1)
                dve.wait_ge(summed, i * TU + u + 1)
                nc.vector.reciprocal(tot[0:TP, u, :], tot[0:TP, u, :]).then_inc(inverted, 1)
                dve.wait_ge(inverted, i * TU + u + 1)
                nc.vector.tensor_tensor(p, p, repeat_last(tot[0:TP, u, :], G), ALU.mult).then_inc(normed, 1)

            with dve.Fori(0, NT // TU) as i:
                centre(i, 0)
                for u in range(TU):
                    if u + 1 < TU:
                        centre(i, u + 1)
                    norm(i, u)

    with phase(m, "multiplied", "taken", "dve_step", "exped") as (block, multiplied, taken, dve_step, exped):

        @block.tensor
        def _(pe):
            pe.wait_ge(taken, 1)
            for j in range(HP):
                for k in range(KD):
                    nc.tensor.transpose(m.banks[k][:, j * P:(j + 1) * P], mixed[:, j, k * P:(k + 1) * P], m.ident[:, :])
                last = nc.tensor.transpose(m.banks[2][0:1, j * P:(j + 1) * P], mixed[:, j, D:D + 1], m.ident[:, :])
            last.then_inc(multiplied, 1)
            pe.wait_ge(taken, 2)
            for j in range(HP):
                cols = slice(j * P, (j + 1) * P)
                for k in range(KD):
                    nc.tensor.matmul(m.banks[3][:, cols], wfx[:, k, cols], mixed_t[:, k, cols], start=k == 0, stop=False)
                last = nc.tensor.matmul(m.banks[3][:, cols], b_fx[0:1, cols], share[0:1, cols], start=False, stop=True)
            last.then_inc(multiplied, 1)
            pe.wait_ge(taken, 3)
            nc.tensor.matmul(m.banks[4][:, :], pair[:, 1, :], tok, start=True, stop=True)
            nc.tensor.matmul(m.banks[5][:, :], pair[:, 2, :], tok, start=True, stop=True)
            for j in range(HP):
                cols = slice(j * P, (j + 1) * P)
                last = nc.tensor.matmul(m.banks[6][:, cols], tok[:, cols], pair[:, 3, :], start=True, stop=True)
            last.then_inc(multiplied, 1)
            pe.wait_ge(taken, 4)
            for j in range(HP):
                cols = slice(j * P, (j + 1) * P)
                last = nc.tensor.matmul(m.banks[7][:, cols], q_t[:, cols], k_t[:, cols], start=True, stop=True)
            last.then_inc(multiplied, 1)
            pe.wait_ge(taken, 5)
            for j in range(HP):
                cols = slice(j * P, (j + 1) * P)
                last = nc.tensor.transpose(m.banks[0][:, cols], attn[:, cols], m.ident[:, :])
            last.then_inc(multiplied, 1)
            pe.wait_ge(taken, 6)
            for j in range(HP):
                cols = slice(j * P, (j + 1) * P)
                last = nc.tensor.matmul(m.banks[1][:, cols], v_s[:, cols], attn_t[:, cols], start=True, stop=True)
            last.then_inc(multiplied, 1)
            pe.wait_ge(taken, 7)
            for j in range(HP):
                last = nc.tensor.matmul(m.banks[2 + j // 2][:, (j % 2) * D:(j % 2 + 1) * D],
                                        out_t[:, j * P:(j + 1) * P], wo[:, j, :], start=True, stop=True)
            last.then_inc(multiplied, 1)

        @block.scalar
        def _(act):
            act.wait_ge(exped, 1)
            nc.scalar.activation(score, score, ACT.Exp).then_inc(exped, 1)

        @block.vector
        def _(dve):
            step = Steps(dve, dve_step)
            norm, inv = tiny[:, 0:HP], tiny[:, HP:2 * HP]
            step(nc.vector.tensor_copy(norm, m.banks[NORM][:, 0:HP]))
            step(nc.vector.tensor_scalar(inv, norm, 1e-5, None, ALU.add))
            step(nc.vector.reciprocal(inv, inv))
            for j in range(HP):
                nc.vector.tensor_tensor(mixed[:, j, D:D + 1], norm[:, j:j + 1], inv[:, j:j + 1], ALU.mult)
                last = nc.vector.tensor_scalar(mixed[:, j, 0:D], m.banks[MIXED[j // 2]][:, (j % 2) * D:(j % 2 + 1) * D],
                                               inv[:, j:j + 1], None, ALU.mult)
            last.then_inc(taken, 1)
            dve.wait_ge(multiplied, 1)
            for k in range(KD):
                nc.vector.tensor_copy(mixed_t[:, k, :], m.banks[k][:, :])
            nc.vector.tensor_copy(share[0:1, :], m.banks[2][0:1, :]).then_inc(taken, 1)
            dve.wait_ge(multiplied, 2)
            nc.vector.tensor_copy(diagonal(tok, 0), diagonal(m.banks[3][:, :], 0))
            nc.vector.tensor_copy(diagonal(tok, 1), diagonal(m.banks[3][:, :], 1)).then_inc(taken, 1)
            dve.wait_ge(multiplied, 3)
            nc.vector.tensor_copy(q_t, m.banks[4][:, :])
            nc.vector.tensor_copy(k_t, m.banks[5][:, :])
            nc.vector.tensor_copy(v_s, m.banks[6][:, :]).then_inc(taken, 1)
            dve.wait_ge(multiplied, 4)
            for b in range(2):
                last = nc.vector.tensor_scalar(score[b * G:(b + 1) * G, :, :], diagonal(m.banks[7][:, :], b),
                                               float(G) ** -0.5, None, ALU.mult)
            step(last)
            step(nc.vector.tensor_reduce(tiny[:, 8:8 + HP], score, AX, ALU.max))
            nc.vector.tensor_tensor(score, score, repeat_last(tiny[:, 8:8 + HP], G), ALU.subtract).then_inc(exped, 1)
            dve.wait_ge(exped, 2)
            step(nc.vector.tensor_reduce(tiny[:, 12:12 + HP], score, AX, ALU.add))
            step(nc.vector.reciprocal(tiny[:, 12:12 + HP], tiny[:, 12:12 + HP]))
            for b in range(2):
                rows = slice(b * G, (b + 1) * G)
                last = nc.vector.tensor_tensor(diagonal(attn, b), score[rows, :, :],
                                               repeat_last(tiny[rows, 12:12 + HP], G), ALU.mult)
            last.then_inc(taken, 1)
            dve.wait_ge(multiplied, 5)
            nc.vector.tensor_copy(attn_t, m.banks[0][:, :]).then_inc(taken, 1)
            dve.wait_ge(multiplied, 6)
            nc.vector.tensor_copy(out_t, m.banks[1][:, :]).then_inc(taken, 1)
            dve.wait_ge(multiplied, 7)
            for b in range(2):
                nc.vector.tensor_copy(mo[:, 2 * b:2 * b + 2, :],
                                      m.banks[2 + b][:, :].rearrange("p (j n) -> p j n", j=2))

    with phase(m, "multiplied", "taken") as (block, multiplied, taken):

        @block.tensor
        def _(pe):
            with pe.Fori(0, NCH // 2) as i:
                for u in range(2):
                    pe.wait_ge(taken, i * 2 + u + 1)
                    for f in range(KD):
                        for j in range(HP):
                            last = nc.tensor.matmul(m.banks[2 * u + f][:, 0:CH], mo[:, j, f * P:(f + 1) * P],
                                                    wT[:, j, tile_at(i, u, CH, 2)], start=j == 0, stop=j == HP - 1)
                    last.then_inc(multiplied, 1)

        @block.vector
        def _(dve):
            dve.sem_inc(taken, 2)
            with dve.Fori(0, NCH // 2) as i:
                for u in range(2):
                    cols = tile_at(i, u, CH, 2)
                    dve.wait_ge(multiplied, i * 2 + u + 1)
                    for f in range(KD):
                        last = nc.vector.scalar_tensor_tensor(m.xT[:, f, cols], m.banks[2 * u + f][:, 0:CH],
                                                              m.vec("L0_ffn_b_out", f), m.xT[:, f, cols],
                                                              ALU.add, ALU.add)
                    last.then_inc(taken, 1)


def gcn(m):
    nc, ins = m.nc, m.ins
    w = m.part(m.REG, KD, D)
    inv_root = m.part(m.REG + 512, NP)
    scaled = m.part(m.REG + 512 + NP, 2, KD, CH)
    with phase(m, "loops_added", "rooted", "scaled_ready") as (block, loops_added, rooted, scaled_ready):

        @block.vector
        def _(dve):
            nc.vector.tensor_scalar(inv_root, m.degree[:, 0:NP], 1.0, None, ALU.add).then_inc(loops_added, 1)
            dve.wait_ge(rooted, 1)
            nc.vector.reciprocal(inv_root, inv_root).then_inc(scaled_ready, 1)
            dve.wait_ge(scaled_ready, 1)
            for k in range(KD):
                nc.vector.tensor_tensor(m.yT[:, k, :], m.yT[:, k, :], inv_root, ALU.mult)

        @block.scalar
        def _(act):
            act.wait_ge(loops_added, 1)
            nc.scalar.activation(inv_root, inv_root, ACT.Sqrt).then_inc(rooted, 1)

    for layer in (1, 2, 3):
        store_rows(m, m.yT, m.table)
        aggregate(m, with_self=True)
        b = f"L1_gnn_b{layer}"
        with phase(m, "loaded", "multiplied", "taken", "scaled_back", "gelu_done") as \
                (block, loaded, multiplied, taken, scaled_back, gelu_done):

            @block.sync
            def _(sp):
                sp.dma_start(w, ins[f"L1_gnn_W{layer}"].rearrange("(k p) o -> p k o", p=P)).then_inc(loaded, 16)

            @block.tensor
            def _(pe):
                pe.wait_ge(loaded, 16)
                with pe.Fori(0, NCH // 2) as i:
                    for u in range(2):
                        pe.wait_ge(taken, i * 2 + u + 1)
                        for f in range(KD):
                            for k in range(KD):
                                last = nc.tensor.matmul(m.banks[2 * u + f][:, 0:CH], w[:, k, f * P:(f + 1) * P],
                                                        m.sums[:, k, tile_at(i, u, CH, 2)], start=k == 0,
                                                        stop=k == KD - 1)
                        last.then_inc(multiplied, 1)

            @block.vector
            def _(dve):
                dve.sem_inc(taken, 2)
                with dve.Fori(0, NCH // 2) as i:
                    for u in range(2):
                        cols = tile_at(i, u, CH, 2)
                        dve.wait_ge(multiplied, i * 2 + u + 1)
                        if layer < 3:
                            dve.wait_ge(gelu_done, i * 2)
                        for f in range(KD):
                            last = nc.vector.tensor_tensor(scaled[:, u, f, :], m.banks[2 * u + f][:, 0:CH],
                                                           inv_root[:, cols], ALU.mult)
                        last.then_inc(taken, 1)
                        if layer == 3:
                            dve.wait_ge(taken, i * 2 + u + 1 + 2)
                            for f in range(KD):
                                nc.vector.scalar_tensor_tensor(m.xT[:, f, cols], scaled[:, u, f, :], m.vec(b, f),
                                                               m.xT[:, f, cols], ALU.add, ALU.add)
                    if layer < 3:
                        for u in range(2):
                            cols = tile_at(i, u, CH, 2)
                            dve.wait_ge(gelu_done, i * 2 + u + 1)
                            for f in range(KD):
                                nc.vector.tensor_tensor(m.yT[:, f, cols], m.yT[:, f, cols], inv_root[:, cols], ALU.mult)

            @block.scalar
            def _(act):
                if layer < 3:
                    with act.Fori(0, NCH // 2) as i:
                        for u in range(2):
                            act.wait_ge(taken, i * 2 + u + 1 + 2)
                            for f in range(KD):
                                last = nc.scalar.activation(m.yT[:, f, tile_at(i, u, CH, 2)], scaled[:, u, f, :],
                                                            ACT.Gelu_apprx_tanh, bias=m.vec(b, f))
                            last.then_inc(gelu_done, 1)


def gates(m, w_r, b_r, top_two):
    nc, ins = m.nc, m.ins
    gate = m.part(0, NP)[0:NE, :]
    logit = m.part(NP, NP)[0:NE, :]
    stage = m.part(2 * NP, TU, TP)
    at = [2 * NP + TU * TP]

    def rows(*shape):
        v = m.part(at[0], *shape)[0:TP]
        at[0] += int(np.prod(shape))
        return v

    L, W, S1, S2, T, O = (rows(NT, NE) for _ in range(6))
    a, b, c = rows(NT), rows(NT), rows(NT)
    order = rows(NE)
    wr = m.small[:, 0:KD * NE].rearrange("p (k e) -> p k e", k=KD)
    br = m.small[0:NE, KD * NE:KD * NE + 1]
    with phase(m, "loaded", "ordered", "multiplied", "logits_taken") as (block, loaded, ordered, multiplied, logits_taken):

        @block.sync
        def _(sp):
            sp.dma_start(wr, ins[w_r].rearrange("(k p) e -> p k e", p=P)).then_inc(loaded, 16)
            sp.dma_start(br, ins[b_r]).then_inc(loaded, 16)

        @block.gpsimd
        def _(pool):
            order_i = rows(NE).bitcast(I32)
            nc.gpsimd.memset(gate[:, N:NP], 0.0)
            nc.gpsimd.iota(order_i, [[-1, NE]], base=NE, channel_multiplier=0).then_inc(ordered, 1)
            pool.wait_ge(ordered, 1)
            nc.gpsimd.tensor_copy(order, order_i)

        @block.tensor
        def _(pe):
            pe.wait_ge(loaded, 32)
            with pe.Fori(0, NCH // 2) as i:
                for u in range(2):
                    pe.wait_ge(logits_taken, i * 2 + u + 1)
                    for k in range(KD):
                        last = nc.tensor.matmul(m.banks[u][0:NE, 0:CH], wr[:, k, :], m.yT[:, k, tile_at(i, u, CH, 2)],
                                                start=k == 0, stop=k == KD - 1)
                    last.then_inc(multiplied, 1)

        @block.vector
        def _(dve):
            dve.wait_ge(loaded, 32)
            dve.sem_inc(logits_taken, 2)
            with dve.Fori(0, NCH // 2) as i:
                for u in range(2):
                    dve.wait_ge(multiplied, i * 2 + u + 1)
                    nc.vector.tensor_scalar(logit[:, tile_at(i, u, CH, 2)], m.banks[u][0:NE, 0:CH], br, None,
                                            ALU.add).then_inc(logits_taken, 1)

    def turn(of, to, back):
        with phase(m, "staged", "transposed", "taken", "bank_claimed") as (block, staged, transposed, taken, bank_claimed):

            @block.scalar
            def _(act):
                with act.Fori(0, NT // TU) as i:
                    for u in range(TU):
                        act.wait_ge(transposed, i * TU)
                        if back:
                            nc.scalar.copy(stage[0:TP, u, 0:NE], of[:, ds(i * TU + u, 1), :]
                                           .rearrange("p a e -> p (a e)")).then_inc(staged, 1)
                        else:
                            nc.scalar.copy(stage[0:NE, u, :], of[:, tile_at(i, u, TP, TU)]).then_inc(staged, 1)

            @block.tensor
            def _(pe):
                with pe.Fori(0, NT // TU) as i:
                    for u in range(TU):
                        pe.wait_ge(staged, i * TU + u + 1)
                        pe.wait_ge(taken, i * TU + u + 1)
                        pe.sem_inc(bank_claimed, 1)
                        if back:
                            last = nc.tensor.transpose(m.banks[u][0:NE, 0:TP], stage[0:TP, u, 0:NE], m.ident[0:TP, 0:TP])
                        else:
                            last = nc.tensor.transpose(m.banks[u][0:TP, 0:NE], stage[0:NE, u, :], m.ident[0:NE, 0:NE])
                        last.then_inc(transposed, 1)

            @block.vector
            def _(dve):
                dve.sem_inc(taken, TU)
                with dve.Fori(0, NT // TU) as i:
                    for u in range(TU):
                        dve.wait_ge(transposed, i * TU + u + 1)
                        if back:
                            nc.vector.tensor_copy(to[:, tile_at(i, u, TP, TU)], m.banks[u][0:NE, 0:TP]).then_inc(taken, 1)
                        else:
                            nc.vector.tensor_copy(to[:, ds(i * TU + u, 1), :].rearrange("p a e -> p (a e)"),
                                                  m.banks[u][0:TP, 0:NE]).then_inc(taken, 1)

    turn(logit, L, False)

    with phase(m, "dve_step", "centred", "exped") as (block, dve_step, centred, exped):

        @block.scalar
        def _(act):
            act.wait_ge(centred, 1)
            v = b if top_two else W
            nc.scalar.activation(v, v, ACT.Exp).then_inc(exped, 1)

        @block.vector
        def _(dve):
            step = Steps(dve, dve_step)
            tt, wide = nc.vector.tensor_tensor, lambda v: repeat_last(v, NE)

            def first_largest(of, largest, mask):
                step(nc.vector.tensor_reduce(largest, of, AX, ALU.max))
                step(tt(T, of, wide(largest), ALU.is_equal))
                step(tt(T, T, repeat_first(order, NT), ALU.mult))
                step(nc.vector.tensor_reduce(c, T, AX, ALU.max))
                step(tt(mask, T, wide(c), ALU.is_equal))

            if top_two:
                first_largest(L, a, S1)
                step(nc.vector.scalar_tensor_tensor(O, S1, -1e30, L, ALU.mult, ALU.add))
                first_largest(O, b, S2)
                nc.vector.tensor_tensor(b, b, a, ALU.subtract).then_inc(centred, 1)
                dve.wait_ge(exped, 1)
                step(nc.vector.tensor_scalar(a, b, 1.0, None, ALU.add))
                step(nc.vector.reciprocal(a, a))
                step(tt(b, a, b, ALU.mult))
                step(tt(W, S1, wide(a), ALU.mult))
                step(tt(O, S2, wide(b), ALU.mult))
                step(tt(W, W, O, ALU.add))
            else:
                step(nc.vector.tensor_reduce(a, L, AX, ALU.max))
                tt(W, L, wide(a), ALU.subtract).then_inc(centred, 1)
                dve.wait_ge(exped, 1)
                step(nc.vector.tensor_reduce(b, W, AX, ALU.add))
                step(nc.vector.reciprocal(b, b))
                step(tt(W, W, wide(b), ALU.mult))

    turn(W, gate, True)
    return gate


def experts_top_two(m, gate):
    nc, ins = m.nc, m.ins
    HT = H1 // P
    w1 = m.part(m.REG, NE, KD * H1).rearrange("p e (k h) -> p e k h", k=KD)
    w2 = m.part(m.REG + NE * KD * H1, NE, HT * D).rearrange("p e (h o) -> p e h o", h=HT)
    b2 = m.gathered[0:NE, 0, :]
    hidden = m.part(NP, 2, HT, CH)
    OUT, GATE = (4, 5), (6, 7)
    with phase(m, "loaded", "hidden_ready", "gelu_done", "gate_spread", "gated", "consumed", "out_ready", "added",
               "bank_claimed") as \
            (block, loaded, hidden_ready, gelu_done, gate_spread, gated, consumed, out_ready, added, bank_claimed):

        @block.sync
        def _(sp):
            for e in range(NE):
                sp.dma_start(w1[:, e, :, :], ins["L1_ffn_W1"][e].rearrange("(k p) h -> p k h", p=P)).then_inc(loaded, 16)
                sp.dma_start(w2[:, e, :, :], ins["L1_ffn_W2"][e].rearrange("(h p) o -> p h o", p=P)).then_inc(loaded, 16)
            sp.dma_start(b2, ins["L1_ffn_b2"]).then_inc(loaded, 16)

        @block.tensor
        def _(pe):
            pe.wait_ge(loaded, 16 * (2 * NE + 1))
            with pe.Fori(0, NCH) as c:
                cols = ds(c * CH, CH)

                def up(e):
                    for h in range(HT):
                        pe.wait_ge(gelu_done, (c * NE + e) * HT + h + 1)
                        for k in range(KD):
                            last = nc.tensor.matmul(m.banks[h][:, 0:CH], w1[:, e, k, h * P:(h + 1) * P],
                                                    m.yT[:, k, cols], start=k == 0, stop=k == KD - 1)
                        last.then_inc(hidden_ready, 1)
                    pe.wait_ge(gated, (c * NE + e) * HT + HT)
                    pe.sem_inc(bank_claimed, 1)
                    nc.tensor.matmul(m.banks[GATE[e % 2]][:, 0:CH], m.pick[:, e, :], gate[:, cols], start=True,
                                     stop=True).then_inc(gate_spread, 1)

                def down(e):
                    for h in range(HT):
                        pe.wait_ge(gated, (c * NE + e) * HT + h + 1 + 2 * HT)
                        for f in range(KD):
                            last = nc.tensor.matmul(m.banks[OUT[f]][:, 0:CH], w2[:, e, h, f * P:(f + 1) * P],
                                                    hidden[:, e % 2, h, :], start=e == 0 and h == 0, stop=False,
                                                    skip_group_check=True)
                        last.then_inc(consumed, 1)

                up(0)
                pe.wait_ge(added, c + 1)
                for e in range(NE):
                    if e + 1 < NE:
                        up(e + 1)
                    down(e)
                for f in range(KD):
                    last = nc.tensor.matmul(m.banks[OUT[f]][:, 0:CH], b2[:, f * P:(f + 1) * P], gate[:, cols],
                                            start=False, stop=True, skip_group_check=True)
                last.then_inc(out_ready, 1)

        @block.scalar
        def _(act):
            act.sem_inc(gelu_done, HT)
            with act.Fori(0, NCH) as c:
                for e in range(NE):
                    for h in range(HT):
                        act.wait_ge(hidden_ready, (c * NE + e) * HT + h + 1)
                        act.wait_ge(consumed, (c * NE + e) * HT + h + 1)
                        nc.scalar.activation(hidden[:, e % 2, h, :], m.banks[h][:, 0:CH], ACT.Gelu,
                                             bias=m.vec("L1_ffn_b1", e * HT + h)).then_inc(gelu_done, 1)

        @block.vector
        def _(dve):
            dve.sem_inc(gated, 2 * HT)
            dve.sem_inc(consumed, 2 * HT)
            dve.sem_inc(added, 1)
            with dve.Fori(0, NCH) as c:
                for e in range(NE):
                    dve.wait_ge(gate_spread, c * NE + e + 1)
                    for h in range(HT):
                        dve.wait_ge(gelu_done, (c * NE + e) * HT + h + 1 + HT)
                        nc.vector.tensor_tensor(hidden[:, e % 2, h, :], hidden[:, e % 2, h, :],
                                                m.banks[GATE[e % 2]][:, 0:CH], ALU.mult).then_inc(gated, 1)
                dve.wait_ge(out_ready, c + 1)
                cols = ds(c * CH, CH)
                for f in range(KD):
                    last = nc.vector.tensor_tensor(m.xT[:, f, cols], m.xT[:, f, cols], m.banks[OUT[f]][:, 0:CH], ALU.add)
                last.then_inc(added, 1)


def directional(m):
    nc, ins = m.nc, m.ins
    store_rows(m, m.yT, m.table)
    aggregate(m, weighted=True)
    sums = m.sums
    wsum = m.part(6 * AW, 2, AW)
    w1 = m.part(8 * AW, 2 * KD, D)
    w2 = m.part(8 * AW + 2 * KD * D, 4 * KD, D)
    own = m.gathered[:, 0:4, :].rearrange("p a b -> p (a b)")[:, 0:KD * CH].rearrange("p (f n) -> p f n", f=KD)
    snorm = m.gathered[:, 4:8, :].rearrange("p a b -> p (a b)")[:, 0:2 * CH].rearrange("p (u n) -> p u n", u=2)
    inv = m.onehot[:, 0:3 * CH].rearrange("p (w n) -> p w n", w=3)
    OWN = (6, 7)
    with phase(m, "loaded", "snorm_loaded0", "snorm_loaded1", "edge_products", "own_taken", "joined", "absolute", "multiplied", "out_taken",
               "dve_step") as \
            (block, loaded, snorm_loaded0, snorm_loaded1, edge_products, own_taken, joined, absolute, multiplied, out_taken,
             dve_step):

        @block.sync
        def _(sp):
            sp.dma_start(w1, ins["L2_gnn_W1"].rearrange("(k p) o -> p k o", p=P)).then_inc(loaded, 16)
            sp.dma_start(w2, ins["L2_gnn_W2"].rearrange("(k p) o -> p k o", p=P)).then_inc(loaded, 16)
            with sp.Fori(0, NCH // 2) as i:
                for u in range(2):
                    sp.wait_ge(out_taken, i * 2)
                    sp.dma_start(snorm[:, u, :], ins["snorm"][ds(i * 2 * CH + u * CH, CH)].partition_broadcast(P))\
                        .then_inc((snorm_loaded0, snorm_loaded1)[u], 16)

        @block.tensor
        def _(pe):
            pe.wait_ge(loaded, 32)
            with pe.Fori(0, NCH) as c:
                cols = ds(c * CH, CH)
                pe.wait_ge(out_taken, c)
                for f in range(KD):
                    for k in range(KD):
                        nc.tensor.matmul(m.banks[OWN[f]][:, 0:CH], w1[:, KD + k, f * P:(f + 1) * P], m.yT[:, k, cols],
                                         start=k == 0, stop=k == KD - 1)
                for w in range(3):
                    for f in range(KD):
                        for k in range(KD):
                            last = nc.tensor.matmul(m.banks[2 * w + f][:, 0:CH], w1[:, k, f * P:(f + 1) * P],
                                                    sums[:, 2 * w + k, cols], start=k == 0, stop=k == KD - 1)
                last.then_inc(edge_products, 1)
                pe.wait_ge(own_taken, c + 1)
                pe.wait_ge(absolute, c + 1)
                for f in range(KD):
                    for k in range(4 * KD):
                        rhs = m.yT[:, k, cols] if k < KD else sums[:, k - KD, cols]
                        last = nc.tensor.matmul(m.banks[OWN[f]][:, 0:CH], w2[:, k, f * P:(f + 1) * P], rhs,
                                                start=k == 0, stop=k == 4 * KD - 1)
                last.then_inc(multiplied, 1)

        @block.scalar
        def _(act):
            with act.Fori(0, NCH) as c:
                cols = ds(c * CH, CH)
                act.wait_ge(edge_products, c + 1)
                act.wait_ge(joined, c)
                for f in range(KD):
                    last = nc.scalar.activation(own[:, f, :], m.banks[OWN[f]][:, 0:CH], ACT.Identity,
                                                bias=m.vec("L2_gnn_b1", f))
                last.then_inc(own_taken, 1)
                act.wait_ge(joined, c + 1)
                for f in range(KD):
                    v = sums[:, 4 + f, cols]
                    last = nc.scalar.activation(v, v, ACT.Abs)
                last.then_inc(absolute, 1)

        @block.vector
        def _(dve):
            PER = 6
            with dve.Fori(0, NCH // 2) as i:
                for u in range(2):
                    c = i * 2 + u
                    cols = ds(i * 2 * CH + u * CH, CH)
                    n = [0]

                    def step(ins_):
                        ins_.then_inc(dve_step, 1)
                        n[0] += 1
                        dve.wait_ge(dve_step, c * PER + n[0])

                    totals = (m.degree[:, cols], wsum[:, 0, cols], wsum[:, 1, cols])
                    nc.vector.tensor_scalar(inv[:, 0, :], totals[0], 1.0, None, ALU.max)
                    step(nc.vector.tensor_scalar(inv[:, 1, :], totals[1], 1e-8, None, ALU.add))
                    step(nc.vector.reciprocal(inv[:, 0:2, :], inv[:, 0:2, :]))
                    dve.wait_ge(own_taken, c + 1)
                    for f in range(KD):
                        for w in range(3):
                            v = sums[:, 2 * w + f, cols]
                            last = nc.vector.tensor_tensor(v, own[:, f, :], totals[w], ALU.mult)
                    step(last)
                    for f in range(KD):
                        for w in range(3):
                            v = sums[:, 2 * w + f, cols]
                            last = nc.vector.tensor_tensor(v, v, m.banks[2 * w + f][:, 0:CH], ALU.add)
                    step(last)
                    for f in range(KD):
                        for w in range(3):
                            v = sums[:, 2 * w + f, cols]
                            last = nc.vector.tensor_tensor(v, v, inv[:, min(w, 1), :], ALU.mult)
                    step(last)
                    for f in range(KD):
                        v = sums[:, 4 + f, cols]
                        last = nc.vector.tensor_tensor(v, v, m.yT[:, f, cols], ALU.subtract)
                    last.then_inc(joined, 1)
                    dve.wait_ge(multiplied, c + 1)
                    for f in range(KD):
                        last = nc.vector.tensor_scalar(sums[:, f, cols], m.banks[OWN[f]][:, 0:CH], m.vec("L2_gnn_b2", f),
                                                       None, ALU.add)
                    step(last)
                    dve.wait_ge((snorm_loaded0, snorm_loaded1)[u], i * 16 + 16)
                    for f in range(KD):
                        last = nc.vector.tensor_tensor(sums[:, f, cols], sums[:, f, cols], snorm[:, u, :], ALU.mult)
                    last.then_inc(out_taken, 1)
                    assert n[0] == PER

    stat = m.small
    sq = m.part(2 * AW, KD, NP)
    with phase(m, "centred", "squared", "rooted", "scaled_ready", "relu_done", "dve_step") as \
            (block, centred, squared, rooted, scaled_ready, relu_done, dve_step):

        @block.scalar
        def _(act):
            act.wait_ge(centred, 1)
            for f in range(KD):
                last = nc.scalar.activation(sq[:, f, 0:N], sums[:, f, 0:N], ACT.Square, accum_out=stat[:, 4 + f:5 + f])
            last.then_inc(squared, 1)
            act.wait_ge(scaled_ready, 1)
            nc.scalar.activation(stat[:, 4:6], stat[:, 4:6], ACT.Sqrt, bias=m.eps[:, 0:1]).then_inc(rooted, 1)
            act.wait_ge(scaled_ready, 2)
            for f in range(KD):
                nc.scalar.activation(sums[:, f, 0:NP], sums[:, f, 0:NP], ACT.Relu, bias=m.vec("L2_gnn_beta", f),
                                     scale=stat[:, 6 + f:7 + f]).then_inc(relu_done, 1)

        @block.vector
        def _(dve):
            step = Steps(dve, dve_step)
            for f in range(KD):
                last = nc.vector.tensor_reduce(stat[:, f:f + 1], sums[:, f, 0:N], AX, ALU.add)
            step(last)
            step(nc.vector.tensor_scalar(stat[:, 0:2], stat[:, 0:2], 1.0 / N, None, ALU.mult))
            for f in range(KD):
                last = nc.vector.tensor_scalar(sums[:, f, 0:NP], sums[:, f, 0:NP], stat[:, f:f + 1], None, ALU.subtract)
            last.then_inc(centred, 1)
            dve.wait_ge(squared, 1)
            nc.vector.tensor_scalar(stat[:, 4:6], stat[:, 4:6], 1.0 / N, None, ALU.mult).then_inc(scaled_ready, 1)
            dve.wait_ge(rooted, 1)
            step(nc.vector.reciprocal(stat[:, 4:6], stat[:, 4:6]))
            nc.vector.tensor_tensor(stat[:, 6:8], stat[:, 4:6], m.vec("L2_gnn_gamma"), ALU.mult).then_inc(scaled_ready, 1)
            for f in range(KD):
                step(nc.vector.tensor_tensor(m.xT[:, f, :], m.xT[:, f, :], m.yT[:, f, :], ALU.add))
                dve.wait_ge(relu_done, f + 1)
                nc.vector.tensor_tensor(m.xT[:, f, 0:N], m.xT[:, f, 0:N], sums[:, f, 0:N], ALU.add)


def experts_for_all(m):
    nc, ins = m.nc, m.ins
    HT = H1 // P
    CAP = float(ceil(N * 1.25 / NE))
    w1 = m.part(m.REG, 2, KD * H1).rearrange("p e (k h) -> p e k h", k=KD)
    w2 = m.part(m.REG + 2048, 2, HT * D).rearrange("p e (h o) -> p e h o", h=HT)
    wr = m.part(m.REG + 4096, KD, NE)
    b1 = m.part(m.REG + 4112, 2, HT)
    b2 = m.part(m.REG + 4120, 2, KD)
    bias = m.part(m.REG + 4124, KD)
    hidden = m.part(m.REG + 4200, 2, HT, CH)
    mean = m.small[:, 0:KD]
    row = lambda j: m.small[0:1, 16 + NE * j:16 + NE * (j + 1)]
    br, logit, weight, scale, picked, masked, order, t8 = (row(j) for j in range(8))
    one = lambda j: m.small[0:1, 100 + j:101 + j]
    chosen = m.small[0:1, 120:122].bitcast(I32)
    order_i = m.small[0:1, 130:138].bitcast(I32)
    both = m.small[:, 140:142]
    with phase(m, "loaded", "ordered", "averaged", "multiplied", "centred", "exped", "dve_step", "chosen_ready",
               "w_loaded", "gates_ready", "gates_spread") as \
            (block, loaded, ordered, averaged, multiplied, centred, exped, dve_step, chosen_ready,
             w_loaded, gates_ready, gates_spread):

        @block.sync
        def _(sp):
            sp.dma_start(wr, ins["L2_ffn_Wr"].rearrange("(k p) e -> p k e", p=P)).then_inc(loaded, 16)
            sp.dma_start(br, ins["L2_ffn_br"]).then_inc(loaded, 16)
            for j in range(2):
                sp.wait_ge(chosen_ready, j + 1)
                e = sp.value_load(chosen[0:1, j:j + 1], min_val=0, max_val=NE - 1)
                one_of = lambda name: ins[name][ds(e, 1)]
                sp.dma_start(w1[:, j, :, :], one_of("L2_ffn_W1").rearrange("e (k p) h -> p (e k) h", p=P)).then_inc(w_loaded, 16)
                sp.dma_start(w2[:, j, :, :], one_of("L2_ffn_W2").rearrange("e (h p) o -> p (e h) o", p=P)).then_inc(w_loaded, 16)
                sp.dma_start(b1[:, j, :], one_of("L2_ffn_b1").rearrange("e p h -> p (e h)")).then_inc(w_loaded, 16)
                sp.dma_start(b2[:, j, :], one_of("L2_ffn_b2").rearrange("e p f -> p (e f)")).then_inc(w_loaded, 16)
            sp.wait_ge(w_loaded, 16 * 8)

        @block.gpsimd
        def _(pool):
            nc.gpsimd.iota(order_i, [[-1, NE]], base=NE, channel_multiplier=0).then_inc(ordered, 1)
            pool.wait_ge(ordered, 1)
            nc.gpsimd.tensor_copy(order, order_i).then_inc(ordered, 1)

        @block.tensor
        def _(pe):
            pe.wait_ge(loaded, 32)
            pe.wait_ge(averaged, 1)
            for k in range(KD):
                last = nc.tensor.matmul(m.banks[0][0:1, 0:NE], mean[:, k:k + 1], wr[:, k, :], start=k == 0,
                                        stop=k == KD - 1)
            last.then_inc(multiplied, 1)
            pe.wait_ge(gates_ready, 1)
            nc.tensor.matmul(m.banks[1][:, 0:2], m.ones[0:1, :], m.small[0:1, 108:110], start=True, stop=True)\
                .then_inc(gates_spread, 1)

        @block.scalar
        def _(act):
            for n, v in enumerate((weight, weight, one(3))):
                act.wait_ge(centred, n + 1)
                nc.scalar.activation(v, v, ACT.Exp).then_inc(exped, 1)

        @block.vector
        def _(dve):
            step = Steps(dve, dve_step)
            for k in range(KD):
                last = nc.vector.tensor_reduce(mean[:, k:k + 1], m.yT[:, k, 0:N], AX, ALU.add)
            step(last)
            nc.vector.tensor_scalar(mean, mean, 1.0 / N, None, ALU.mult).then_inc(averaged, 1)
            dve.wait_ge(multiplied, 1)
            step(nc.vector.tensor_tensor(logit, m.banks[0][0:1, 0:NE], br, ALU.add))

            def softmax(of, n):
                step(nc.vector.tensor_reduce(one(0), of, AX, ALU.max))
                nc.vector.tensor_scalar(weight, of, one(0), None, ALU.subtract).then_inc(centred, 1)
                dve.wait_ge(exped, n)
                step(nc.vector.tensor_reduce(one(1), weight, AX, ALU.add))
                step(nc.vector.reciprocal(one(1), one(1)))
                step(nc.vector.tensor_scalar(weight, weight, one(1), None, ALU.mult))

            softmax(logit, 1)
            step(nc.vector.tensor_scalar(scale, weight, float(N), 1e-30, ALU.mult, ALU.max))
            step(nc.vector.reciprocal(scale, scale))
            step(nc.vector.tensor_scalar(scale, scale, CAP, 1.0, ALU.mult, ALU.min))
            step(nc.vector.tensor_tensor(scale, scale, weight, ALU.mult))
            softmax(scale, 2)
            dve.wait_ge(ordered, 2)
            for j, of in enumerate((weight, masked)):
                step(nc.vector.tensor_reduce(one(4 + j), of, AX, ALU.max))
                step(nc.vector.tensor_scalar(t8, of, one(4 + j), None, ALU.is_equal))
                step(nc.vector.tensor_tensor(t8, t8, order, ALU.mult))
                step(nc.vector.tensor_reduce(one(6), t8, AX, ALU.max))
                step(nc.vector.tensor_scalar(picked, t8, one(6), None, ALU.is_equal))
                step(nc.vector.tensor_scalar(one(6), one(6), -1.0, float(NE), ALU.mult, ALU.add))
                nc.vector.tensor_copy(chosen[0:1, j:j + 1], one(6)).then_inc(chosen_ready, 1)
                if j == 0:
                    step(nc.vector.scalar_tensor_tensor(masked, picked, -1e30, weight, ALU.mult, ALU.add))
            nc.vector.tensor_tensor(one(3), one(5), one(4), ALU.subtract).then_inc(centred, 1)
            dve.wait_ge(exped, 3)
            step(nc.vector.tensor_scalar(one(2), one(3), 1.0, None, ALU.add))
            step(nc.vector.reciprocal(one(8), one(2)))
            nc.vector.tensor_tensor(one(9), one(8), one(3), ALU.mult).then_inc(gates_ready, 1)
            dve.wait_ge(gates_spread, 1)
            step(nc.vector.tensor_copy(both, m.banks[1][:, 0:2]))
            dve.wait_ge(w_loaded, 16 * 8)
            for j in range(2):
                g = both[:, j:j + 1]
                nc.vector.tensor_scalar(w2[:, j, :, :], w2[:, j, :, :], g, None, ALU.mult)
                last = nc.vector.tensor_scalar(b2[:, j, :], b2[:, j, :], g, None, ALU.mult)
            step(last)
            nc.vector.tensor_tensor(bias, b2[:, 0, :], b2[:, 1, :], ALU.add)

    OUT = (4, 5)
    with phase(m, "hidden_ready", "gelu_done", "consumed", "out_ready", "added") as \
            (block, hidden_ready, gelu_done, consumed, out_ready, added):

        @block.tensor
        def _(pe):
            with pe.Fori(0, NCH) as c:
                cols = ds(c * CH, CH)

                def up(e):
                    for h in range(HT):
                        pe.wait_ge(gelu_done, (c * 2 + e) * HT + h + 1)
                        for k in range(KD):
                            last = nc.tensor.matmul(m.banks[h][:, 0:CH], w1[:, e, k, h * P:(h + 1) * P],
                                                    m.yT[:, k, cols], start=k == 0, stop=k == KD - 1)
                        last.then_inc(hidden_ready, 1)

                def down(e):
                    for h in range(HT):
                        pe.wait_ge(gelu_done, (c * 2 + e) * HT + h + 1 + HT)
                        for f in range(KD):
                            last = nc.tensor.matmul(m.banks[OUT[f]][:, 0:CH], w2[:, e, h, f * P:(f + 1) * P],
                                                    hidden[:, e, h, :], start=e == 0 and h == 0,
                                                    stop=e == 1 and h == HT - 1, skip_group_check=True)
                        last.then_inc(consumed, 1)
                    return last

                up(0)
                up(1)
                pe.wait_ge(added, c + 1)
                down(0)
                down(1)
                pe.sem_inc(out_ready, 1)

        @block.scalar
        def _(act):
            act.sem_inc(gelu_done, HT)
            with act.Fori(0, NCH) as c:
                for e in range(2):
                    for h in range(HT):
                        act.wait_ge(hidden_ready, (c * 2 + e) * HT + h + 1)
                        act.wait_ge(consumed, (c * 2 + e) * HT + h + 1)
                        nc.scalar.activation(hidden[:, e, h, :], m.banks[h][:, 0:CH], ACT.Gelu,
                                             bias=b1[:, e, h:h + 1]).then_inc(gelu_done, 1)

        @block.vector
        def _(dve):
            dve.sem_inc(consumed, 2 * HT)
            dve.sem_inc(added, 1)
            with dve.Fori(0, NCH) as c:
                cols = ds(c * CH, CH)
                dve.wait_ge(consumed, (c * 2 + 2) * HT + 2 * HT)
                for f in range(KD):
                    last = nc.vector.scalar_tensor_tensor(m.yT[:, f, cols], m.banks[OUT[f]][:, 0:CH], bias[:, f:f + 1],
                                                          m.yT[:, f, cols], ALU.add, ALU.add)
                last.then_inc(added, 1)

    layer_norm(m, m.yT, m.yT, "L2_ffn_gamma", "L2_ffn_beta", add_to=m.xT)


def experts_deep(m, gate):
    nc, ins = m.nc, m.ins
    w = [m.part(m.REG + l * NE * KD * D, NE, KD * D).rearrange("p e (k h) -> p e k h", k=KD) for l in range(3)]
    scale = m.small[:, 32:64].rearrange("p (l n) -> p l n", l=2)
    bias = m.small[:, 64:96].rearrange("p (l n) -> p l n", l=2)
    bo = m.gathered[0:NE, 0, :]
    hid = m.part(NP, 3, KD, CH)
    act2 = m.part(NP + 3 * KD * CH, 2, KD, CH)
    A, B, OUT, GATE = (0, 1), (2, 3), (4, 5), (6, 7)
    with phase(m, "loaded", "rooted", "dve_step", "folded", "first_ready", "first_done", "second_ready", "second_done",
               "gate_spread", "gated", "consumed", "out_ready", "added", "bank_claimed") as \
            (block, loaded, rooted, dve_step, folded, first_ready, first_done, second_ready, second_done,
             gate_spread, gated, consumed, out_ready, added, bank_claimed):

        @block.sync
        def _(sp):
            for l, name in enumerate(("L3_ffn_W1", "L3_ffn_W2", "L3_ffn_Wo")):
                for e in range(NE):
                    sp.dma_start(w[l][:, e, :, :], ins[name][e].rearrange("(k p) h -> p k h", p=P)).then_inc(loaded, 16)
            sp.dma_start(bo, ins["L3_ffn_bo"]).then_inc(loaded, 16)

        @block.tensor
        def _(pe):
            pe.wait_ge(loaded, 16 * (3 * NE + 1))
            with pe.Fori(0, NCH) as c:
                cols = ds(c * CH, CH)

                def first(e):
                    pe.wait_ge(first_done, c * NE + e + 1)
                    for f in range(KD):
                        for k in range(KD):
                            last = nc.tensor.matmul(m.banks[A[f]][:, 0:CH], w[0][:, e, k, f * P:(f + 1) * P],
                                                    m.yT[:, k, cols], start=k == 0, stop=k == KD - 1)
                    last.then_inc(first_ready, 1)
                    pe.wait_ge(gated, c * NE + e + 1)
                    pe.sem_inc(bank_claimed, 1)
                    nc.tensor.matmul(m.banks[GATE[e % 2]][:, 0:CH], m.pick[:, e, :], gate[:, cols], start=True,
                                     stop=True).then_inc(gate_spread, 1)

                def second(e):
                    pe.wait_ge(first_done, c * NE + e + 1 + 1)
                    pe.wait_ge(second_done, c * NE + e + 1)
                    for f in range(KD):
                        for k in range(KD):
                            last = nc.tensor.matmul(m.banks[B[f]][:, 0:CH], w[1][:, e, k, f * P:(f + 1) * P],
                                                    hid[:, e % 2, k, :], start=k == 0, stop=k == KD - 1)
                    last.then_inc(second_ready, 1)

                def third(e):
                    pe.wait_ge(gated, c * NE + e + 1 + 2)
                    for f in range(KD):
                        for k in range(KD):
                            last = nc.tensor.matmul(m.banks[OUT[f]][:, 0:CH], w[2][:, e, k, f * P:(f + 1) * P],
                                                    act2[:, e % 2, k, :], start=e == 0 and k == 0, stop=False,
                                                    skip_group_check=True)
                    last.then_inc(consumed, 1)

                first(0)
                first(1)
                second(0)
                pe.wait_ge(added, c + 1)
                for e in range(NE):
                    if e + 2 < NE:
                        first(e + 2)
                    if e + 1 < NE:
                        second(e + 1)
                    third(e)
                for f in range(KD):
                    last = nc.tensor.matmul(m.banks[OUT[f]][:, 0:CH], bo[:, f * P:(f + 1) * P], gate[:, cols],
                                            start=False, stop=True, skip_group_check=True)
                last.then_inc(out_ready, 1)

        @block.scalar
        def _(act):
            act.wait_ge(folded, 0)
            for l, n in enumerate("12"):
                last = nc.scalar.activation(scale[:, l, :], m.vec("L3_ffn_v" + n), ACT.Sqrt, bias=m.eps[:, 1:2])
            last.then_inc(rooted, 1)
            act.sem_inc(first_done, 1)
            act.sem_inc(second_done, 1)
            act.wait_ge(folded, 1)
            with act.Fori(0, NCH) as c:

                def relu(e, l, banks, to, ready, done):
                    act.wait_ge(ready, c * NE + e + 1)
                    if l == 0:
                        act.wait_ge(second_ready, c * NE + max(e - 1, 0))
                    else:
                        act.wait_ge(consumed, c * NE + e + 1)
                    for f in range(KD):
                        last = nc.scalar.activation(to[:, e % 2, f, :], m.banks[banks[f]][:, 0:CH], ACT.Relu,
                                                    bias=bias[:, l, e * KD + f:e * KD + f + 1],
                                                    scale=scale[:, l, e * KD + f:e * KD + f + 1])
                    last.then_inc(done, 1)

                relu(0, 0, A, hid, first_ready, first_done)
                for e in range(NE):
                    if e + 1 < NE:
                        relu(e + 1, 0, A, hid, first_ready, first_done)
                    relu(e, 1, B, act2, second_ready, second_done)

        @block.vector
        def _(dve):
            step = Steps(dve, dve_step)
            dve.sem_inc(gated, 2)
            dve.sem_inc(consumed, 2)
            dve.sem_inc(added, 1)
            dve.wait_ge(rooted, 1)
            step(nc.vector.reciprocal(scale, scale))
            for l, n in enumerate("12"):
                nc.vector.tensor_tensor(bias[:, l, :], m.vec("L3_ffn_b" + n), m.vec("L3_ffn_m" + n), ALU.subtract)
                last = nc.vector.tensor_tensor(scale[:, l, :], scale[:, l, :], m.vec("L3_ffn_g" + n), ALU.mult)
            step(last)
            step(nc.vector.tensor_tensor(bias, bias, scale, ALU.mult))
            for l, n in enumerate("12"):
                last = nc.vector.tensor_tensor(bias[:, l, :], bias[:, l, :], m.vec("L3_ffn_be" + n), ALU.add)
            last.then_inc(folded, 1)
            with dve.Fori(0, NCH) as c:
                for e in range(NE):
                    dve.wait_ge(gate_spread, c * NE + e + 1)
                    dve.wait_ge(second_done, c * NE + e + 1 + 1)
                    for k in range(KD):
                        last = nc.vector.tensor_tensor(act2[:, e % 2, k, :], act2[:, e % 2, k, :],
                                                       m.banks[GATE[e % 2]][:, 0:CH], ALU.mult)
                    last.then_inc(gated, 1)
                dve.wait_ge(out_ready, c + 1)
                cols = ds(c * CH, CH)
                for f in range(KD):
                    last = nc.vector.tensor_tensor(m.xT[:, f, cols], m.xT[:, f, cols], m.banks[OUT[f]][:, 0:CH], ALU.add)
                last.then_inc(added, 1)


def moe_top_two(m):
    layer_norm(m, m.yT, m.yT, "L1_ffn_gamma", "L1_ffn_beta")
    experts_top_two(m, gates(m, "L1_ffn_Wr", "L1_ffn_br", top_two=True))


def program(nc, ins, out, stop=8):
    with ExitStack() as stack:
        m = Machine(nc, stack, ins, out)
        setup(m)
        load_rows(m, ins["x"], m.xT)
        sublayers = [
            lambda: sage(m, "L0_gnn_W1_l", "L0_gnn_W1_r", "L0_gnn_b1", "L0_gnn_W2_l", "L0_gnn_W2_r",
                         "L0_gnn_b2", degrees=True),
            lambda: slice_attention(m),
            lambda: gcn(m),
            lambda: moe_top_two(m),
            lambda: directional(m),
            lambda: experts_for_all(m),
            lambda: sage(m, "L3_gnn_w1_l", "L3_gnn_w1_r", "L3_gnn_b1", "L3_gnn_w2_l", "L3_gnn_w2_r", "L3_gnn_b2"),
            lambda: experts_deep(m, gates(m, "L3_ffn_Wr", "L3_ffn_br", top_two=False)),
        ]
        for sub in sublayers[:stop]:
            layer_norm(m, m.xT, m.yT)
            sub()
        store_rows(m, m.xT, out)




def kernel(**inputs):
    import concourse.bacc as bacc
    from concourse.bass_utils import run_bass_kernel_spmd as run

    a = {k: np.asarray(v) for k, v in inputs.items()}

    def by_group(v, pad):
        full = np.full(P * EG, pad, v.dtype)
        full[:E] = v
        return np.ascontiguousarray(full.reshape(EG, P).T)

    ins = {
        "x": a["x"],
        "src": by_group(a["src"], 0),
        "dst": by_group(a["dst"], PAD_DST),
        "edge_w": by_group(a["edge_attr_2"][:, 0], 0),
        "snorm": np.pad(a["node_vec1"][:, 0], (0, NP - N)),
    }
    for name in ("w1_l", "w1_r", "w2_l", "w2_r"):
        ins[f"L3_gnn_{name}"] = a[f"L3_gnn_{name}"].T
    for name in ("L1_ffn_br", "L3_ffn_br"):
        ins[name] = a[name][:, None]
    ins["L2_ffn_br"] = a["L2_ffn_br"][None]
    for name in ("L2_ffn_b1", "L2_ffn_b2"):
        ins[name] = a[name].reshape(NE, -1, P).transpose(0, 2, 1)
    ins["L0_ffn_W_x_t"] = a["L0_ffn_W_x"].T
    ins["L0_ffn_b_fx"] = a["L0_ffn_b_fx"][None]
    ins["L0_ffn_b_slice"] = a["L0_ffn_b_slice"][None]
    ins["L0_ffn_temperature"] = a["L0_ffn_temperature"].reshape(HEADS)
    for name in ("L0_gnn_W1_l", "L0_gnn_W1_r", "L0_gnn_W2_l", "L0_gnn_W2_r", "L0_ffn_W_fx", "L0_ffn_W_out",
                 "L0_ffn_W_slice", "L0_ffn_W_q", "L0_ffn_W_k", "L0_ffn_W_v", "L1_gnn_W1", "L1_gnn_W2", "L1_gnn_W3",
                 "L1_ffn_Wr", "L1_ffn_W1", "L1_ffn_W2", "L1_ffn_b2", "L2_gnn_W1", "L2_gnn_W2", "L2_ffn_Wr",
                 "L2_ffn_W1", "L2_ffn_W2", "L3_ffn_Wr", "L3_ffn_W1", "L3_ffn_W2", "L3_ffn_Wo", "L3_ffn_bo"):
        ins[name] = a[name]
    ins["vecs"] = np.concatenate([a[n].reshape(-1, P).T for n in VECS], axis=1)
    nc = bacc.Bacc("TRN2", target_bir_lowering=False, num_devices=1)
    arrays, aps = {}, {}
    for name, v in ins.items():
        arrays[f"in_{name}"] = np.ascontiguousarray(v)
        aps[name] = nc.dram_tensor(f"in_{name}", v.shape, mybir.dt.from_np(v.dtype), kind="ExternalInput").ap()
    out = nc.dram_tensor("out", (N, D), F32, kind="ExternalOutput").ap()
    program(nc, aps, out)
    return run(nc, [arrays], core_ids=[0]).results[0]["out"]
```

```python
from contextlib import ExitStack, contextmanager
from math import ceil

import numpy as np

import concourse.bass as bass
from concourse import mybir

F32 = mybir.dt.float32
F32R = mybir.dt.float32r
F16 = mybir.dt.float16
BF16 = mybir.dt.bfloat16
I32 = mybir.dt.int32
U32 = mybir.dt.uint32
ALU = mybir.AluOpType
ACT = mybir.ActivationFunctionType
AX = mybir.AxisListType.X
RMAX = bass.bass_isa.ReduceOp.max
ds = bass.ds

N = 3125
D = 256
P = 128
KD = D // P
TP = 125
NT = N // TP
TU = 5
CH = 392
NCH = 8
NP = CH * NCH
HALF = NP // 2
PARTS = 2
WIN = 16
KEYS = NT * WIN
AW = NP + WIN // 2
BIG = 4 * AW + 16384
DT = 112
NDT = HALF // DT
MOST = 256
E = 53125
EG = 416
EU = 16
SLOTS = 8
AHEAD = 4
BANKS = 4
PAD_DST = 1 << 20
NE = 8
H1 = 512
HEADS = 8
G = 64
HG = HEADS * G

LN_EPS = 1e-5

VECS = {}
_at = 0
for _name, _n in [
    ("L0_gnn_b1", 2), ("L0_gnn_b2", 2), ("L0_ffn_b_out", 2), ("L0_ffn_b_x", 4),
    ("L1_gnn_b1", 2), ("L1_gnn_b2", 2), ("L1_gnn_b3", 2),
    ("L1_ffn_gamma", 2), ("L1_ffn_beta", 2), ("L1_ffn_b1", 32),
    ("L2_gnn_b1", 2), ("L2_gnn_b2", 2), ("L2_gnn_gamma", 2), ("L2_gnn_beta", 2),
    ("L2_ffn_gamma", 2), ("L2_ffn_beta", 2),
    ("L3_gnn_b1", 2), ("L3_gnn_b2", 2),
    ("L3_ffn_b1", 16), ("L3_ffn_g1", 16), ("L3_ffn_be1", 16), ("L3_ffn_m1", 16), ("L3_ffn_v1", 16),
    ("L3_ffn_b2", 16), ("L3_ffn_g2", 16), ("L3_ffn_be2", 16), ("L3_ffn_m2", 16), ("L3_ffn_v2", 16),
]:
    VECS[_name] = (_at, _n)
    _at += _n
NVEC = _at


class Machine:

    def __init__(self, nc, stack, ins, out):
        self.nc, self.stack, self.ins, self.out = nc, stack, ins, out
        self.stale = []
        self.in_branch = False
        self.rooms = 0
        sb = self.sb
        self.degree = sb("degree", [P, AW])
        self.onehot = sb("onehot", [P, 1536])
        self.flag = sb("flag", [1, 1], I32)
        self.spans = sb("spans", [P, 4])
        self.src = sb("src", [P, EG], I32)
        self.dst_rel = sb("dst_rel", [P, EG + SLOTS])
        self.edge_w = sb("edge_w", [P, EG + SLOTS])
        self.edge_abs = sb("edge_abs", [P, EG + SLOTS])
        self.base = sb("base", [1, EG], I32)
        self.src_cols = sb("src_cols", [P, 2, SLOTS], I32)
        self.ident = sb("ident", [P, P])
        self.ones = sb("ones", [P, P])
        self.mean_of = sb("mean_of", [P, P])
        self.count = sb("count", [P, P])
        self.zeros = sb("zeros", [P, CH], BF16)
        self.pick = sb("pick", [NE, NE, P])
        self.vecs = sb("vecs", [P, NVEC])
        self.eps = sb("eps", [P, 2])
        self.small = sb("small", [P, 320])
        self.banks = [stack.enter_context(nc.psum_tensor(f"bank{i}", [P, 512], F32)) for i in range(8)]
        self.fetched = [stack.enter_context(nc.semaphore(f"fetched{s}")) for s in range(SLOTS)]
        self.table = nc.dram_tensor("table", [N, D], F32, kind="Internal").ap()
        self.counts = nc.dram_tensor("counts", [2, NT, TP, HALF], BF16, kind="Internal").ap()
        self.counts_rest = nc.dram_tensor("counts_rest", [2, NT, TP, HALF], BF16, kind="Internal").ap()

    def place_activations(self):
        self.yT = self.sb("activations", [P, KD, NP])
        self.xT = self.sb("residual", [P, KD, NP])

    @contextmanager
    def room(self, words=BIG, split=0):
        with ExitStack() as stack:
            self.rooms += 1
            self.big = stack.enter_context(self.nc.sbuf_tensor(f"big{self.rooms}", [P, words], F32))
            if split:
                self.split = stack.enter_context(self.nc.sbuf_tensor(f"split{self.rooms}", [P, split], F32R))
            else:
                self.gathered = stack.enter_context(self.nc.sbuf_tensor(f"gathered{self.rooms}", [P, SLOTS, D], F32))
            yield

    def sb(self, name, shape, dt=F32):
        return self.stack.enter_context(self.nc.sbuf_tensor(name, shape, dt))

    def vec(self, name, i=None):
        at, n = VECS[name]
        return self.vecs[:, at:at + n] if i is None else self.vecs[:, at + i:at + i + 1]

    def part(self, at, *shape):
        n = int(np.prod(shape))
        v = self.big[:, at:at + n]
        if len(shape) == 2:
            v = v.rearrange("p (a b) -> p a b", a=shape[0])
        if len(shape) == 3:
            v = v.rearrange("p (a b c) -> p a b c", a=shape[0], b=shape[1])
        return v

    @property
    def sums(self):
        return self.part(0, 6, AW)

    REG = 4 * AW


@contextmanager
def phase(m, *names):
    with ExitStack() as stack:
        sems = [stack.enter_context(m.nc.semaphore(n)) for n in names]
        stale, m.stale = m.stale, sems
        block = stack.enter_context(m.nc.Block())
        if m.in_branch:
            for engine in (block.sync, block.scalar, block.vector, block.tensor, block.gpsimd):
                @engine
                def _(eng):
                    eng.nop()

        @block.sync
        def _(sp):
            for s in stale:
                sp.sem_clear(s)

        yield block, *sems


@contextmanager
def branch(m, cond):
    with cond:
        m.in_branch = True
        before, m.stale = m.stale, []
        yield
        m.stale = before + m.stale
        m.in_branch = False


def settle(m):
    with phase(m):
        pass


class Steps:

    def __init__(self, eng, sem):
        self.eng, self.sem, self.n = eng, sem, 0

    def __call__(self, ins):
        ins.then_inc(self.sem, 1)
        self.n += 1
        self.eng.wait_ge(self.sem, self.n)


def tile_at(i, u, width, per):
    return ds(i * (width * per) + u * width, width)


def setup(m, lo, key):
    nc, ins = m.nc, m.ins
    dst = m.part(0, EG).bitcast(I32)
    neg = m.part(EG, EG)
    neg_base = m.part(2 * EG, EG)
    dst_f = m.part(3 * EG, EG)
    src_f = m.part(4 * EG, EG)
    base_f = m.part(5 * EG, EG)
    tile_i = m.part(6 * EG, EG).bitcast(I32)
    off = m.part(7 * EG, EG)
    real = m.part(8 * EG, EG)
    iota_i = m.part(9 * EG, KEYS).bitcast(I32)
    with phase(m, "loaded", "pool_step", "dst_ready", "base_ready", "dve_step") as \
            (block, loaded, pool_step, dst_ready, base_ready, dve_step):

        @block.sync
        def _(sp):
            sp.dma_start(dst, ins["dst"]).then_inc(loaded, 16)
            sp.dma_start(m.src[:, :], ins["src"]).then_inc(loaded, 16)
            sp.dma_start(m.edge_w[:, 0:EG], ins["edge_w"]).then_inc(loaded, 16)
            sp.dma_start(m.vecs[:, :], ins["vecs"]).then_inc(loaded, 16)
            sp.wait_ge(loaded, 64)

        @block.gpsimd
        def _(pool):
            step = Steps(pool, pool_step)
            nc.gpsimd.memset(m.ones[:, :], 1.0)
            nc.gpsimd.memset(m.mean_of[:, :], 1.0 / D)
            nc.gpsimd.memset(m.eps[:, 0:1], LN_EPS)
            nc.gpsimd.memset(m.eps[:, 1:2], 1e-3)
            nc.gpsimd.memset(m.pick[:, :, :], 1.0)
            nc.gpsimd.memset(m.zeros[:, :], 0.0)
            nc.gpsimd.memset(m.dst_rel[:, EG:], 0.0)
            nc.gpsimd.memset(m.edge_w[:, EG:], 0.0)
            nc.gpsimd.memset(lo[:, EG:], 0.0)
            nc.gpsimd.memset(key[:, EG:], 0.0)
            step(nc.gpsimd.iota(iota_i, [[1, KEYS]], base=0, channel_multiplier=0))
            nc.gpsimd.tensor_copy(m.count[:, :], iota_i[:, 0:P])
            nc.gpsimd.tensor_copy(key_count(m), iota_i)
            nc.gpsimd.affine_select(m.ident[:, :], m.ones[:, :], [[1, P]], ALU.is_equal, 0.0,
                                    base=0, channel_multiplier=-1)
            step(nc.gpsimd.affine_select(m.pick[:, :, :], m.pick[:, :, :], [[1, NE], [0, P]],
                                         ALU.is_equal, 0.0, base=0, channel_multiplier=-1))
            pool.wait_ge(dst_ready, 1)
            nc.gpsimd.partition_all_reduce(neg_base, neg, P, RMAX).then_inc(base_ready, 1)

        @block.scalar
        def _(act):
            act.wait_ge(loaded, 64)
            act.wait_ge(pool_step, 1)
            nc.scalar.activation(m.edge_abs[:, :], m.edge_w[:, :], ACT.Abs)

        @block.vector
        def _(dve):
            step = Steps(dve, dve_step)
            dve.wait_ge(loaded, 64)
            step(nc.vector.tensor_copy(dst_f, dst))
            dve.wait_ge(pool_step, 1)
            nc.vector.tensor_scalar(neg, dst_f, -1.0, None, ALU.mult).then_inc(dst_ready, 1)
            step(nc.vector.tensor_copy(src_f, m.src[:, :]))
            step(nc.vector.tensor_scalar(off, src_f, 1.0 / TP, -0.496, ALU.mult, ALU.add))
            step(nc.vector.tensor_copy(tile_i, off))
            step(nc.vector.tensor_copy(key[:, 0:EG], tile_i))
            for bound, sign in ((TP - 0.5, 1.0), (-0.5, -1.0)):
                step(nc.vector.scalar_tensor_tensor(lo[:, 0:EG], key[:, 0:EG], -float(TP), src_f, ALU.mult, ALU.add))
                step(nc.vector.tensor_scalar(off, lo[:, 0:EG], bound, sign, ALU.is_gt if sign > 0 else ALU.is_lt,
                                             ALU.mult))
                step(nc.vector.tensor_tensor(key[:, 0:EG], key[:, 0:EG], off, ALU.add))
            step(nc.vector.scalar_tensor_tensor(lo[:, 0:EG], key[:, 0:EG], -float(TP), src_f, ALU.mult, ALU.add))
            dve.wait_ge(base_ready, 1)
            step(nc.vector.tensor_tensor(m.dst_rel[:, 0:EG], dst_f, neg_base, ALU.add))
            nc.vector.scalar_tensor_tensor(key[:, 0:EG], key[:, 0:EG], float(WIN), m.dst_rel[:, 0:EG],
                                           ALU.mult, ALU.add)
            step(nc.vector.scalar_tensor_tensor(real, m.dst_rel[:, 0:EG], float(PAD_DST // 2), m.dst_rel[:, 0:EG],
                                                ALU.is_lt, ALU.mult))
            nc.vector.tensor_reduce(m.spans[:, 0:1], real, AX, ALU.max)
            step(nc.vector.tensor_scalar(base_f[0:1, :], neg_base[0:1, :], -1.0, None, ALU.mult))
            step(nc.vector.tensor_copy(m.base[:, :], base_f[0:1, :]))


def key_count(m):
    return m.onehot[:, 1200:1200 + KEYS // 2].bitcast(F16)


def build_counts(m, counts, lo, key, hot):
    nc = m.nc
    src_hot = hot[:, 0:2 * AHEAD * P].rearrange("p (s n) -> p s n", s=2 * AHEAD)
    key_hot = hot[:, 2 * AHEAD * P:].rearrange("p (s n) -> p s n", s=2 * AHEAD)
    lo_h, count_h = m.onehot[:, 0:(EG + 2 * AHEAD) // 2].bitcast(F16), m.onehot[:, 600:600 + P // 2].bitcast(F16)
    with phase(m, "src_made", "key_made", "multiplied", "added", "cleared", "dve_step") as \
            (block, src_made, key_made, multiplied, added, cleared, dve_step):

        @block.gpsimd
        def _(pool):
            nc.gpsimd.memset(counts[:, NT // 2:, :], 0.0).then_inc(cleared, 1)

        @block.tensor
        def _(pe):
            with pe.Fori(0, EG // EU) as i:
                for k in range(EU):
                    s = k % (2 * AHEAD)
                    pe.wait_ge(src_made, i * (EU // AHEAD) + k // AHEAD + 1)
                    pe.wait_ge(key_made, i * EU + k + 1)
                    pe.wait_ge(added, i * EU + k + 1)
                    nc.tensor.matmul(m.banks[k % BANKS][:, 0:KEYS], src_hot[:, s, :], key_hot[:, s, :],
                                     start=True, stop=True).then_inc(multiplied, 1)

        @block.vector
        def _(dve):
            step = Steps(dve, dve_step)

            def make_src(o, c):
                nc.vector.tensor_tensor(src_hot[:, o:o + AHEAD, :], repeat_first(count_h, AHEAD),
                                        repeat_last(lo_h[:, ds(c, AHEAD)], P), ALU.is_equal).then_inc(src_made, 1)

            def make_key(o, c):
                nc.vector.tensor_scalar(key_hot[:, o, :], key_count(m), key[:, ds(c, 1)], None, ALU.is_equal)\
                    .then_inc(key_made, 1)

            nc.vector.tensor_copy(count_h, m.count[:, :])
            step(nc.vector.tensor_copy(lo_h, lo[:, 0:EG + 2 * AHEAD]))
            for b in range(2):
                make_src(b * AHEAD, b * AHEAD)
            for k in range(2 * AHEAD):
                make_key(k, k)
            nc.vector.memset(counts[:, 0:NT // 2, :], 0.0).then_inc(cleared, 1)
            dve.wait_ge(cleared, 2)
            dve.sem_inc(added, BANKS)
            with dve.Fori(0, EG // EU) as i:
                for k in range(EU):
                    at = dve.value_load(m.base[0:1, ds(i * EU + k, 1)], min_val=0, max_val=N - 1)
                    dve.wait_ge(multiplied, i * EU + k + 1)
                    dve.wait_ge(added, i * EU + k + BANKS)
                    view = counts[:, :, ds(at, WIN)]
                    nc.vector.tensor_tensor(view, view, m.banks[k % BANKS][:, 0:KEYS].rearrange("p (t n) -> p t n", t=NT),
                                            ALU.add).then_inc(added, 1)
                    make_key(k % (2 * AHEAD), i * EU + k + 2 * AHEAD)
                    if k % AHEAD == AHEAD - 1:
                        b = k // AHEAD
                        make_src(b % 2 * AHEAD, i * EU + (b + 2) * AHEAD)

    ones = m.onehot[:, 0:P // 2].bitcast(BF16)
    degree = m.degree[:, 0:NP]
    with phase(m, "stored", "ones_ready", "multiplied", "taken", "spans_ready", "dve_step") as \
            (block, stored, ones_ready, multiplied, taken, spans_ready, dve_step):

        @block.sync
        def _(sp):
            for h in range(2):
                for t in range(0, NT, 5):
                    sp.dma_start(m.counts[h, t:t + 5].rearrange("t p n -> p t n"),
                                 counts[0:TP, t:t + 5, h * HALF:(h + 1) * HALF]).then_inc(stored, 16)
            sp.wait_ge(stored, 16 * 10)

        @block.tensor
        def _(pe):
            pe.wait_ge(ones_ready, 1)
            for c in range(NCH):
                for t in range(NT):
                    last = nc.tensor.matmul(m.banks[c][:, 0:CH], ones, counts[:, t, c * CH:(c + 1) * CH],
                                            start=t == 0, stop=t == NT - 1)
                last.then_inc(multiplied, 1)

        @block.gpsimd
        def _(pool):
            nc.gpsimd.memset(ones, 1.0).then_inc(ones_ready, 1)
            pool.wait_ge(taken, 1)
            nc.gpsimd.partition_all_reduce(m.spans[:, 1:2], m.spans[:, 0:1], P, RMAX).then_inc(spans_ready, 1)

        @block.vector
        def _(dve):
            step = Steps(dve, dve_step)
            for c in range(NCH):
                dve.wait_ge(multiplied, c + 1)
                last = nc.vector.tensor_copy(degree[:, c * CH:(c + 1) * CH], m.banks[c][:, 0:CH])
            step(last)
            nc.vector.tensor_reduce(m.spans[:, 2:3], degree, AX, ALU.max).then_inc(taken, 1)
            dve.wait_ge(spans_ready, 1)
            dve.wait_ge(taken, 1)
            nc.vector.tensor_scalar(m.spans[:, 1:2], m.spans[:, 1:2], WIN - 0.5, None, ALU.is_gt)
            step(nc.vector.tensor_scalar(m.spans[:, 2:3], m.spans[:, 2:3], MOST - 0.5, None, ALU.is_gt))
            step(nc.vector.tensor_tensor(m.spans[:, 0:1], m.spans[:, 1:2], m.spans[:, 2:3], ALU.add))
            nc.vector.tensor_copy(m.flag[:, :], m.spans[0:1, 0:1])


def if_general(m):
    settle(m)
    flag = m.nc.values_load(m.flag[0:1, 0:1], min_val=0, max_val=2)
    return branch(m, m.nc.If(flag > 0))


def general_sums(m, weighted=False):
    nc, ins = m.nc, m.ins
    nw = 3 if weighted else 1
    W = nw * DT
    at = [6 * AW + 2 * AW if weighted else 0]

    def reg(n):
        at[0] += n
        return m.part(at[0] - n, n)

    rel, src_f, src_rel, raw = reg(EG), reg(EG), reg(EG), reg(EG)
    hot = m.onehot[:, 0:2 * (P + W)].rearrange("p (u n) -> p u n", u=2)
    block_sums, acc, rows = reg(W), reg(3 * W).rearrange("p (f n) -> p f n", f=3), reg(D)
    if not weighted:
        hi, lo, back = reg(W // 2).bitcast(BF16), reg(W // 2).bitcast(BF16), reg(W)
    with phase(m, "loaded", "dve_step") as (block, loaded, dve_step):

        @block.sync
        def _(sp):
            sp.dma_start(raw.bitcast(I32), ins["dst"]).then_inc(loaded, 16)

        @block.vector
        def _(dve):
            nc.vector.tensor_copy(src_f, m.src[:, :])
            dve.wait_ge(loaded, 16)
            nc.vector.tensor_copy(rel, raw.bitcast(I32))

    with nc.Fori(0, 2) as h, nc.Fori(0, NDT) as j:
        with phase(m) as (block,):

            @block.vector
            def _(dve):
                nc.vector.tensor_copy(src_rel, src_f)
                nc.vector.memset(acc, 0.0)

        with nc.Fori(0, NT) as t:
            with phase(m, "made", "multiplied", "dve_step", "acc_ready", "block_ready", "rows_loaded", "stored") as \
                    (block, made, multiplied, dve_step, acc_ready, block_ready, rows_loaded, stored):

                @block.sync
                def _(sp):
                    if weighted:
                        sp.dma_start(rows[0:TP, :], m.table[ds(t * TP, TP), :]).then_inc(rows_loaded, 16)
                    else:
                        sp.wait_ge(block_ready, 2)
                        for of, to in ((hi, m.counts), (lo, m.counts_rest)):
                            sp.dma_start(to[ds(h, 1), ds(t, 1), :, ds(j * DT, DT)].rearrange("a b p n -> p (a b n)"),
                                         of[0:TP, :]).then_inc(stored, 16)
                        sp.wait_ge(stored, 32)

                @block.tensor
                def _(pe):
                    bank = m.banks[0][:, 0:W]
                    nc.tensor.matmul(bank, m.zeros[:, 0:P], m.zeros[:, 0:W], start=True, stop=False)
                    with pe.Fori(0, EG // 2) as i:
                        for u in range(2):
                            pe.wait_ge(made, i * 2 + u + 1)
                            nc.tensor.matmul(bank, hot[:, u, 0:P], hot[:, u, P:], start=False, stop=False,
                                             skip_group_check=True).then_inc(multiplied, 1)
                    nc.tensor.matmul(bank, m.zeros[:, 0:P], m.zeros[:, 0:W], start=False, stop=True)\
                        .then_inc(multiplied, 1)
                    pe.wait_ge(block_ready, 1)
                    if weighted:
                        pe.wait_ge(rows_loaded, 16)
                        for f in range(KD):
                            nc.tensor.matmul(m.banks[1 + f][:, 0:W], rows[0:TP, f * P:(f + 1) * P],
                                             block_sums[0:TP, :], start=True, stop=True)
                    nc.tensor.matmul(m.banks[3][:, 0:W], m.ones[0:TP, :], block_sums[0:TP, :], start=True,
                                     stop=True).then_inc(acc_ready, 1)

                @block.vector
                def _(dve):
                    dve.sem_inc(multiplied, 2)
                    with dve.Fori(0, EG // 2) as i:
                        for u in range(2):
                            c = ds(i * 2 + u, 1)
                            dve.wait_ge(multiplied, i * 2 + u + 1)
                            nc.vector.tensor_scalar(hot[:, u, 0:P], m.count[:, :], src_rel[:, c], None, ALU.is_equal)
                            if weighted:
                                for w, of in ((1, m.edge_abs), (2, m.edge_w)):
                                    nc.vector.tensor_scalar(hot[:, u, P + w * DT:P + (w + 1) * DT], m.count[:, 0:DT],
                                                            rel[:, c], of[:, c], ALU.is_equal, ALU.mult)
                            nc.vector.tensor_scalar(hot[:, u, P:P + DT], m.count[:, 0:DT], rel[:, c], None,
                                                    ALU.is_equal).then_inc(made, 1)
                    step = Steps(dve, dve_step)
                    dve.wait_ge(multiplied, EG + 3)
                    nc.vector.tensor_copy(block_sums, m.banks[0][:, 0:W]).then_inc(block_ready, 1)
                    nc.vector.tensor_scalar(src_rel, src_rel, -float(TP), None, ALU.add)
                    if not weighted:
                        dve.wait_ge(block_ready, 1)
                        step(nc.vector.tensor_copy(hi, block_sums))
                        step(nc.vector.tensor_copy(back, hi))
                        nc.vector.tensor_tensor(lo, block_sums, back, ALU.subtract).then_inc(block_ready, 1)
                    dve.wait_ge(acc_ready, 1)
                    for f in range(0 if weighted else 2, 3):
                        nc.vector.tensor_tensor(acc[:, f, :], acc[:, f, :], m.banks[1 + f][:, 0:W], ALU.add)

            settle(m)

        with phase(m) as (block,):

            @block.vector
            def _(dve):
                cols = ds(h * HALF + j * DT, DT)
                nc.vector.tensor_scalar(rel, rel, -float(DT), None, ALU.add)
                if weighted:
                    for w in range(3):
                        for f in range(KD):
                            nc.vector.tensor_copy(m.sums[:, 2 * w + f, cols], acc[:, f, w * DT:(w + 1) * DT])
                        if w:
                            nc.vector.tensor_copy(m.part(6 * AW, 2, AW)[:, w - 1, cols], acc[:, 2, w * DT:(w + 1) * DT])
                else:
                    nc.vector.tensor_copy(m.degree[:, cols], acc[:, 2, :])


def load_rows(m, rows, to):
    nc = m.nc
    stage = m.part(0, TU, D)
    with phase(m, "row_free", "transposed", *[f"row_loaded{u}" for u in range(TU)], "evacuated") as \
            (block, row_free, transposed, *row_loaded, evacuated):

        @block.sync
        def _(sp):
            with sp.Fori(0, NT // TU) as i:
                for u in range(TU):
                    sp.wait_ge(transposed, i * TU + u + 1)
                    sp.dma_start(stage[0:TP, u, :], rows[ds(i * (TU * TP) + u * TP, TP), :])\
                        .then_inc(row_loaded[u], 16)

        @block.gpsimd
        def _(pool):
            nc.gpsimd.memset(to[:, :, N:NP], 0.0)

        @block.tensor
        def _(pe):
            pe.sem_inc(transposed, TU)
            with pe.Fori(0, NT // TU) as i:
                for u in range(TU):
                    pe.wait_ge(row_loaded[u], i * 16 + 16)
                    pe.wait_ge(evacuated, i * TU + u + 1)
                    for k in range(KD):
                        last = nc.tensor.transpose(m.banks[u][:, k * TP:(k + 1) * TP],
                                                   stage[0:TP, u, k * P:(k + 1) * P], m.ident[0:TP, 0:TP])
                    last.then_inc(transposed, 1)

        @block.vector
        def _(dve):
            dve.sem_inc(evacuated, TU)
            with dve.Fori(0, NT // TU) as i:
                for u in range(TU):
                    dve.wait_ge(transposed, i * TU + u + 1 + TU)
                    nc.vector.tensor_copy(to[:, :, tile_at(i, u, TP, TU)],
                                          m.banks[u][:, 0:KD * TP].rearrange("p (k n) -> p k n", k=KD))\
                        .then_inc(evacuated, 1)


def store_rows(m, of, rows):
    nc = m.nc
    cols = m.part(0, TU, KD, TP)
    tile = m.part(TU * KD * TP, TU, D)
    with phase(m, "staged", "transposed", *[f"row_stored{u}" for u in range(TU)], "evacuated") as \
            (block, staged, transposed, *row_stored, evacuated):

        @block.scalar
        def _(act):
            with act.Fori(0, NT // TU) as i:
                for u in range(TU):
                    act.wait_ge(transposed, i * TU + u + 1)
                    nc.scalar.copy(cols[:, u, :, :], of[:, :, tile_at(i, u, TP, TU)]).then_inc(staged, 1)

        @block.tensor
        def _(pe):
            pe.sem_inc(transposed, TU)
            with pe.Fori(0, NT // TU) as i:
                for u in range(TU):
                    pe.wait_ge(staged, i * TU + u + 1)
                    pe.wait_ge(evacuated, i * TU + u + 1)
                    for k in range(KD):
                        last = nc.tensor.transpose(m.banks[u][0:TP, k * P:(k + 1) * P],
                                                   cols[:, u, k, :], m.ident[:, :])
                    last.then_inc(transposed, 1)

        @block.vector
        def _(dve):
            dve.sem_inc(evacuated, TU)
            with dve.Fori(0, NT // TU) as i:
                for u in range(TU):
                    dve.wait_ge(transposed, i * TU + u + 1 + TU)
                    dve.wait_ge(row_stored[u], i * 16 + 16)
                    nc.vector.tensor_copy(tile[0:TP, u, :], m.banks[u][0:TP, 0:D]).then_inc(evacuated, 1)

        @block.sync
        def _(sp):
            for u in range(TU):
                sp.sem_inc(row_stored[u], 16)
            with sp.Fori(0, NT // TU) as i:
                for u in range(TU):
                    sp.wait_ge(evacuated, i * TU + u + 1 + TU)
                    sp.dma_start(rows[ds(i * (TU * TP) + u * TP, TP), :], tile[0:TP, u, :])\
                        .then_inc(row_stored[u], 16)
            for u in range(TU):
                sp.wait_ge(row_stored[u], 16 * (NT // TU) + 16)


def layer_norm(m, of, to, gamma=None, beta=None, add_to=None):
    nc = m.nc
    LU = 4
    squares = m.part(0, LU, KD, CH)
    root = m.part(LU * KD * CH, LU, CH)
    with phase(m, "mean_ready", "centred", "squared", "var_ready", "root_ready", "normed", "scaled", "dve_step") as \
            (block, mean_ready, centred, squared, var_ready, root_ready, normed, scaled, dve_step):

        @block.tensor
        def _(pe):
            pe.sem_inc(var_ready, LU)
            with pe.Fori(0, NCH // LU) as i:
                for u in range(LU):
                    pe.wait_ge(centred, i * LU + u + 1)
                    for k in range(KD):
                        last = nc.tensor.matmul(m.banks[u][:, 0:CH], m.mean_of[:, :],
                                                of[:, k, tile_at(i, u, CH, LU)], start=k == 0, stop=k == KD - 1)
                    last.then_inc(mean_ready, 1)
                for u in range(LU):
                    pe.wait_ge(squared, i * LU + u + 1)
                    pe.wait_ge(root_ready, i * LU + u + 1)
                    for k in range(KD):
                        last = nc.tensor.matmul(m.banks[LU + u][:, 0:CH], m.mean_of[:, :],
                                                squares[:, u, k, :], start=k == 0, stop=k == KD - 1)
                    last.then_inc(var_ready, 1)

        @block.scalar
        def _(act):
            act.sem_inc(root_ready, LU)
            with act.Fori(0, NCH // LU) as i:
                for u in range(LU):
                    act.wait_ge(centred, i * LU + u + 1 + LU)
                    act.wait_ge(var_ready, i * LU + u + 1)
                    nc.scalar.activation(squares[:, u, :, :], to[:, :, tile_at(i, u, CH, LU)], ACT.Square)\
                        .then_inc(squared, 1)
                for u in range(LU):
                    act.wait_ge(var_ready, i * LU + u + 1 + LU)
                    act.wait_ge(normed, i * LU + u + 1)
                    nc.scalar.activation(root[:, u, :], m.banks[LU + u][:, 0:CH], ACT.Sqrt, bias=m.eps[:, 0:1])\
                        .then_inc(root_ready, 1)

        @block.vector
        def _(dve):
            dve.sem_inc(centred, LU)
            dve.sem_inc(normed, LU)
            with dve.Fori(0, NCH // LU) as i:
                for u in range(LU):
                    dve.wait_ge(mean_ready, i * LU + u + 1)
                    for k in range(KD):
                        cols = tile_at(i, u, CH, LU)
                        last = nc.vector.tensor_tensor(to[:, k, cols], of[:, k, cols], m.banks[u][:, 0:CH],
                                                       ALU.subtract)
                    last.then_inc(centred, 1)
                for u in range(LU):
                    cols = tile_at(i, u, CH, LU)
                    dve.wait_ge(root_ready, i * LU + u + 1 + LU)
                    nc.vector.reciprocal(root[:, u, :], root[:, u, :]).then_inc(dve_step, 1)
                    dve.wait_ge(dve_step, i * LU + u + 1)
                    dve.wait_ge(squared, i * LU + u + 1)
                    for k in range(KD):
                        last = nc.vector.tensor_tensor(to[:, k, cols], to[:, k, cols], root[:, u, :], ALU.mult)
                    last.then_inc(normed, 1)
                    if gamma:
                        dve.wait_ge(normed, i * LU + u + 1 + LU)
                        for k in range(KD):
                            last = nc.vector.tensor_scalar(to[:, k, cols], to[:, k, cols], m.vec(gamma, k),
                                                           m.vec(beta, k), ALU.mult, ALU.add)
                        last.then_inc(scaled, 1)
                    if add_to is not None:
                        dve.wait_ge(scaled, i * LU + u + 1)
                        for k in range(KD):
                            nc.vector.tensor_tensor(add_to[:, k, cols], add_to[:, k, cols], to[:, k, cols], ALU.add)


def turn_rows(m, of):
    nc = m.nc
    cols = m.part(0, TU, KD, TP)
    rows = row_tiles(m)
    with phase(m, "staged", "transposed", "evacuated") as (block, staged, transposed, evacuated):

        @block.scalar
        def _(act):
            with act.Fori(0, NT // TU) as i:
                for u in range(TU):
                    act.wait_ge(transposed, i * TU + u + 1)
                    nc.scalar.copy(cols[:, u, :, :], of[:, :, tile_at(i, u, TP, TU)]).then_inc(staged, 1)

        @block.tensor
        def _(pe):
            pe.sem_inc(transposed, TU)
            with pe.Fori(0, NT // TU) as i:
                for u in range(TU):
                    pe.wait_ge(staged, i * TU + u + 1)
                    pe.wait_ge(evacuated, i * TU + u + 1)
                    for k in range(KD):
                        last = nc.tensor.transpose(m.banks[u][0:TP, k * P:(k + 1) * P],
                                                   cols[:, u, k, :], m.ident[:, :])
                    last.then_inc(transposed, 1)

        @block.vector
        def _(dve):
            dve.sem_inc(evacuated, TU)
            with dve.Fori(0, NT // TU) as i:
                for u in range(TU):
                    dve.wait_ge(transposed, i * TU + u + 1 + TU)
                    nc.vector.tensor_copy(one_tile(rows, i, u), m.banks[u][0:TP, 0:D]).then_inc(evacuated, 1)


def row_tiles(m):
    return m.part(2 * AW + NP, NT, D)


def one_tile(rows, i, u):
    return rows[0:TP, ds(i * TU + u, 1), :].rearrange("p a d -> p (a d)")


SUM_ROOM = 2 * AW + NP + NT * D + TU * HALF // 2
SUM_SPLIT = TU * (HALF + PARTS * D)


def count_product(m, counts, first, with_self=False):
    nc = m.nc
    sums = m.sums
    rows = row_tiles(m)
    stream = m.part(SUM_ROOM - TU * HALF // 2, TU * HALF // 2).bitcast(BF16).rearrange("p (u n) -> p u n", u=TU)
    wide = m.split[:, 0:TU * HALF].rearrange("p (u n) -> p u n", u=TU)
    parts = m.split[:, TU * HALF:SUM_SPLIT].rearrange("p (u s d) -> p u s d", u=TU, s=PARTS)
    Q = HALF // CH
    CUT = HALF // 2
    with phase(m, *[f"counts_loaded{u}" for u in range(TU)], "high_ready", "act_ready", "dve_ready", "consumed",
               "half_ready", "taken") as \
            (block, *counts_loaded, high_ready, act_ready, dve_ready, consumed, half_ready, taken):

        @block.sync
        def _(sp):
            for h in range(2):
                with sp.Fori(0, NT // TU) as i:
                    for u in range(TU):
                        sp.wait_ge(act_ready, h * NT + i * TU + u + 1)
                        sp.wait_ge(dve_ready, h * NT + i * TU + u + 1)
                        sp.dma_start(stream[0:TP, u, :], counts[h][ds(i * TU + u, 1)].rearrange("a p n -> p (a n)"))\
                            .then_inc(counts_loaded[u], 16)

        @block.tensor
        def _(pe):
            pe.sem_inc(consumed, TU)
            for h in range(2):
                if h:
                    pe.wait_ge(taken, 2 * h)
                for bank in m.banks:
                    nc.tensor.matmul(bank[:, 0:CH], m.zeros[:, 0:P], m.zeros[:, :], start=True, stop=False)
                with pe.Fori(0, NT // TU) as i:
                    for u in range(TU):
                        pe.wait_ge(act_ready, h * NT + i * TU + u + 1 + TU)
                        pe.wait_ge(dve_ready, h * NT + i * TU + u + 1 + TU)
                        for part in range(PARTS):
                            for f in range(KD):
                                for q in range(Q):
                                    last = nc.tensor.matmul(m.banks[f * Q + q][:, 0:CH],
                                                            parts[0:TP, u, part, f * P:(f + 1) * P],
                                                            wide[0:TP, u, q * CH:(q + 1) * CH],
                                                            start=False, stop=False, skip_group_check=True)
                        last.then_inc(consumed, 1)
                for bank in m.banks:
                    last = nc.tensor.matmul(bank[:, 0:CH], m.zeros[:, 0:P], m.zeros[:, :], start=False, stop=True)
                last.then_inc(half_ready, 1)

        def take(h, f, plain):
            for q in range(Q):
                cols = slice((h * Q + q) * CH, (h * Q + q + 1) * CH)
                bank = m.banks[f * Q + q][:, 0:CH]
                if not first:
                    last = nc.vector.tensor_tensor(sums[:, f, cols], sums[:, f, cols], bank, ALU.add)
                elif with_self:
                    last = nc.vector.tensor_tensor(sums[:, f, cols], m.yT[:, f, cols], bank, ALU.add)
                else:
                    last = plain(sums[:, f, cols], bank)
            last.then_inc(taken, 1)

        plain_on_act = first and not with_self

        @block.scalar
        def _(act):
            act.sem_inc(act_ready, TU)
            for h in range(2):
                with act.Fori(0, NT // TU) as i:
                    for u in range(TU):
                        act.wait_ge(consumed, h * NT + i * TU + u + 1)
                        nc.scalar.copy(parts[0:TP, u, 0, :], one_tile(rows, i, u)).then_inc(high_ready, 1)
                        act.wait_ge(counts_loaded[u], (h * (NT // TU) + i + 1) * 16)
                        nc.scalar.copy(wide[0:TP, u, 0:CUT], stream[0:TP, u, 0:CUT]).then_inc(act_ready, 1)
                if plain_on_act:
                    act.wait_ge(half_ready, h + 1)
                    take(h, 0, nc.scalar.copy)

        @block.vector
        def _(dve):
            dve.sem_inc(dve_ready, TU)
            for h in range(2):
                with dve.Fori(0, NT // TU) as i:
                    for u in range(TU):
                        dve.wait_ge(consumed, h * NT + i * TU + u + 1)
                        dve.wait_ge(counts_loaded[u], (h * (NT // TU) + i + 1) * 16)
                        nc.vector.tensor_copy(wide[0:TP, u, CUT:], stream[0:TP, u, CUT:])
                        dve.wait_ge(high_ready, h * NT + i * TU + u + 1)
                        nc.vector.tensor_tensor(parts[0:TP, u, 1, :], one_tile(rows, i, u), parts[0:TP, u, 0, :]
                                                .bitcast(F32), ALU.subtract).then_inc(dve_ready, 1)
                dve.wait_ge(half_ready, h + 1)
                if not plain_on_act:
                    take(h, 0, None)
                take(h, 1, nc.vector.tensor_copy)


def neighbour_sums(m, with_self=False):
    turn_rows(m, m.yT)
    count_product(m, m.counts, True, with_self)
    with if_general(m):
        count_product(m, m.counts_rest, False)


def weighted_sums(m):
    nc = m.nc
    all_sums = m.part(0, 8, AW)
    hot = m.onehot[:, 0:SLOTS * 3 * WIN].rearrange("p (s w n) -> p s w n", s=SLOTS, w=3)
    W = 3 * WIN
    fetched = m.fetched
    with phase(m, "staged", "made", "multiplied", "added", "cleared", "slot_claimed") as \
            (block, staged, made, multiplied, added, cleared, slot_claimed):

        @block.scalar
        def _(act):
            with act.Fori(0, EG // EU) as i:
                for h in range(2):
                    act.wait_ge(multiplied, i * EU + h * SLOTS + 1)
                    nc.scalar.copy(m.src_cols[:, h, :], m.src[:, ds(i * EU + h * SLOTS, SLOTS)]).then_inc(staged, 1)

        @block.gpsimd
        def _(pool):
            with pool.Fori(0, EG // EU) as i:
                for k in range(EU):
                    s = k % SLOTS
                    if s == 0:
                        pool.wait_ge(staged, i * 2 + k // SLOTS + 1)
                    pool.wait_ge(multiplied, i * EU + k + 1)
                    pool.sem_inc(slot_claimed, 1)
                    nc.gpsimd.indirect_dma_start(
                        m.gathered[:, s, :], None, m.table,
                        bass.IndirectOffsetOnAxis(ap=m.src_cols[:, k // SLOTS, s:s + 1].bitcast(U32), axis=0),
                    ).then_inc(fetched[s], 16)

        @block.tensor
        def _(pe):
            pe.sem_inc(multiplied, SLOTS)
            with pe.Fori(0, EG // EU) as i:
                for k in range(EU):
                    s, b = k % SLOTS, k % BANKS
                    pe.wait_ge(fetched[s], (i * 2 + k // SLOTS + 1) * 16)
                    pe.wait_ge(made, i * EU + k + 1)
                    pe.wait_ge(added, i * EU + k + 1)
                    for f in range(KD):
                        to = m.banks[b][:, 0:KD * W].rearrange("p (w f n) -> p f w n", w=3, f=KD)[:, f, :, :]
                        nc.tensor.matmul(to, m.gathered[:, s, f * P:(f + 1) * P], hot[:, s, :, :], start=True, stop=True)
                    nc.tensor.matmul(m.banks[b][:, KD * W:KD * W + 2 * WIN], m.ones[:, :], hot[:, s, 1:3, :],
                                     start=True, stop=True).then_inc(multiplied, 1)

        @block.vector
        def _(dve):
            def make(o, c):
                rel = m.dst_rel[:, ds(c, 1)]
                nc.vector.tensor_scalar(hot[:, o, 0, :], m.count[:, 0:WIN], rel, None, ALU.is_equal)
                nc.vector.tensor_scalar(hot[:, o, 2, :], m.count[:, 0:WIN], rel, m.edge_w[:, ds(c, 1)],
                                        ALU.is_equal, ALU.mult)
                nc.vector.tensor_scalar(hot[:, o, 1, :], m.count[:, 0:WIN], rel, m.edge_abs[:, ds(c, 1)],
                                        ALU.is_equal, ALU.mult).then_inc(made, 1)

            for k in range(SLOTS):
                make(k, k)
            nc.vector.memset(all_sums, 0.0).then_inc(cleared, 1)
            dve.wait_ge(cleared, 1)
            dve.sem_inc(added, BANKS)
            with dve.Fori(0, EG // EU) as i:
                for k in range(EU):
                    at = dve.value_load(m.base[0:1, ds(i * EU + k, 1)], min_val=0, max_val=N - 1)
                    dve.wait_ge(multiplied, i * EU + k + 1 + SLOTS)
                    dve.wait_ge(added, i * EU + k + BANKS)
                    view = all_sums[:, :, ds(at, WIN)]
                    nc.vector.tensor_tensor(view, view, m.banks[k % BANKS][:, 0:8 * WIN].rearrange(
                        "p (w n) -> p w n", w=8), ALU.add).then_inc(added, 1)
                    make(k % SLOTS, i * EU + k + SLOTS)


def sage_update(m, w_l, w_r, b, last_layer):
    nc, ins = m.nc, m.ins
    w = m.part(m.REG, 2, KD, D)
    inverse = m.part(m.REG + 1024, NP)
    mean = m.part(m.REG + 1024 + NP, 2, KD * CH)
    sums = m.sums
    with phase(m, "loaded", "dve_step", "averaged", "multiplied", "taken") as \
            (block, loaded, dve_step, averaged, multiplied, taken):

        @block.sync
        def _(sp):
            for j, name in enumerate((w_l, w_r)):
                sp.dma_start(w[:, j, :, :], ins[name].rearrange("(k p) o -> p k o", p=P)).then_inc(loaded, 16)

        @block.tensor
        def _(pe):
            pe.sem_inc(multiplied, 2)
            pe.wait_ge(loaded, 32)
            with pe.Fori(0, NCH // 2) as i:
                for u in range(2):
                    pe.wait_ge(averaged, i * 2 + u + 1 + 2)
                    pe.wait_ge(taken, i * 2 + u + 1)
                    mu = mean[:, u, :].rearrange("p (k n) -> p k n", k=KD)
                    for f in range(KD):
                        cols = slice(f * P, (f + 1) * P)
                        for k in range(KD):
                            nc.tensor.matmul(m.banks[2 * u + f][:, 0:CH], w[:, 1, k, cols],
                                             m.yT[:, k, tile_at(i, u, CH, 2)], start=k == 0, stop=False)
                        for k in range(KD):
                            last = nc.tensor.matmul(m.banks[2 * u + f][:, 0:CH], w[:, 0, k, cols],
                                                    mu[:, k, :], start=False, stop=k == KD - 1)
                    last.then_inc(multiplied, 1)

        @block.vector
        def _(dve):
            step = Steps(dve, dve_step)
            step(nc.vector.tensor_scalar(inverse, m.degree[:, 0:NP], 1.0, None, ALU.max))
            step(nc.vector.reciprocal(inverse, inverse))
            dve.sem_inc(averaged, 2)

            def average(i, u):
                mu = mean[:, u, :].rearrange("p (k n) -> p k n", k=KD)
                cols = tile_at(i, u, CH, 2)
                for k in range(KD):
                    last = nc.vector.tensor_tensor(mu[:, k, :], sums[:, k, cols], inverse[:, cols], ALU.mult)
                last.then_inc(averaged, 1)

            with dve.Fori(0, NCH // 2) as i:
                for u in range(2):
                    dve.wait_ge(multiplied, i * 2 + u + 1)
                    average(i, u)
                if last_layer:
                    for u in range(2):
                        cols = tile_at(i, u, CH, 2)
                        dve.wait_ge(multiplied, i * 2 + u + 1 + 2)
                        for f in range(KD):
                            last = nc.vector.scalar_tensor_tensor(
                                m.xT[:, f, cols], m.banks[2 * u + f][:, 0:CH], m.vec(b, f), m.xT[:, f, cols],
                                ALU.add, ALU.add)
                        last.then_inc(taken, 1)

        @block.scalar
        def _(act):
            act.sem_inc(taken, 2)
            if not last_layer:
                with act.Fori(0, NCH // 2) as i:
                    for u in range(2):
                        act.wait_ge(multiplied, i * 2 + u + 1 + 2)
                        for f in range(KD):
                            last = nc.scalar.activation(m.yT[:, f, tile_at(i, u, CH, 2)],
                                                        m.banks[2 * u + f][:, 0:CH], ACT.Relu, bias=m.vec(b, f))
                        last.then_inc(taken, 1)


def sage(m, w1_l, w1_r, b1, w2_l, w2_r, b2):
    neighbour_sums(m)
    sage_update(m, w1_l, w1_r, b1, False)
    neighbour_sums(m)
    sage_update(m, w2_l, w2_r, b2, True)


def repeat_last(ap, n):
    return ap.unsqueeze(2).broadcast_to([*ap.shape, n])


def repeat_first(ap, n):
    return ap.unsqueeze(1).broadcast_to([ap.shape[0], n, ap.shape[1]])


def slice_attention(m):
    nc, ins = m.nc, m.ins
    at = [m.REG]

    def reg(*shape):
        v = m.part(at[0], *shape)
        at[0] += int(np.prod(shape))
        return v

    HP = HG // P
    wT = m.part(0, HP, NP)
    wx_t = reg(HP, D)
    wfx = reg(KD, HG)
    wo = reg(HP, D)
    pair = reg(4, P)
    wc = reg(KD, HG)
    bc = reg(HG)
    b_fx = reg(HG)
    b_slice = reg(G)
    inv_temp = reg(HEADS)
    mixed = reg(HP, D + 1)
    mixed_t = reg(KD, HG)
    share = reg(HG)
    tok = reg(HG)
    q_t, k_t, v_s = reg(HG), reg(HG), reg(HG)
    score = reg(HP, G)
    attn, attn_t, out_t = reg(HG), reg(HG), reg(HG)
    mo = reg(HP, D)
    probs = reg(TU, HG)
    assert at[0] <= 4 * AW + 16384
    zero = attn
    y_rows = m.gathered
    y_cols = m.onehot[:, 0:TU * KD * TP].rearrange("p (u k n) -> p u k n", u=TU, k=KD)
    top = m.small[:, 0:TU * HEADS].rearrange("p (u h) -> p u h", u=TU)
    tot = m.small[:, 64:64 + TU * HEADS].rearrange("p (u h) -> p u h", u=TU)
    tiny = m.small[:, 128:160]

    def four(ap):
        return ap.rearrange("p (j n) -> p j n", j=HP)

    def diagonal(ap, b):
        return four(ap)[b * G:(b + 1) * G, :, b * G:(b + 1) * G]

    with phase(m, "cleared", "loaded", "multiplied", "dve_step") as (block, cleared, loaded, multiplied, dve_step):

        @block.gpsimd
        def _(pool):
            nc.gpsimd.memset(attn, 0.0)
            nc.gpsimd.memset(tok, 0.0)
            nc.gpsimd.memset(wT[:, :, N:NP], 0.0)
            nc.gpsimd.memset(pair, 0.0).then_inc(cleared, 1)

        @block.sync
        def _(sp):
            def load(to, of):
                sp.dma_start(to, of).then_inc(loaded, 16)

            load(wx_t, ins["L0_ffn_W_x_t"].rearrange("(j p) f -> p j f", p=P))
            load(wfx, ins["L0_ffn_W_fx"].rearrange("(k p) o -> p k o", p=P))
            load(wo, ins["L0_ffn_W_out"].rearrange("(j p) o -> p j o", p=P))
            load(b_fx[0:1, :], ins["L0_ffn_b_fx"])
            load(b_slice[0:1, :], ins["L0_ffn_b_slice"])
            load(inv_temp, ins["L0_ffn_temperature"].partition_broadcast(P))
            sp.wait_ge(cleared, 1)
            for w, name in enumerate(("W_slice", "W_q", "W_k", "W_v")):
                for b in range(2):
                    load(pair[b * G:(b + 1) * G, w, b * G:(b + 1) * G], ins["L0_ffn_" + name])
            sp.wait_ge(loaded, 16 * 14)

        @block.tensor
        def _(pe):
            pe.wait_ge(loaded, 16 * 14)
            for j in range(HP):
                for k in range(KD):
                    nc.tensor.matmul(m.banks[k][:, j * P:(j + 1) * P], wx_t[:, j, k * P:(k + 1) * P], pair[:, 0, :],
                                     start=True, stop=True)
                last = nc.tensor.matmul(m.banks[2][0:1, j * P:(j + 1) * P], m.vec("L0_ffn_b_x", j), pair[:, 0, :],
                                        start=True, stop=True)
            last.then_inc(multiplied, 1)

        @block.vector
        def _(dve):
            step = Steps(dve, dve_step)
            dve.wait_ge(loaded, 16 * 14)
            step(nc.vector.tensor_scalar(inv_temp, inv_temp, 0.1, 5.0, ALU.max, ALU.min))
            step(nc.vector.reciprocal(inv_temp, inv_temp))
            dve.wait_ge(multiplied, 1)
            heads = lambda ap: ap.rearrange("p (h g) -> p h g", h=HEADS)
            for k in range(KD):
                nc.vector.tensor_tensor(heads(wc[:, k, :]), heads(m.banks[k][:, :]), repeat_last(inv_temp, G), ALU.mult)
            step(nc.vector.tensor_tensor(heads(bc[0:1, :]), heads(m.banks[2][0:1, :]),
                                         repeat_first(b_slice[0:1, :], HEADS), ALU.add))
            step(nc.vector.tensor_tensor(heads(bc[0:1, :]), heads(bc[0:1, :]), repeat_last(inv_temp[0:1, :], G),
                                         ALU.mult))

    LOGITS, ROWS, TURNED, NORM, MIXED = (0, 1), 2, (3, 4), 5, (6, 7)
    with phase(m, "staged", "y_turned", "y_taken", "logits_ready", "centred", "exped", "normed", "mixed_in",
               "w_turned", "w_taken", "maxed", "summed", "inverted") as \
            (block, staged, y_turned, y_taken, logits_ready, centred, exped, normed, mixed_in,
             w_turned, w_taken, maxed, summed, inverted):

        @block.scalar
        def _(act):
            act.sem_inc(y_taken, 1)
            act.sem_inc(w_taken, 2)

            def front(i, u):
                act.wait_ge(mixed_in, i * TU + u + 1)
                nc.scalar.copy(y_cols[:, u, :, :], m.yT[:, :, tile_at(i, u, TP, TU)]).then_inc(staged, 1)
                act.wait_ge(y_turned, i * TU + u + 1)
                nc.scalar.copy(y_rows[0:TP, u, :], m.banks[ROWS][0:TP, 0:D]).then_inc(y_taken, 1)

            def back(i, u):
                act.wait_ge(centred, i * TU + u + 1 + 1)
                nc.scalar.activation(probs[0:TP, u, :], probs[0:TP, u, :], ACT.Exp).then_inc(exped, 1)

            def last(i, u):
                act.wait_ge(w_turned, i * TU + u + 1)
                nc.scalar.copy(wT[:, :, tile_at(i, u, TP, TU)],
                               m.banks[TURNED[u % 2]][:, 0:HP * TP].rearrange("p (j n) -> p j n", j=HP))\
                    .then_inc(w_taken, 1)

            with act.Fori(0, NT // TU) as i:
                front(i, 0)
                for u in range(TU):
                    if u + 1 < TU:
                        front(i, u + 1)
                    back(i, u)
                    if u:
                        last(i, u - 1)
                last(i, TU - 1)

        @block.tensor
        def _(pe):
            pe.sem_inc(mixed_in, TU)
            for b in MIXED:
                nc.tensor.matmul(m.banks[b][:, :], zero[:, 0:P], zero, start=True, stop=False)
            nc.tensor.matmul(m.banks[NORM][:, 0:HP], zero[:, 0:P], zero[:, 0:HP], start=True, stop=False)

            def front(i, u):
                pe.wait_ge(staged, i * TU + u + 1)
                pe.wait_ge(y_taken, i * TU + u + 1)
                for k in range(KD):
                    last = nc.tensor.transpose(m.banks[ROWS][0:TP, k * P:(k + 1) * P], y_cols[:, u, k, :], m.ident[:, :])
                last.then_inc(y_turned, 1)
                pe.wait_ge(centred, i * TU + max(u - 1, 0) + 1)
                logits = m.banks[LOGITS[u % 2]][0:TP, :]
                for k in range(KD):
                    nc.tensor.matmul(logits, y_cols[:, u, k, :], wc[:, k, :], start=k == 0, stop=False)
                nc.tensor.matmul(logits, m.ones[0:1, 0:TP], bc[0:1, :], start=False, stop=True)\
                    .then_inc(logits_ready, 1)

            def back(i, u):
                pe.wait_ge(normed, i * TU + u + 1)
                pe.wait_ge(y_taken, i * TU + u + 1 + 1)
                pe.wait_ge(w_taken, i * TU + u + 1 + (u == 0))
                for j in range(HP):
                    w = probs[0:TP, u, j * P:(j + 1) * P]
                    nc.tensor.transpose(m.banks[TURNED[u % 2]][:, j * TP:(j + 1) * TP], w, m.ident[0:TP, 0:TP])\
                        .then_inc(w_turned, 1) if j == HP - 1 else \
                        nc.tensor.transpose(m.banks[TURNED[u % 2]][:, j * TP:(j + 1) * TP], w, m.ident[0:TP, 0:TP])
                for j in range(HP):
                    w = probs[0:TP, u, j * P:(j + 1) * P]
                    nc.tensor.matmul(m.banks[MIXED[j // 2]][:, (j % 2) * D:(j % 2 + 1) * D], w, y_rows[0:TP, u, :],
                                     start=False, stop=False, skip_group_check=True)
                    last = nc.tensor.matmul(m.banks[NORM][:, j:j + 1], w, m.ones[0:TP, 0:1], start=False, stop=False,
                                            skip_group_check=True)
                last.then_inc(mixed_in, 1)

            with pe.Fori(0, NT // TU) as i:
                front(i, 0)
                for u in range(TU):
                    if u + 1 < TU:
                        front(i, u + 1)
                    back(i, u)
            for b in MIXED:
                nc.tensor.matmul(m.banks[b][:, :], zero[:, 0:P], zero, start=False, stop=True)
            nc.tensor.matmul(m.banks[NORM][:, 0:HP], zero[:, 0:P], zero[:, 0:HP], start=False, stop=True)

        @block.vector
        def _(dve):
            heads = lambda ap: ap.rearrange("p (h g) -> p h g", h=HEADS)

            def centre(i, u):
                logits = heads(m.banks[LOGITS[u % 2]][0:TP, :])
                dve.wait_ge(logits_ready, i * TU + u + 1)
                nc.vector.tensor_reduce(top[0:TP, u, :], logits, AX, ALU.max).then_inc(maxed, 1)
                dve.wait_ge(maxed, i * TU + u + 1)
                dve.wait_ge(mixed_in, i * TU + u + 1)
                nc.vector.tensor_tensor(heads(probs[0:TP, u, :]), logits, repeat_last(top[0:TP, u, :], G),
                                        ALU.subtract).then_inc(centred, 1)

            def norm(i, u):
                p = heads(probs[0:TP, u, :])
                dve.wait_ge(exped, i * TU + u + 1)
                nc.vector.tensor_reduce(tot[0:TP, u, :], p, AX, ALU.add).then_inc(summed, 1)
                dve.wait_ge(summed, i * TU + u + 1)
                nc.vector.reciprocal(tot[0:TP, u, :], tot[0:TP, u, :]).then_inc(inverted, 1)
                dve.wait_ge(inverted, i * TU + u + 1)
                nc.vector.tensor_tensor(p, p, repeat_last(tot[0:TP, u, :], G), ALU.mult).then_inc(normed, 1)

            dve.sem_inc(centred, 1)
            with dve.Fori(0, NT // TU) as i:
                centre(i, 0)
                for u in range(TU):
                    if u + 1 < TU:
                        centre(i, u + 1)
                    norm(i, u)

    with phase(m, "multiplied", "taken", "dve_step", "exped") as (block, multiplied, taken, dve_step, exped):

        @block.tensor
        def _(pe):
            pe.wait_ge(taken, 1)
            for j in range(HP):
                for k in range(KD):
                    nc.tensor.transpose(m.banks[k][:, j * P:(j + 1) * P], mixed[:, j, k * P:(k + 1) * P], m.ident[:, :])
                last = nc.tensor.transpose(m.banks[2][0:1, j * P:(j + 1) * P], mixed[:, j, D:D + 1], m.ident[:, :])
            last.then_inc(multiplied, 1)
            pe.wait_ge(taken, 2)
            for j in range(HP):
                cols = slice(j * P, (j + 1) * P)
                for k in range(KD):
                    nc.tensor.matmul(m.banks[3][:, cols], wfx[:, k, cols], mixed_t[:, k, cols], start=k == 0, stop=False)
                last = nc.tensor.matmul(m.banks[3][:, cols], b_fx[0:1, cols], share[0:1, cols], start=False, stop=True)
            last.then_inc(multiplied, 1)
            pe.wait_ge(taken, 3)
            nc.tensor.matmul(m.banks[4][:, :], pair[:, 1, :], tok, start=True, stop=True)
            nc.tensor.matmul(m.banks[5][:, :], pair[:, 2, :], tok, start=True, stop=True)
            for j in range(HP):
                cols = slice(j * P, (j + 1) * P)
                last = nc.tensor.matmul(m.banks[6][:, cols], tok[:, cols], pair[:, 3, :], start=True, stop=True)
            last.then_inc(multiplied, 1)
            pe.wait_ge(taken, 4)
            for j in range(HP):
                cols = slice(j * P, (j + 1) * P)
                last = nc.tensor.matmul(m.banks[7][:, cols], q_t[:, cols], k_t[:, cols], start=True, stop=True)
            last.then_inc(multiplied, 1)
            pe.wait_ge(taken, 5)
            for j in range(HP):
                cols = slice(j * P, (j + 1) * P)
                last = nc.tensor.transpose(m.banks[0][:, cols], attn[:, cols], m.ident[:, :])
            last.then_inc(multiplied, 1)
            pe.wait_ge(taken, 6)
            for j in range(HP):
                cols = slice(j * P, (j + 1) * P)
                last = nc.tensor.matmul(m.banks[1][:, cols], v_s[:, cols], attn_t[:, cols], start=True, stop=True)
            last.then_inc(multiplied, 1)
            pe.wait_ge(taken, 7)
            for j in range(HP):
                last = nc.tensor.matmul(m.banks[2 + j // 2][:, (j % 2) * D:(j % 2 + 1) * D],
                                        out_t[:, j * P:(j + 1) * P], wo[:, j, :], start=True, stop=True)
            last.then_inc(multiplied, 1)

        @block.scalar
        def _(act):
            act.wait_ge(exped, 1)
            nc.scalar.activation(score, score, ACT.Exp).then_inc(exped, 1)

        @block.vector
        def _(dve):
            step = Steps(dve, dve_step)
            norm, inv = tiny[:, 0:HP], tiny[:, HP:2 * HP]
            step(nc.vector.tensor_copy(norm, m.banks[NORM][:, 0:HP]))
            step(nc.vector.tensor_scalar(inv, norm, 1e-5, None, ALU.add))
            step(nc.vector.reciprocal(inv, inv))
            for j in range(HP):
                nc.vector.tensor_tensor(mixed[:, j, D:D + 1], norm[:, j:j + 1], inv[:, j:j + 1], ALU.mult)
                last = nc.vector.tensor_scalar(mixed[:, j, 0:D], m.banks[MIXED[j // 2]][:, (j % 2) * D:(j % 2 + 1) * D],
                                               inv[:, j:j + 1], None, ALU.mult)
            last.then_inc(taken, 1)
            dve.wait_ge(multiplied, 1)
            for k in range(KD):
                nc.vector.tensor_copy(mixed_t[:, k, :], m.banks[k][:, :])
            nc.vector.tensor_copy(share[0:1, :], m.banks[2][0:1, :]).then_inc(taken, 1)
            dve.wait_ge(multiplied, 2)
            nc.vector.tensor_copy(diagonal(tok, 0), diagonal(m.banks[3][:, :], 0))
            nc.vector.tensor_copy(diagonal(tok, 1), diagonal(m.banks[3][:, :], 1)).then_inc(taken, 1)
            dve.wait_ge(multiplied, 3)
            nc.vector.tensor_copy(q_t, m.banks[4][:, :])
            nc.vector.tensor_copy(k_t, m.banks[5][:, :])
            nc.vector.tensor_copy(v_s, m.banks[6][:, :]).then_inc(taken, 1)
            dve.wait_ge(multiplied, 4)
            for b in range(2):
                last = nc.vector.tensor_scalar(score[b * G:(b + 1) * G, :, :], diagonal(m.banks[7][:, :], b),
                                               float(G) ** -0.5, None, ALU.mult)
            step(last)
            step(nc.vector.tensor_reduce(tiny[:, 8:8 + HP], score, AX, ALU.max))
            nc.vector.tensor_tensor(score, score, repeat_last(tiny[:, 8:8 + HP], G), ALU.subtract).then_inc(exped, 1)
            dve.wait_ge(exped, 2)
            step(nc.vector.tensor_reduce(tiny[:, 12:12 + HP], score, AX, ALU.add))
            step(nc.vector.reciprocal(tiny[:, 12:12 + HP], tiny[:, 12:12 + HP]))
            for b in range(2):
                rows = slice(b * G, (b + 1) * G)
                last = nc.vector.tensor_tensor(diagonal(attn, b), score[rows, :, :],
                                               repeat_last(tiny[rows, 12:12 + HP], G), ALU.mult)
            last.then_inc(taken, 1)
            dve.wait_ge(multiplied, 5)
            nc.vector.tensor_copy(attn_t, m.banks[0][:, :]).then_inc(taken, 1)
            dve.wait_ge(multiplied, 6)
            nc.vector.tensor_copy(out_t, m.banks[1][:, :]).then_inc(taken, 1)
            dve.wait_ge(multiplied, 7)
            for b in range(2):
                nc.vector.tensor_copy(mo[:, 2 * b:2 * b + 2, :],
                                      m.banks[2 + b][:, :].rearrange("p (j n) -> p j n", j=2))

    with phase(m, "multiplied", "taken") as (block, multiplied, taken):

        @block.tensor
        def _(pe):
            with pe.Fori(0, NCH // 2) as i:
                for u in range(2):
                    pe.wait_ge(taken, i * 2 + u + 1)
                    for f in range(KD):
                        for j in range(HP):
                            last = nc.tensor.matmul(m.banks[2 * u + f][:, 0:CH], mo[:, j, f * P:(f + 1) * P],
                                                    wT[:, j, tile_at(i, u, CH, 2)], start=j == 0, stop=j == HP - 1)
                    last.then_inc(multiplied, 1)

        @block.vector
        def _(dve):
            dve.sem_inc(taken, 2)
            with dve.Fori(0, NCH // 2) as i:
                for u in range(2):
                    cols = tile_at(i, u, CH, 2)
                    dve.wait_ge(multiplied, i * 2 + u + 1)
                    for f in range(KD):
                        last = nc.vector.scalar_tensor_tensor(m.xT[:, f, cols], m.banks[2 * u + f][:, 0:CH],
                                                              m.vec("L0_ffn_b_out", f), m.xT[:, f, cols],
                                                              ALU.add, ALU.add)
                    last.then_inc(taken, 1)


def gcn(m):
    nc, ins = m.nc, m.ins
    w = m.part(m.REG, KD, D)
    inv_root = m.part(2 * AW, NP)
    scaled = m.part(m.REG + 512, 2, KD, CH)
    with phase(m, "loops_added", "rooted", "scaled_ready") as (block, loops_added, rooted, scaled_ready):

        @block.vector
        def _(dve):
            nc.vector.tensor_scalar(inv_root, m.degree[:, 0:NP], 1.0, None, ALU.add).then_inc(loops_added, 1)
            dve.wait_ge(rooted, 1)
            nc.vector.reciprocal(inv_root, inv_root).then_inc(scaled_ready, 1)
            dve.wait_ge(scaled_ready, 1)
            for k in range(KD):
                nc.vector.tensor_tensor(m.yT[:, k, :], m.yT[:, k, :], inv_root, ALU.mult)

        @block.scalar
        def _(act):
            act.wait_ge(loops_added, 1)
            nc.scalar.activation(inv_root, inv_root, ACT.Sqrt).then_inc(rooted, 1)

    for layer in (1, 2, 3):
        neighbour_sums(m, with_self=True)
        b = f"L1_gnn_b{layer}"
        with phase(m, "loaded", "multiplied", "taken", "scaled_back", "gelu_done") as \
                (block, loaded, multiplied, taken, scaled_back, gelu_done):

            @block.sync
            def _(sp):
                sp.dma_start(w, ins[f"L1_gnn_W{layer}"].rearrange("(k p) o -> p k o", p=P)).then_inc(loaded, 16)

            @block.tensor
            def _(pe):
                pe.wait_ge(loaded, 16)
                with pe.Fori(0, NCH // 2) as i:
                    for u in range(2):
                        pe.wait_ge(taken, i * 2 + u + 1)
                        for f in range(KD):
                            for k in range(KD):
                                last = nc.tensor.matmul(m.banks[2 * u + f][:, 0:CH], w[:, k, f * P:(f + 1) * P],
                                                        m.sums[:, k, tile_at(i, u, CH, 2)], start=k == 0,
                                                        stop=k == KD - 1)
                        last.then_inc(multiplied, 1)

            @block.vector
            def _(dve):
                dve.sem_inc(taken, 2)
                with dve.Fori(0, NCH // 2) as i:
                    for u in range(2):
                        cols = tile_at(i, u, CH, 2)
                        dve.wait_ge(multiplied, i * 2 + u + 1)
                        if layer < 3:
                            dve.wait_ge(gelu_done, i * 2 + u + 1)
                        for f in range(KD):
                            last = nc.vector.tensor_tensor(scaled[:, u, f, :], m.banks[2 * u + f][:, 0:CH],
                                                           inv_root[:, cols], ALU.mult)
                        last.then_inc(taken, 1)
                        if layer == 3:
                            dve.wait_ge(taken, i * 2 + u + 1 + 2)
                            for f in range(KD):
                                nc.vector.scalar_tensor_tensor(m.xT[:, f, cols], scaled[:, u, f, :], m.vec(b, f),
                                                               m.xT[:, f, cols], ALU.add, ALU.add)
                    if layer < 3:
                        for u in range(2):
                            cols = tile_at(i, u, CH, 2)
                            dve.wait_ge(gelu_done, i * 2 + u + 1 + 2)
                            for f in range(KD):
                                nc.vector.tensor_tensor(m.yT[:, f, cols], m.yT[:, f, cols], inv_root[:, cols], ALU.mult)

            @block.scalar
            def _(act):
                if layer < 3:
                    act.sem_inc(gelu_done, 2)
                    with act.Fori(0, NCH // 2) as i:
                        for u in range(2):
                            act.wait_ge(taken, i * 2 + u + 1 + 2)
                            for f in range(KD):
                                last = nc.scalar.activation(m.yT[:, f, tile_at(i, u, CH, 2)], scaled[:, u, f, :],
                                                            ACT.Gelu_apprx_tanh, bias=m.vec(b, f))
                            last.then_inc(gelu_done, 1)


def gates(m, w_r, b_r, top_two):
    nc, ins = m.nc, m.ins
    gate = m.part(0, NP)[0:NE, :]
    logit = m.part(NP, NP)[0:NE, :]
    stage = m.part(2 * NP, TU, TP)
    at = [2 * NP + TU * TP]

    def rows(*shape):
        v = m.part(at[0], *shape)[0:TP]
        at[0] += int(np.prod(shape))
        return v

    L, W, S1, S2, T, O = (rows(NT, NE) for _ in range(6))
    a, b, c = rows(NT), rows(NT), rows(NT)
    order = rows(NE)
    wr = m.small[:, 0:KD * NE].rearrange("p (k e) -> p k e", k=KD)
    br = m.small[0:NE, KD * NE:KD * NE + 1]
    with phase(m, "loaded", "ordered", "multiplied", "logits_taken") as (block, loaded, ordered, multiplied, logits_taken):

        @block.sync
        def _(sp):
            sp.dma_start(wr, ins[w_r].rearrange("(k p) e -> p k e", p=P)).then_inc(loaded, 16)
            sp.dma_start(br, ins[b_r]).then_inc(loaded, 16)

        @block.gpsimd
        def _(pool):
            order_i = rows(NE).bitcast(I32)
            nc.gpsimd.memset(gate[:, N:NP], 0.0)
            nc.gpsimd.iota(order_i, [[-1, NE]], base=NE, channel_multiplier=0).then_inc(ordered, 1)
            pool.wait_ge(ordered, 1)
            nc.gpsimd.tensor_copy(order, order_i)

        @block.tensor
        def _(pe):
            pe.wait_ge(loaded, 32)
            with pe.Fori(0, NCH // 2) as i:
                for u in range(2):
                    pe.wait_ge(logits_taken, i * 2 + u + 1)
                    for k in range(KD):
                        last = nc.tensor.matmul(m.banks[u][0:NE, 0:CH], wr[:, k, :], m.yT[:, k, tile_at(i, u, CH, 2)],
                                                start=k == 0, stop=k == KD - 1)
                    last.then_inc(multiplied, 1)

        @block.vector
        def _(dve):
            dve.wait_ge(loaded, 32)
            dve.sem_inc(logits_taken, 2)
            with dve.Fori(0, NCH // 2) as i:
                for u in range(2):
                    dve.wait_ge(multiplied, i * 2 + u + 1)
                    nc.vector.tensor_scalar(logit[:, tile_at(i, u, CH, 2)], m.banks[u][0:NE, 0:CH], br, None,
                                            ALU.add).then_inc(logits_taken, 1)

    def turn(of, to, back):
        with phase(m, "staged", "transposed", "taken", "bank_claimed") as (block, staged, transposed, taken, bank_claimed):

            @block.scalar
            def _(act):
                with act.Fori(0, NT // TU) as i:
                    for u in range(TU):
                        act.wait_ge(transposed, i * TU + u + 1)
                        if back:
                            nc.scalar.copy(stage[0:TP, u, 0:NE], of[:, ds(i * TU + u, 1), :]
                                           .rearrange("p a e -> p (a e)")).then_inc(staged, 1)
                        else:
                            nc.scalar.copy(stage[0:NE, u, :], of[:, tile_at(i, u, TP, TU)]).then_inc(staged, 1)

            @block.tensor
            def _(pe):
                pe.sem_inc(transposed, TU)
                with pe.Fori(0, NT // TU) as i:
                    for u in range(TU):
                        pe.wait_ge(staged, i * TU + u + 1)
                        pe.wait_ge(taken, i * TU + u + 1)
                        pe.sem_inc(bank_claimed, 1)
                        if back:
                            last = nc.tensor.transpose(m.banks[u][0:NE, 0:TP], stage[0:TP, u, 0:NE], m.ident[0:TP, 0:TP])
                        else:
                            last = nc.tensor.transpose(m.banks[u][0:TP, 0:NE], stage[0:NE, u, :], m.ident[0:NE, 0:NE])
                        last.then_inc(transposed, 1)

            @block.vector
            def _(dve):
                dve.sem_inc(taken, TU)
                with dve.Fori(0, NT // TU) as i:
                    for u in range(TU):
                        dve.wait_ge(transposed, i * TU + u + 1 + TU)
                        if back:
                            nc.vector.tensor_copy(to[:, tile_at(i, u, TP, TU)], m.banks[u][0:NE, 0:TP]).then_inc(taken, 1)
                        else:
                            nc.vector.tensor_copy(to[:, ds(i * TU + u, 1), :].rearrange("p a e -> p (a e)"),
                                                  m.banks[u][0:TP, 0:NE]).then_inc(taken, 1)

    turn(logit, L, False)

    with phase(m, "dve_step", "centred", "exped") as (block, dve_step, centred, exped):

        @block.scalar
        def _(act):
            act.wait_ge(centred, 1)
            v = b if top_two else W
            nc.scalar.activation(v, v, ACT.Exp).then_inc(exped, 1)

        @block.vector
        def _(dve):
            step = Steps(dve, dve_step)
            tt, wide = nc.vector.tensor_tensor, lambda v: repeat_last(v, NE)

            def first_largest(of, largest, mask):
                step(nc.vector.tensor_reduce(largest, of, AX, ALU.max))
                step(tt(T, of, wide(largest), ALU.is_equal))
                step(tt(T, T, repeat_first(order, NT), ALU.mult))
                step(nc.vector.tensor_reduce(c, T, AX, ALU.max))
                step(tt(mask, T, wide(c), ALU.is_equal))

            if top_two:
                first_largest(L, a, S1)
                step(nc.vector.scalar_tensor_tensor(O, S1, -1e30, L, ALU.mult, ALU.add))
                first_largest(O, b, S2)
                nc.vector.tensor_tensor(b, b, a, ALU.subtract).then_inc(centred, 1)
                dve.wait_ge(exped, 1)
                step(nc.vector.tensor_scalar(a, b, 1.0, None, ALU.add))
                step(nc.vector.reciprocal(a, a))
                step(tt(b, a, b, ALU.mult))
                step(tt(W, S1, wide(a), ALU.mult))
                step(tt(O, S2, wide(b), ALU.mult))
                step(tt(W, W, O, ALU.add))
            else:
                step(nc.vector.tensor_reduce(a, L, AX, ALU.max))
                tt(W, L, wide(a), ALU.subtract).then_inc(centred, 1)
                dve.wait_ge(exped, 1)
                step(nc.vector.tensor_reduce(b, W, AX, ALU.add))
                step(nc.vector.reciprocal(b, b))
                step(tt(W, W, wide(b), ALU.mult))

    turn(W, gate, True)
    return gate


def experts_top_two(m, gate):
    nc, ins = m.nc, m.ins
    HT = H1 // P
    w1 = m.part(m.REG, NE, KD * H1).rearrange("p e (k h) -> p e k h", k=KD)
    w2 = m.part(m.REG + NE * KD * H1, NE, HT * D).rearrange("p e (h o) -> p e h o", h=HT)
    b2 = m.gathered[0:NE, 0, :]
    hidden = m.part(NP, 2, HT, CH)
    OUT, GATE = (4, 5), (6, 7)
    with phase(m, "loaded", "hidden_ready", "gelu_done", "gate_spread", "gated", "consumed", "out_ready", "added",
               "bank_claimed") as \
            (block, loaded, hidden_ready, gelu_done, gate_spread, gated, consumed, out_ready, added, bank_claimed):

        @block.sync
        def _(sp):
            for e in range(NE):
                sp.dma_start(w1[:, e, :, :], ins["L1_ffn_W1"][e].rearrange("(k p) h -> p k h", p=P)).then_inc(loaded, 16)
                sp.dma_start(w2[:, e, :, :], ins["L1_ffn_W2"][e].rearrange("(h p) o -> p h o", p=P)).then_inc(loaded, 16)
            sp.dma_start(b2, ins["L1_ffn_b2"]).then_inc(loaded, 16)

        @block.tensor
        def _(pe):
            pe.wait_ge(loaded, 16 * (2 * NE + 1))
            with pe.Fori(0, NCH) as c:
                cols = ds(c * CH, CH)

                def up(e):
                    for h in range(HT):
                        pe.wait_ge(gelu_done, (c * NE + e) * HT + h + 1)
                        for k in range(KD):
                            last = nc.tensor.matmul(m.banks[h][:, 0:CH], w1[:, e, k, h * P:(h + 1) * P],
                                                    m.yT[:, k, cols], start=k == 0, stop=k == KD - 1)
                        last.then_inc(hidden_ready, 1)
                    pe.wait_ge(gated, (c * NE + e) * HT + HT)
                    pe.sem_inc(bank_claimed, 1)
                    nc.tensor.matmul(m.banks[GATE[e % 2]][:, 0:CH], m.pick[:, e, :], gate[:, cols], start=True,
                                     stop=True).then_inc(gate_spread, 1)

                def down(e):
                    for h in range(HT):
                        pe.wait_ge(gated, (c * NE + e) * HT + h + 1 + 2 * HT)
                        for f in range(KD):
                            last = nc.tensor.matmul(m.banks[OUT[f]][:, 0:CH], w2[:, e, h, f * P:(f + 1) * P],
                                                    hidden[:, e % 2, h, :], start=e == 0 and h == 0, stop=False,
                                                    skip_group_check=True)
                        last.then_inc(consumed, 1)

                up(0)
                pe.wait_ge(added, c + 1)
                for e in range(NE):
                    if e + 1 < NE:
                        up(e + 1)
                    down(e)
                for f in range(KD):
                    last = nc.tensor.matmul(m.banks[OUT[f]][:, 0:CH], b2[:, f * P:(f + 1) * P], gate[:, cols],
                                            start=False, stop=True, skip_group_check=True)
                last.then_inc(out_ready, 1)

        @block.scalar
        def _(act):
            act.sem_inc(gelu_done, HT)
            with act.Fori(0, NCH) as c:
                for e in range(NE):
                    for h in range(HT):
                        act.wait_ge(hidden_ready, (c * NE + e) * HT + h + 1)
                        act.wait_ge(consumed, (c * NE + e) * HT + h + 1)
                        nc.scalar.activation(hidden[:, e % 2, h, :], m.banks[h][:, 0:CH], ACT.Gelu,
                                             bias=m.vec("L1_ffn_b1", e * HT + h)).then_inc(gelu_done, 1)

        @block.vector
        def _(dve):
            dve.sem_inc(gated, 2 * HT)
            dve.sem_inc(consumed, 2 * HT)
            dve.sem_inc(added, 1)
            with dve.Fori(0, NCH) as c:
                for e in range(NE):
                    dve.wait_ge(gate_spread, c * NE + e + 1)
                    for h in range(HT):
                        dve.wait_ge(gelu_done, (c * NE + e) * HT + h + 1 + HT)
                        nc.vector.tensor_tensor(hidden[:, e % 2, h, :], hidden[:, e % 2, h, :],
                                                m.banks[GATE[e % 2]][:, 0:CH], ALU.mult).then_inc(gated, 1)
                dve.wait_ge(out_ready, c + 1)
                cols = ds(c * CH, CH)
                for f in range(KD):
                    last = nc.vector.tensor_tensor(m.xT[:, f, cols], m.xT[:, f, cols], m.banks[OUT[f]][:, 0:CH], ALU.add)
                last.then_inc(added, 1)


def directional(m):
    nc, ins = m.nc, m.ins
    store_rows(m, m.yT, m.table)
    with if_general(m):
        general_sums(m, weighted=True)
    with branch(m, nc.Else()):
        weighted_sums(m)
    sums = m.sums
    wsum = m.part(6 * AW, 2, AW)
    w1 = m.part(8 * AW, 2 * KD, D)
    w2 = m.part(8 * AW + 2 * KD * D, 4 * KD, D)
    own = m.gathered[:, 0:4, :].rearrange("p a b -> p (a b)")[:, 0:KD * CH].rearrange("p (f n) -> p f n", f=KD)
    snorm = m.gathered[:, 4:8, :].rearrange("p a b -> p (a b)")[:, 0:2 * CH].rearrange("p (u n) -> p u n", u=2)
    inv = m.onehot[:, 0:3 * CH].rearrange("p (w n) -> p w n", w=3)
    OWN = (6, 7)
    with phase(m, "loaded", "snorm_loaded0", "snorm_loaded1", "edge_products", "own_taken", "joined", "absolute", "multiplied", "out_taken",
               "dve_step") as \
            (block, loaded, snorm_loaded0, snorm_loaded1, edge_products, own_taken, joined, absolute, multiplied, out_taken,
             dve_step):

        @block.sync
        def _(sp):
            sp.dma_start(w1, ins["L2_gnn_W1"].rearrange("(k p) o -> p k o", p=P)).then_inc(loaded, 16)
            sp.dma_start(w2, ins["L2_gnn_W2"].rearrange("(k p) o -> p k o", p=P)).then_inc(loaded, 16)
            with sp.Fori(0, NCH // 2) as i:
                for u in range(2):
                    sp.wait_ge(out_taken, i * 2 + u + 1)
                    sp.dma_start(snorm[:, u, :], ins["snorm"][ds(i * 2 * CH + u * CH, CH)].partition_broadcast(P))\
                        .then_inc((snorm_loaded0, snorm_loaded1)[u], 16)

        @block.tensor
        def _(pe):
            pe.wait_ge(loaded, 32)
            with pe.Fori(0, NCH) as c:
                cols = ds(c * CH, CH)
                pe.wait_ge(out_taken, c + 2)
                for f in range(KD):
                    for k in range(KD):
                        nc.tensor.matmul(m.banks[OWN[f]][:, 0:CH], w1[:, KD + k, f * P:(f + 1) * P], m.yT[:, k, cols],
                                         start=k == 0, stop=k == KD - 1)
                for w in range(3):
                    for f in range(KD):
                        for k in range(KD):
                            last = nc.tensor.matmul(m.banks[2 * w + f][:, 0:CH], w1[:, k, f * P:(f + 1) * P],
                                                    sums[:, 2 * w + k, cols], start=k == 0, stop=k == KD - 1)
                last.then_inc(edge_products, 1)
                pe.wait_ge(own_taken, c + 1)
                pe.wait_ge(absolute, c + 1)
                for f in range(KD):
                    for k in range(4 * KD):
                        rhs = m.yT[:, k, cols] if k < KD else sums[:, k - KD, cols]
                        last = nc.tensor.matmul(m.banks[OWN[f]][:, 0:CH], w2[:, k, f * P:(f + 1) * P], rhs,
                                                start=k == 0, stop=k == 4 * KD - 1)
                last.then_inc(multiplied, 1)

        @block.scalar
        def _(act):
            with act.Fori(0, NCH) as c:
                cols = ds(c * CH, CH)
                act.wait_ge(edge_products, c + 1)
                act.wait_ge(joined, c + 1)
                for f in range(KD):
                    last = nc.scalar.activation(own[:, f, :], m.banks[OWN[f]][:, 0:CH], ACT.Identity,
                                                bias=m.vec("L2_gnn_b1", f))
                last.then_inc(own_taken, 1)
                act.wait_ge(joined, c + 2)
                for f in range(KD):
                    v = sums[:, 4 + f, cols]
                    last = nc.scalar.activation(v, v, ACT.Abs)
                last.then_inc(absolute, 1)

        @block.vector
        def _(dve):
            PER = 6
            dve.sem_inc(out_taken, 2)
            dve.sem_inc(joined, 1)
            with dve.Fori(0, NCH // 2) as i:
                for u in range(2):
                    c = i * 2 + u
                    cols = ds(i * 2 * CH + u * CH, CH)
                    n = [0]

                    def step(ins_):
                        ins_.then_inc(dve_step, 1)
                        n[0] += 1
                        dve.wait_ge(dve_step, c * PER + n[0])

                    totals = (m.degree[:, cols], wsum[:, 0, cols], wsum[:, 1, cols])
                    nc.vector.tensor_scalar(inv[:, 0, :], totals[0], 1.0, None, ALU.max)
                    step(nc.vector.tensor_scalar(inv[:, 1, :], totals[1], 1e-8, None, ALU.add))
                    step(nc.vector.reciprocal(inv[:, 0:2, :], inv[:, 0:2, :]))
                    dve.wait_ge(own_taken, c + 1)
                    for f in range(KD):
                        for w in range(3):
                            v = sums[:, 2 * w + f, cols]
                            last = nc.vector.tensor_tensor(v, own[:, f, :], totals[w], ALU.mult)
                    step(last)
                    for f in range(KD):
                        for w in range(3):
                            v = sums[:, 2 * w + f, cols]
                            last = nc.vector.tensor_tensor(v, v, m.banks[2 * w + f][:, 0:CH], ALU.add)
                    step(last)
                    for f in range(KD):
                        for w in range(3):
                            v = sums[:, 2 * w + f, cols]
                            last = nc.vector.tensor_tensor(v, v, inv[:, min(w, 1), :], ALU.mult)
                    step(last)
                    for f in range(KD):
                        v = sums[:, 4 + f, cols]
                        last = nc.vector.tensor_tensor(v, v, m.yT[:, f, cols], ALU.subtract)
                    last.then_inc(joined, 1)
                    dve.wait_ge(multiplied, c + 1)
                    for f in range(KD):
                        last = nc.vector.tensor_scalar(sums[:, f, cols], m.banks[OWN[f]][:, 0:CH], m.vec("L2_gnn_b2", f),
                                                       None, ALU.add)
                    step(last)
                    dve.wait_ge((snorm_loaded0, snorm_loaded1)[u], i * 16 + 16)
                    for f in range(KD):
                        last = nc.vector.tensor_tensor(sums[:, f, cols], sums[:, f, cols], snorm[:, u, :], ALU.mult)
                    last.then_inc(out_taken, 1)
                    assert n[0] == PER

    stat = m.small
    sq = m.part(2 * AW, KD, NP)
    with phase(m, "centred", "squared", "rooted", "scaled_ready", "relu_done", "dve_step") as \
            (block, centred, squared, rooted, scaled_ready, relu_done, dve_step):

        @block.scalar
        def _(act):
            act.wait_ge(centred, 1)
            for f in range(KD):
                last = nc.scalar.activation(sq[:, f, 0:N], sums[:, f, 0:N], ACT.Square, accum_out=stat[:, 4 + f:5 + f])
            last.then_inc(squared, 1)
            act.wait_ge(scaled_ready, 1)
            nc.scalar.activation(stat[:, 4:6], stat[:, 4:6], ACT.Sqrt, bias=m.eps[:, 0:1]).then_inc(rooted, 1)
            act.wait_ge(scaled_ready, 2)
            for f in range(KD):
                nc.scalar.activation(sums[:, f, 0:NP], sums[:, f, 0:NP], ACT.Relu, bias=m.vec("L2_gnn_beta", f),
                                     scale=stat[:, 6 + f:7 + f]).then_inc(relu_done, 1)

        @block.vector
        def _(dve):
            step = Steps(dve, dve_step)
            for f in range(KD):
                last = nc.vector.tensor_reduce(stat[:, f:f + 1], sums[:, f, 0:N], AX, ALU.add)
            step(last)
            step(nc.vector.tensor_scalar(stat[:, 0:2], stat[:, 0:2], 1.0 / N, None, ALU.mult))
            for f in range(KD):
                last = nc.vector.tensor_scalar(sums[:, f, 0:NP], sums[:, f, 0:NP], stat[:, f:f + 1], None, ALU.subtract)
            last.then_inc(centred, 1)
            dve.wait_ge(squared, 1)
            nc.vector.tensor_scalar(stat[:, 4:6], stat[:, 4:6], 1.0 / N, None, ALU.mult).then_inc(scaled_ready, 1)
            dve.wait_ge(rooted, 1)
            step(nc.vector.reciprocal(stat[:, 4:6], stat[:, 4:6]))
            nc.vector.tensor_tensor(stat[:, 6:8], stat[:, 4:6], m.vec("L2_gnn_gamma"), ALU.mult).then_inc(scaled_ready, 1)
            for f in range(KD):
                step(nc.vector.tensor_tensor(m.xT[:, f, :], m.xT[:, f, :], m.yT[:, f, :], ALU.add))
                dve.wait_ge(relu_done, f + 1)
                nc.vector.tensor_tensor(m.xT[:, f, 0:N], m.xT[:, f, 0:N], sums[:, f, 0:N], ALU.add)


def experts_for_all(m):
    nc, ins = m.nc, m.ins
    HT = H1 // P
    CAP = float(ceil(N * 1.25 / NE))
    w1 = m.part(m.REG, 2, KD * H1).rearrange("p e (k h) -> p e k h", k=KD)
    w2 = m.part(m.REG + 2048, 2, HT * D).rearrange("p e (h o) -> p e h o", h=HT)
    wr = m.part(m.REG + 4096, KD, NE)
    b1 = m.part(m.REG + 4112, 2, HT)
    b2 = m.part(m.REG + 4120, 2, KD)
    bias = m.part(m.REG + 4124, KD)
    hidden = m.part(m.REG + 4200, 2, HT, CH)
    mean = m.small[:, 0:KD]
    row = lambda j: m.small[0:1, 16 + NE * j:16 + NE * (j + 1)]
    br, logit, weight, scale, picked, masked, order, t8 = (row(j) for j in range(8))
    one = lambda j: m.small[0:1, 100 + j:101 + j]
    chosen = m.small[0:1, 120:122].bitcast(I32)
    order_i = m.small[0:1, 130:138].bitcast(I32)
    both = m.small[:, 140:142]
    with phase(m, "loaded", "ordered", "averaged", "multiplied", "centred", "exped", "dve_step", "chosen_ready",
               "w_loaded", "gates_ready", "gates_spread") as \
            (block, loaded, ordered, averaged, multiplied, centred, exped, dve_step, chosen_ready,
             w_loaded, gates_ready, gates_spread):

        @block.sync
        def _(sp):
            sp.dma_start(wr, ins["L2_ffn_Wr"].rearrange("(k p) e -> p k e", p=P)).then_inc(loaded, 16)
            sp.dma_start(br, ins["L2_ffn_br"]).then_inc(loaded, 16)
            for j in range(2):
                sp.wait_ge(chosen_ready, j + 1)
                e = sp.value_load(chosen[0:1, j:j + 1], min_val=0, max_val=NE - 1)
                one_of = lambda name: ins[name][ds(e, 1)]
                sp.dma_start(w1[:, j, :, :], one_of("L2_ffn_W1").rearrange("e (k p) h -> p (e k) h", p=P)).then_inc(w_loaded, 16)
                sp.dma_start(w2[:, j, :, :], one_of("L2_ffn_W2").rearrange("e (h p) o -> p (e h) o", p=P)).then_inc(w_loaded, 16)
                sp.dma_start(b1[:, j, :], one_of("L2_ffn_b1").rearrange("e p h -> p (e h)")).then_inc(w_loaded, 16)
                sp.dma_start(b2[:, j, :], one_of("L2_ffn_b2").rearrange("e p f -> p (e f)")).then_inc(w_loaded, 16)
            sp.wait_ge(w_loaded, 16 * 8)

        @block.gpsimd
        def _(pool):
            nc.gpsimd.iota(order_i, [[-1, NE]], base=NE, channel_multiplier=0).then_inc(ordered, 1)
            pool.wait_ge(ordered, 1)
            nc.gpsimd.tensor_copy(order, order_i).then_inc(ordered, 1)

        @block.tensor
        def _(pe):
            pe.wait_ge(loaded, 32)
            pe.wait_ge(averaged, 1)
            for k in range(KD):
                last = nc.tensor.matmul(m.banks[0][0:1, 0:NE], mean[:, k:k + 1], wr[:, k, :], start=k == 0,
                                        stop=k == KD - 1)
            last.then_inc(multiplied, 1)
            pe.wait_ge(gates_ready, 1)
            nc.tensor.matmul(m.banks[1][:, 0:2], m.ones[0:1, :], m.small[0:1, 108:110], start=True, stop=True)\
                .then_inc(gates_spread, 1)

        @block.scalar
        def _(act):
            for n, v in enumerate((weight, weight, one(3))):
                act.wait_ge(centred, n + 1)
                nc.scalar.activation(v, v, ACT.Exp).then_inc(exped, 1)

        @block.vector
        def _(dve):
            step = Steps(dve, dve_step)
            for k in range(KD):
                last = nc.vector.tensor_reduce(mean[:, k:k + 1], m.yT[:, k, 0:N], AX, ALU.add)
            step(last)
            nc.vector.tensor_scalar(mean, mean, 1.0 / N, None, ALU.mult).then_inc(averaged, 1)
            dve.wait_ge(multiplied, 1)
            step(nc.vector.tensor_tensor(logit, m.banks[0][0:1, 0:NE], br, ALU.add))

            def softmax(of, n):
                step(nc.vector.tensor_reduce(one(0), of, AX, ALU.max))
                nc.vector.tensor_scalar(weight, of, one(0), None, ALU.subtract).then_inc(centred, 1)
                dve.wait_ge(exped, n)
                step(nc.vector.tensor_reduce(one(1), weight, AX, ALU.add))
                step(nc.vector.reciprocal(one(1), one(1)))
                step(nc.vector.tensor_scalar(weight, weight, one(1), None, ALU.mult))

            softmax(logit, 1)
            step(nc.vector.tensor_scalar(scale, weight, float(N), 1e-30, ALU.mult, ALU.max))
            step(nc.vector.reciprocal(scale, scale))
            step(nc.vector.tensor_scalar(scale, scale, CAP, 1.0, ALU.mult, ALU.min))
            step(nc.vector.tensor_tensor(scale, scale, weight, ALU.mult))
            softmax(scale, 2)
            dve.wait_ge(ordered, 2)
            for j, of in enumerate((weight, masked)):
                step(nc.vector.tensor_reduce(one(4 + j), of, AX, ALU.max))
                step(nc.vector.tensor_scalar(t8, of, one(4 + j), None, ALU.is_equal))
                step(nc.vector.tensor_tensor(t8, t8, order, ALU.mult))
                step(nc.vector.tensor_reduce(one(6), t8, AX, ALU.max))
                step(nc.vector.tensor_scalar(picked, t8, one(6), None, ALU.is_equal))
                step(nc.vector.tensor_scalar(one(6), one(6), -1.0, float(NE), ALU.mult, ALU.add))
                nc.vector.tensor_copy(chosen[0:1, j:j + 1], one(6)).then_inc(chosen_ready, 1)
                if j == 0:
                    step(nc.vector.scalar_tensor_tensor(masked, picked, -1e30, weight, ALU.mult, ALU.add))
            nc.vector.tensor_tensor(one(3), one(5), one(4), ALU.subtract).then_inc(centred, 1)
            dve.wait_ge(exped, 3)
            step(nc.vector.tensor_scalar(one(2), one(3), 1.0, None, ALU.add))
            step(nc.vector.reciprocal(one(8), one(2)))
            nc.vector.tensor_tensor(one(9), one(8), one(3), ALU.mult).then_inc(gates_ready, 1)
            dve.wait_ge(gates_spread, 1)
            step(nc.vector.tensor_copy(both, m.banks[1][:, 0:2]))
            dve.wait_ge(w_loaded, 16 * 8)
            for j in range(2):
                g = both[:, j:j + 1]
                nc.vector.tensor_scalar(w2[:, j, :, :], w2[:, j, :, :], g, None, ALU.mult)
                last = nc.vector.tensor_scalar(b2[:, j, :], b2[:, j, :], g, None, ALU.mult)
            step(last)
            nc.vector.tensor_tensor(bias, b2[:, 0, :], b2[:, 1, :], ALU.add)

    OUT = (4, 5)
    with phase(m, "hidden_ready", "gelu_done", "consumed", "added") as \
            (block, hidden_ready, gelu_done, consumed, added):

        @block.tensor
        def _(pe):
            with pe.Fori(0, NCH) as c:
                cols = ds(c * CH, CH)

                def up(e):
                    for h in range(HT):
                        pe.wait_ge(gelu_done, (c * 2 + e) * HT + h + 1)
                        for k in range(KD):
                            last = nc.tensor.matmul(m.banks[h][:, 0:CH], w1[:, e, k, h * P:(h + 1) * P],
                                                    m.yT[:, k, cols], start=k == 0, stop=k == KD - 1)
                        last.then_inc(hidden_ready, 1)

                def down(e):
                    for h in range(HT):
                        pe.wait_ge(gelu_done, (c * 2 + e) * HT + h + 1 + HT)
                        for f in range(KD):
                            last = nc.tensor.matmul(m.banks[OUT[f]][:, 0:CH], w2[:, e, h, f * P:(f + 1) * P],
                                                    hidden[:, e, h, :], start=e == 0 and h == 0,
                                                    stop=e == 1 and h == HT - 1, skip_group_check=True)
                        last.then_inc(consumed, 1)
                    return last

                up(0)
                up(1)
                pe.wait_ge(added, c + 1)
                down(0)
                down(1)

        @block.scalar
        def _(act):
            act.sem_inc(gelu_done, HT)
            with act.Fori(0, NCH) as c:
                for e in range(2):
                    for h in range(HT):
                        act.wait_ge(hidden_ready, (c * 2 + e) * HT + h + 1)
                        act.wait_ge(consumed, (c * 2 + e) * HT + h + 1)
                        nc.scalar.activation(hidden[:, e, h, :], m.banks[h][:, 0:CH], ACT.Gelu,
                                             bias=b1[:, e, h:h + 1]).then_inc(gelu_done, 1)

        @block.vector
        def _(dve):
            dve.sem_inc(consumed, 2 * HT)
            dve.sem_inc(added, 1)
            with dve.Fori(0, NCH) as c:
                cols = ds(c * CH, CH)
                dve.wait_ge(consumed, (c * 2 + 2) * HT + 2 * HT)
                for f in range(KD):
                    last = nc.vector.scalar_tensor_tensor(m.yT[:, f, cols], m.banks[OUT[f]][:, 0:CH], bias[:, f:f + 1],
                                                          m.yT[:, f, cols], ALU.add, ALU.add)
                last.then_inc(added, 1)

    layer_norm(m, m.yT, m.yT, "L2_ffn_gamma", "L2_ffn_beta", add_to=m.xT)


def experts_deep(m, gate):
    nc, ins = m.nc, m.ins
    w = [m.part(m.REG + l * NE * KD * D, NE, KD * D).rearrange("p e (k h) -> p e k h", k=KD) for l in range(3)]
    scale = m.small[:, 32:64].rearrange("p (l n) -> p l n", l=2)
    bias = m.small[:, 64:96].rearrange("p (l n) -> p l n", l=2)
    bo = m.gathered[0:NE, 0, :]
    hid = m.part(NP, 3, KD, CH)
    act2 = m.part(NP + 3 * KD * CH, 2, KD, CH)
    A, B, OUT, GATE = (0, 1), (2, 3), (4, 5), (6, 7)
    with phase(m, "loaded", "rooted", "dve_step", "folded", "first_ready", "first_done", "second_ready", "second_done",
               "gate_spread", "gated", "consumed", "out_ready", "added", "bank_claimed") as \
            (block, loaded, rooted, dve_step, folded, first_ready, first_done, second_ready, second_done,
             gate_spread, gated, consumed, out_ready, added, bank_claimed):

        @block.sync
        def _(sp):
            for l, name in enumerate(("L3_ffn_W1", "L3_ffn_W2", "L3_ffn_Wo")):
                for e in range(NE):
                    sp.dma_start(w[l][:, e, :, :], ins[name][e].rearrange("(k p) h -> p k h", p=P)).then_inc(loaded, 16)
            sp.dma_start(bo, ins["L3_ffn_bo"]).then_inc(loaded, 16)

        @block.tensor
        def _(pe):
            pe.sem_inc(second_ready, 1)
            pe.wait_ge(loaded, 16 * (3 * NE + 1))
            with pe.Fori(0, NCH) as c:
                cols = ds(c * CH, CH)

                def first(e):
                    pe.wait_ge(first_done, c * NE + e + 1)
                    for f in range(KD):
                        for k in range(KD):
                            last = nc.tensor.matmul(m.banks[A[f]][:, 0:CH], w[0][:, e, k, f * P:(f + 1) * P],
                                                    m.yT[:, k, cols], start=k == 0, stop=k == KD - 1)
                    last.then_inc(first_ready, 1)
                    pe.wait_ge(gated, c * NE + e + 1)
                    pe.sem_inc(bank_claimed, 1)
                    nc.tensor.matmul(m.banks[GATE[e % 2]][:, 0:CH], m.pick[:, e, :], gate[:, cols], start=True,
                                     stop=True).then_inc(gate_spread, 1)

                def second(e):
                    pe.wait_ge(first_done, c * NE + e + 1 + 1)
                    pe.wait_ge(second_done, c * NE + e + 1)
                    for f in range(KD):
                        for k in range(KD):
                            last = nc.tensor.matmul(m.banks[B[f]][:, 0:CH], w[1][:, e, k, f * P:(f + 1) * P],
                                                    hid[:, e % 2, k, :], start=k == 0, stop=k == KD - 1)
                    last.then_inc(second_ready, 1)

                def third(e):
                    pe.wait_ge(gated, c * NE + e + 1 + 2)
                    for f in range(KD):
                        for k in range(KD):
                            last = nc.tensor.matmul(m.banks[OUT[f]][:, 0:CH], w[2][:, e, k, f * P:(f + 1) * P],
                                                    act2[:, e % 2, k, :], start=e == 0 and k == 0, stop=False,
                                                    skip_group_check=True)
                    last.then_inc(consumed, 1)

                first(0)
                first(1)
                second(0)
                pe.wait_ge(added, c + 1)
                for e in range(NE):
                    if e + 2 < NE:
                        first(e + 2)
                    if e + 1 < NE:
                        second(e + 1)
                    third(e)
                for f in range(KD):
                    last = nc.tensor.matmul(m.banks[OUT[f]][:, 0:CH], bo[:, f * P:(f + 1) * P], gate[:, cols],
                                            start=False, stop=True, skip_group_check=True)
                last.then_inc(out_ready, 1)

        @block.scalar
        def _(act):
            for l, n in enumerate("12"):
                last = nc.scalar.activation(scale[:, l, :], m.vec("L3_ffn_v" + n), ACT.Sqrt, bias=m.eps[:, 1:2])
            last.then_inc(rooted, 1)
            act.sem_inc(first_done, 1)
            act.sem_inc(second_done, 1)
            act.wait_ge(folded, 1)
            with act.Fori(0, NCH) as c:

                def relu(e, l, banks, to, ready, done):
                    act.wait_ge(ready, c * NE + e + 1 + l)
                    if l == 0:
                        act.wait_ge(second_ready, c * NE + max(e - 1, 0) + 1)
                    else:
                        act.wait_ge(consumed, c * NE + e + 1)
                    for f in range(KD):
                        last = nc.scalar.activation(to[:, e % 2, f, :], m.banks[banks[f]][:, 0:CH], ACT.Relu,
                                                    bias=bias[:, l, e * KD + f:e * KD + f + 1],
                                                    scale=scale[:, l, e * KD + f:e * KD + f + 1])
                    last.then_inc(done, 1)

                relu(0, 0, A, hid, first_ready, first_done)
                for e in range(NE):
                    if e + 1 < NE:
                        relu(e + 1, 0, A, hid, first_ready, first_done)
                    relu(e, 1, B, act2, second_ready, second_done)

        @block.vector
        def _(dve):
            step = Steps(dve, dve_step)
            dve.sem_inc(gated, 2)
            dve.sem_inc(consumed, 2)
            dve.sem_inc(added, 1)
            dve.wait_ge(rooted, 1)
            step(nc.vector.reciprocal(scale, scale))
            for l, n in enumerate("12"):
                nc.vector.tensor_tensor(bias[:, l, :], m.vec("L3_ffn_b" + n), m.vec("L3_ffn_m" + n), ALU.subtract)
                last = nc.vector.tensor_tensor(scale[:, l, :], scale[:, l, :], m.vec("L3_ffn_g" + n), ALU.mult)
            step(last)
            step(nc.vector.tensor_tensor(bias, bias, scale, ALU.mult))
            for l, n in enumerate("12"):
                last = nc.vector.tensor_tensor(bias[:, l, :], bias[:, l, :], m.vec("L3_ffn_be" + n), ALU.add)
            last.then_inc(folded, 1)
            with dve.Fori(0, NCH) as c:
                for e in range(NE):
                    dve.wait_ge(gate_spread, c * NE + e + 1)
                    dve.wait_ge(second_done, c * NE + e + 1 + 1)
                    for k in range(KD):
                        last = nc.vector.tensor_tensor(act2[:, e % 2, k, :], act2[:, e % 2, k, :],
                                                       m.banks[GATE[e % 2]][:, 0:CH], ALU.mult)
                    last.then_inc(gated, 1)
                dve.wait_ge(out_ready, c + 1)
                cols = ds(c * CH, CH)
                for f in range(KD):
                    last = nc.vector.tensor_tensor(m.xT[:, f, cols], m.xT[:, f, cols], m.banks[OUT[f]][:, 0:CH], ALU.add)
                last.then_inc(added, 1)


def moe_top_two(m):
    layer_norm(m, m.yT, m.yT, "L1_ffn_gamma", "L1_ffn_beta")
    experts_top_two(m, gates(m, "L1_ffn_Wr", "L1_ffn_br", top_two=True))


def program(nc, ins, out, stop=8):
    with ExitStack() as stack:
        m = Machine(nc, stack, ins, out)
        with nc.sbuf_tensor("source_tiles", [P, 2, EG + 2 * AHEAD], F32) as tiles:
            lo, key = tiles[:, 0, :], tiles[:, 1, :]
            with m.room(10 * EG + KEYS):
                setup(m, lo, key)
            with nc.sbuf_tensor("counts_in_sbuf", [P, NT, AW], BF16) as counts, \
                    nc.sbuf_tensor("edge_one_hots", [P, 2 * AHEAD * (P + KEYS)], BF16) as hot:
                build_counts(m, counts, lo, key, hot)
        with m.room():
            with if_general(m):
                general_sums(m)
        m.place_activations()
        with m.room():
            load_rows(m, ins["x"], m.xT)
        summing, other = dict(words=SUM_ROOM, split=SUM_SPLIT), {}
        sublayers = [
            (summing, lambda: sage(m, "L0_gnn_W1_l", "L0_gnn_W1_r", "L0_gnn_b1", "L0_gnn_W2_l", "L0_gnn_W2_r",
                                   "L0_gnn_b2")),
            (other, lambda: slice_attention(m)),
            (summing, lambda: gcn(m)),
            (other, lambda: moe_top_two(m)),
            (other, lambda: directional(m)),
            (other, lambda: experts_for_all(m)),
            (summing, lambda: sage(m, "L3_gnn_w1_l", "L3_gnn_w1_r", "L3_gnn_b1", "L3_gnn_w2_l", "L3_gnn_w2_r",
                                   "L3_gnn_b2")),
            (other, lambda: experts_deep(m, gates(m, "L3_ffn_Wr", "L3_ffn_br", top_two=False))),
        ]
        for room, sub in sublayers[:stop]:
            with m.room(**room):
                layer_norm(m, m.xT, m.yT)
                sub()
        with m.room():
            store_rows(m, m.xT, out)




def kernel(**inputs):
    import concourse.bacc as bacc
    from concourse.bass_utils import run_bass_kernel_spmd as run

    a = {k: np.asarray(v) for k, v in inputs.items()}

    def by_group(v, pad):
        full = np.full(P * EG, pad, v.dtype)
        full[:E] = v
        return np.ascontiguousarray(full.reshape(EG, P).T)

    ins = {
        "x": a["x"],
        "src": by_group(a["src"], 0),
        "dst": by_group(a["dst"], PAD_DST),
        "edge_w": by_group(a["edge_attr_2"][:, 0], 0),
        "snorm": np.pad(a["node_vec1"][:, 0], (0, NP - N)),
    }
    for name in ("w1_l", "w1_r", "w2_l", "w2_r"):
        ins[f"L3_gnn_{name}"] = a[f"L3_gnn_{name}"].T
    for name in ("L1_ffn_br", "L3_ffn_br"):
        ins[name] = a[name][:, None]
    ins["L2_ffn_br"] = a["L2_ffn_br"][None]
    for name in ("L2_ffn_b1", "L2_ffn_b2"):
        ins[name] = a[name].reshape(NE, -1, P).transpose(0, 2, 1)
    ins["L0_ffn_W_x_t"] = a["L0_ffn_W_x"].T
    ins["L0_ffn_b_fx"] = a["L0_ffn_b_fx"][None]
    ins["L0_ffn_b_slice"] = a["L0_ffn_b_slice"][None]
    ins["L0_ffn_temperature"] = a["L0_ffn_temperature"].reshape(HEADS)
    for name in ("L0_gnn_W1_l", "L0_gnn_W1_r", "L0_gnn_W2_l", "L0_gnn_W2_r", "L0_ffn_W_fx", "L0_ffn_W_out",
                 "L0_ffn_W_slice", "L0_ffn_W_q", "L0_ffn_W_k", "L0_ffn_W_v", "L1_gnn_W1", "L1_gnn_W2", "L1_gnn_W3",
                 "L1_ffn_Wr", "L1_ffn_W1", "L1_ffn_W2", "L1_ffn_b2", "L2_gnn_W1", "L2_gnn_W2", "L2_ffn_Wr",
                 "L2_ffn_W1", "L2_ffn_W2", "L3_ffn_Wr", "L3_ffn_W1", "L3_ffn_W2", "L3_ffn_Wo", "L3_ffn_bo"):
        ins[name] = a[name]
    ins["vecs"] = np.concatenate([a[n].reshape(-1, P).T for n in VECS], axis=1)
    nc = bacc.Bacc("TRN2", target_bir_lowering=False, num_devices=1)
    arrays, aps = {}, {}
    for name, v in ins.items():
        arrays[f"in_{name}"] = np.ascontiguousarray(v)
        aps[name] = nc.dram_tensor(f"in_{name}", v.shape, mybir.dt.from_np(v.dtype), kind="ExternalInput").ap()
    out = nc.dram_tensor("out", (N, D), F32, kind="ExternalOutput").ap()
    program(nc, aps, out)
    return run(nc, [arrays], core_ids=[0]).results[0]["out"]
```

```python
from contextlib import ExitStack, contextmanager
from math import ceil

import numpy as np

import concourse.bass as bass
from concourse import mybir

F32 = mybir.dt.float32
F32R = mybir.dt.float32r
F16 = mybir.dt.float16
BF16 = mybir.dt.bfloat16
I32 = mybir.dt.int32
U32 = mybir.dt.uint32
ALU = mybir.AluOpType
ACT = mybir.ActivationFunctionType
AX = mybir.AxisListType.X
RMAX = bass.bass_isa.ReduceOp.max
ds = bass.ds

N = 3125
D = 256
P = 128
KD = D // P
TP = 125
NT = N // TP
TU = 5
CH = 392
NCH = 8
NP = CH * NCH
HALF = NP // 2
PARTS = 2
WIN = 16
KEYS = NT * WIN
AW = NP + WIN // 2
BIG = 4 * AW + 16384
DT = 112
NDT = HALF // DT
MOST = 256
E = 53125
EG = 416
EU = 16
SLOTS = 8
AHEAD = 4
PAD_DST = 1 << 20
NE = 8
H1 = 512
HEADS = 8
G = 64
HG = HEADS * G

LN_EPS = 1e-5

VECS = {}
_at = 0
for _name, _n in [
    ("L0_gnn_b1", 2), ("L0_gnn_b2", 2), ("L0_ffn_b_out", 2), ("L0_ffn_b_x", 4),
    ("L1_gnn_b1", 2), ("L1_gnn_b2", 2), ("L1_gnn_b3", 2),
    ("L1_ffn_gamma", 2), ("L1_ffn_beta", 2), ("L1_ffn_b1", 32), ("L1_ffn_b2", 16),
    ("L2_gnn_b1", 2), ("L2_gnn_b2", 2), ("L2_gnn_gamma", 2), ("L2_gnn_beta", 2),
    ("L2_ffn_gamma", 2), ("L2_ffn_beta", 2),
    ("L3_gnn_b1", 2), ("L3_gnn_b2", 2),
    ("L3_ffn_b1", 16), ("L3_ffn_g1", 16), ("L3_ffn_be1", 16), ("L3_ffn_m1", 16), ("L3_ffn_v1", 16),
    ("L3_ffn_b2", 16), ("L3_ffn_g2", 16), ("L3_ffn_be2", 16), ("L3_ffn_m2", 16), ("L3_ffn_v2", 16), ("L3_ffn_bo", 16),
]:
    VECS[_name] = (_at, _n)
    _at += _n
NVEC = _at


class Machine:

    def __init__(self, nc, stack, ins, out):
        self.nc, self.stack, self.ins, self.out = nc, stack, ins, out
        self.stale = []
        self.in_branch = False
        self.rooms = 0
        sb = self.sb
        self.degree = sb("degree", [P, AW])
        self.onehot = sb("onehot", [P, 1536])
        self.flag = sb("flag", [1, 1], I32)
        self.spans = sb("spans", [P, 4])
        self.src = sb("src", [P, EG], I32)
        self.dst_rel = sb("dst_rel", [P, EG + SLOTS])
        self.edge_w = sb("edge_w", [P, EG + SLOTS])
        self.edge_abs = sb("edge_abs", [P, EG + SLOTS])
        self.base = sb("base", [1, EG], I32)
        self.src_cols = sb("src_cols", [P, 2, SLOTS], I32)
        self.base_cols = sb("base_cols", [1, 2, SLOTS], I32)
        self.ident = sb("ident", [P, P])
        self.ones = sb("ones", [P, P])
        self.mean_of = sb("mean_of", [P, P])
        self.count = sb("count", [P, P])
        self.zeros = sb("zeros", [P, AW // 8], BF16)
        self.vecs = sb("vecs", [P, NVEC])
        self.eps = sb("eps", [P, 2])
        self.small = sb("small", [P, 320])
        self.banks = [stack.enter_context(nc.psum_tensor(f"bank{i}", [P, 512], F32)) for i in range(8)]
        self.fetched = [stack.enter_context(nc.semaphore(f"fetched{s}")) for s in range(EU)]
        self.table = nc.dram_tensor("table", [N, D], F32, kind="Internal").ap()
        self.inverses = nc.dram_tensor("inverses", [2, NP], F32, kind="Internal").ap()
        self.gate_rows = nc.dram_tensor("gate_rows", [NE, NP], F32, kind="Internal").ap()
        self.counts = nc.dram_tensor("counts", [2, NT, TP, HALF], BF16, kind="Internal").ap()
        self.counts_rest = nc.dram_tensor("counts_rest", [2, NT, TP, HALF], BF16, kind="Internal").ap()

    def place_activations(self):
        self.yT = self.sb("activations", [P, KD, NP])
        self.xT = self.sb("residual", [P, KD, NP])

    @contextmanager
    def room(self, words=BIG, split=0):
        with ExitStack() as stack:
            self.rooms += 1
            self.big = stack.enter_context(self.nc.sbuf_tensor(f"big{self.rooms}", [P, words], F32))
            if split:
                self.split = stack.enter_context(self.nc.sbuf_tensor(f"split{self.rooms}", [P, split], F32R))
            else:
                self.gathered = stack.enter_context(self.nc.sbuf_tensor(f"gathered{self.rooms}", [P, SLOTS, D], F32))
            yield

    def sb(self, name, shape, dt=F32):
        return self.stack.enter_context(self.nc.sbuf_tensor(name, shape, dt))

    def vec(self, name, i=None):
        at, n = VECS[name]
        return self.vecs[:, at:at + n] if i is None else self.vecs[:, at + i:at + i + 1]

    def part(self, at, *shape):
        n = int(np.prod(shape))
        v = self.big[:, at:at + n]
        if len(shape) == 2:
            v = v.rearrange("p (a b) -> p a b", a=shape[0])
        if len(shape) == 3:
            v = v.rearrange("p (a b c) -> p a b c", a=shape[0], b=shape[1])
        return v

    @property
    def sums(self):
        return self.part(0, 6, AW)

    REG = 4 * AW


@contextmanager
def phase(m, *names):
    with ExitStack() as stack:
        sems = [stack.enter_context(m.nc.semaphore(n)) for n in names]
        stale, m.stale = m.stale, sems
        block = stack.enter_context(m.nc.Block())
        if m.in_branch:
            for engine in (block.sync, block.scalar, block.vector, block.tensor, block.gpsimd):
                @engine
                def _(eng):
                    eng.nop()

        @block.sync
        def _(sp):
            for s in stale:
                sp.sem_clear(s)

        yield block, *sems


@contextmanager
def branch(m, cond):
    with cond:
        m.in_branch = True
        before, m.stale = m.stale, []
        yield
        m.stale = before + m.stale
        m.in_branch = False


def settle(m):
    with phase(m):
        pass


class Steps:

    def __init__(self, eng, sem):
        self.eng, self.sem, self.n = eng, sem, 0

    def __call__(self, ins):
        ins.then_inc(self.sem, 1)
        self.n += 1
        self.eng.wait_ge(self.sem, self.n)


def tile_at(i, u, width, per):
    return ds(i * (width * per) + u * width, width)


def setup(m, lo, key):
    nc, ins = m.nc, m.ins
    dst = m.part(0, EG).bitcast(I32)
    neg = m.part(EG, EG)
    neg_base = m.part(2 * EG, EG)
    dst_f = m.part(3 * EG, EG)
    src_f = m.part(4 * EG, EG)
    base_f = m.part(5 * EG, EG)
    tile_i = m.part(6 * EG, EG).bitcast(I32)
    off = m.part(7 * EG, EG)
    real = m.part(8 * EG, EG)
    iota_i = m.part(9 * EG, KEYS).bitcast(I32)
    with phase(m, "loaded", "pool_step", "dst_ready", "base_ready", "dve_step") as \
            (block, loaded, pool_step, dst_ready, base_ready, dve_step):

        @block.sync
        def _(sp):
            sp.dma_start(dst, ins["dst"]).then_inc(loaded, 16)
            sp.dma_start(m.src[:, :], ins["src"]).then_inc(loaded, 16)
            sp.dma_start(m.edge_w[:, 0:EG], ins["edge_w"]).then_inc(loaded, 16)
            sp.dma_start(m.vecs[:, :], ins["vecs"]).then_inc(loaded, 16)
            sp.wait_ge(loaded, 64)

        @block.gpsimd
        def _(pool):
            step = Steps(pool, pool_step)
            nc.gpsimd.memset(m.ones[:, :], 1.0)
            nc.gpsimd.memset(m.mean_of[:, :], 1.0 / D)
            nc.gpsimd.memset(m.eps[:, 0:1], LN_EPS)
            nc.gpsimd.memset(m.eps[:, 1:2], 1e-3)
            nc.gpsimd.memset(m.zeros[:, :], 0.0)
            nc.gpsimd.memset(m.dst_rel[:, EG:], 0.0)
            nc.gpsimd.memset(m.edge_w[:, EG:], 0.0)
            nc.gpsimd.memset(lo[:, EG:], 0.0)
            nc.gpsimd.memset(key[:, EG:], 0.0)
            step(nc.gpsimd.iota(iota_i, [[1, KEYS]], base=0, channel_multiplier=0))
            nc.gpsimd.tensor_copy(m.count[:, :], iota_i[:, 0:P])
            nc.gpsimd.tensor_copy(key_count(m), iota_i)
            nc.gpsimd.affine_select(m.ident[:, :], m.ones[:, :], [[1, P]], ALU.is_equal, 0.0,
                                    base=0, channel_multiplier=-1)
            pool.wait_ge(dst_ready, 1)
            nc.gpsimd.partition_all_reduce(neg_base, neg, P, RMAX).then_inc(base_ready, 1)

        @block.scalar
        def _(act):
            act.wait_ge(loaded, 64)
            act.wait_ge(pool_step, 1)
            nc.scalar.activation(m.edge_abs[:, :], m.edge_w[:, :], ACT.Abs)

        @block.vector
        def _(dve):
            step = Steps(dve, dve_step)
            dve.wait_ge(loaded, 64)
            step(nc.vector.tensor_copy(dst_f, dst))
            dve.wait_ge(pool_step, 1)
            nc.vector.tensor_scalar(neg, dst_f, -1.0, None, ALU.mult).then_inc(dst_ready, 1)
            step(nc.vector.tensor_copy(src_f, m.src[:, :]))
            step(nc.vector.tensor_scalar(off, src_f, 1.0 / TP, -0.496, ALU.mult, ALU.add))
            step(nc.vector.tensor_copy(tile_i, off))
            step(nc.vector.tensor_copy(key[:, 0:EG], tile_i))
            for bound, sign in ((TP - 0.5, 1.0), (-0.5, -1.0)):
                step(nc.vector.scalar_tensor_tensor(lo[:, 0:EG], key[:, 0:EG], -float(TP), src_f, ALU.mult, ALU.add))
                step(nc.vector.tensor_scalar(off, lo[:, 0:EG], bound, sign, ALU.is_gt if sign > 0 else ALU.is_lt,
                                             ALU.mult))
                step(nc.vector.tensor_tensor(key[:, 0:EG], key[:, 0:EG], off, ALU.add))
            step(nc.vector.scalar_tensor_tensor(lo[:, 0:EG], key[:, 0:EG], -float(TP), src_f, ALU.mult, ALU.add))
            dve.wait_ge(base_ready, 1)
            step(nc.vector.tensor_tensor(m.dst_rel[:, 0:EG], dst_f, neg_base, ALU.add))
            nc.vector.scalar_tensor_tensor(key[:, 0:EG], key[:, 0:EG], float(WIN), m.dst_rel[:, 0:EG],
                                           ALU.mult, ALU.add)
            step(nc.vector.scalar_tensor_tensor(real, m.dst_rel[:, 0:EG], float(PAD_DST // 2), m.dst_rel[:, 0:EG],
                                                ALU.is_lt, ALU.mult))
            nc.vector.tensor_reduce(m.spans[:, 0:1], real, AX, ALU.max)
            step(nc.vector.tensor_scalar(base_f[0:1, :], neg_base[0:1, :], -1.0, None, ALU.mult))
            step(nc.vector.tensor_copy(m.base[:, :], base_f[0:1, :]))


def key_count(m):
    return m.onehot[:, 1200:1200 + KEYS // 2].bitcast(F16)


def build_counts(m, counts, lo, key, hot):
    nc = m.nc
    src_hot = hot[:, 0:2 * AHEAD * P].rearrange("p (s n) -> p s n", s=2 * AHEAD)
    key_hot = hot[:, 2 * AHEAD * P:].rearrange("p (s n) -> p s n", s=2 * AHEAD)
    MADE = EU // AHEAD
    lo_cols = m.small[:, 2 * SLOTS:4 * SLOTS].rearrange("p (h n) -> p h n", h=2)
    key_cols = m.small[:, 0:2 * SLOTS].rearrange("p (h n) -> p h n", h=2)
    with phase(m, "src_made", "key_made", "multiplied", "added", "cleared", "staged",
               "half_claimed", "lo_staged", "pool_claimed") as \
            (block, src_made, key_made, multiplied, added, cleared, staged, half_claimed,
             lo_staged, pool_claimed):

        @block.gpsimd
        def _(pool):
            nc.gpsimd.memset(counts[:, NT // 2:, :], 0.0).then_inc(cleared, 1)
            with pool.Fori(0, EG // EU) as i:
                for k in range(EU):
                    s = k % SLOTS
                    if s == 0:
                        pool.wait_ge(lo_staged, i * 2 + k // SLOTS + 1)
                    if k % AHEAD == 0:
                        pool.wait_ge(multiplied, i * (EU // AHEAD) + k // AHEAD - 1 + MADE)
                        pool.sem_inc(pool_claimed, 1)
                    last = nc.gpsimd.tensor_scalar(src_hot[:, s, :], m.count[:, :], lo_cols[:, k // SLOTS, s:s + 1], None,
                                                   ALU.is_equal)
                    if k % AHEAD == AHEAD - 1:
                        last.then_inc(src_made, 1)

        @block.scalar
        def _(act):
            act.sem_inc(src_made, MADE)
            with act.Fori(0, EG // EU) as i:
                for h in range(2):
                    act.wait_ge(src_made, i * (EU // AHEAD) + (h + 1) * (SLOTS // AHEAD))
                    nc.scalar.copy(lo_cols[:, h, :], lo[:, ds(i * EU + h * SLOTS, SLOTS)]).then_inc(lo_staged, 1)
                    act.wait_ge(key_made, i * EU + h * SLOTS + 1)
                    nc.scalar.copy(m.base_cols[:, h, :], m.base[:, ds(i * EU + h * SLOTS, SLOTS)])
                    nc.scalar.copy(key_cols[:, h, :], key[:, ds(i * EU + (h + 1) * SLOTS, SLOTS)]).then_inc(staged, 1)

        @block.tensor
        def _(pe):
            pe.sem_inc(multiplied, MADE)
            with pe.Fori(0, EG // EU) as i:
                for b in range(EU // AHEAD):
                    pe.wait_ge(src_made, i * (EU // AHEAD) + b + 1 + MADE)
                    pe.wait_ge(key_made, i * EU + (b + 1) * AHEAD)
                    pe.wait_ge(added, i * EU + (b + 1) * AHEAD)
                    for k in range(AHEAD):
                        s = b % 2 * AHEAD + k
                        last = nc.tensor.matmul(m.banks[s][:, 0:KEYS], src_hot[:, s, :], key_hot[:, s, :],
                                                start=True, stop=True)
                    last.then_inc(multiplied, 1)

        @block.vector
        def _(dve):
            def make_key(o, of):
                nc.vector.tensor_scalar(key_hot[:, o, :], key_count(m), of, None, ALU.is_equal)\
                    .then_inc(key_made, 1)

            for k in range(2 * AHEAD):
                make_key(k, key[:, k:k + 1])
            nc.vector.memset(counts[:, 0:NT // 2, :], 0.0).then_inc(cleared, 1)
            dve.wait_ge(cleared, 2)
            dve.sem_inc(added, 2 * AHEAD)
            with dve.Fori(0, EG // EU) as i:
                for k in range(EU):
                    s, half = k % SLOTS, k // SLOTS
                    if s == 0:
                        dve.wait_ge(staged, i * 2 + half + 1)
                        dve.sem_inc(half_claimed, 1)
                    at = dve.value_load(m.base_cols[0:1, half, s:s + 1], min_val=0, max_val=N - 1)
                    if k % AHEAD == 0:
                        dve.wait_ge(multiplied, i * (EU // AHEAD) + k // AHEAD + 1 + MADE)
                    dve.wait_ge(added, i * EU + k + 2 * AHEAD)
                    view = counts[:, :, ds(at, WIN)]
                    nc.vector.tensor_tensor(view, view, m.banks[s][:, 0:KEYS].rearrange("p (t n) -> p t n", t=NT),
                                            ALU.add).then_inc(added, 1)
                    make_key(s, key_cols[:, half, s:s + 1])

    ones = m.onehot[:, 0:P // 2].bitcast(BF16)
    degree = m.degree[:, 0:NP]
    with phase(m, "stored", "ones_ready", "multiplied", "taken", "spans_ready", "dve_step") as \
            (block, stored, ones_ready, multiplied, taken, spans_ready, dve_step):

        @block.sync
        def _(sp):
            for h in range(2):
                for t in range(0, NT, 5):
                    sp.dma_start(m.counts[h, t:t + 5].rearrange("t p n -> p t n"),
                                 counts[0:TP, t:t + 5, h * HALF:(h + 1) * HALF]).then_inc(stored, 16)
            sp.wait_ge(stored, 16 * 10)

        @block.tensor
        def _(pe):
            pe.wait_ge(ones_ready, 1)
            for c in range(NCH):
                for t in range(NT):
                    last = nc.tensor.matmul(m.banks[c][:, 0:CH], ones, counts[:, t, c * CH:(c + 1) * CH],
                                            start=t == 0, stop=t == NT - 1)
                last.then_inc(multiplied, 1)

        @block.gpsimd
        def _(pool):
            nc.gpsimd.memset(ones, 1.0).then_inc(ones_ready, 1)
            pool.wait_ge(taken, 1)
            nc.gpsimd.partition_all_reduce(m.spans[:, 1:2], m.spans[:, 0:1], P, RMAX).then_inc(spans_ready, 1)

        @block.vector
        def _(dve):
            step = Steps(dve, dve_step)
            for c in range(NCH):
                dve.wait_ge(multiplied, c + 1)
                last = nc.vector.tensor_copy(degree[:, c * CH:(c + 1) * CH], m.banks[c][:, 0:CH])
            step(last)
            nc.vector.tensor_reduce(m.spans[:, 2:3], degree, AX, ALU.max).then_inc(taken, 1)
            dve.wait_ge(spans_ready, 1)
            dve.wait_ge(taken, 1)
            nc.vector.tensor_scalar(m.spans[:, 1:2], m.spans[:, 1:2], WIN - 0.5, None, ALU.is_gt)
            step(nc.vector.tensor_scalar(m.spans[:, 2:3], m.spans[:, 2:3], MOST - 0.5, None, ALU.is_gt))
            step(nc.vector.tensor_tensor(m.spans[:, 0:1], m.spans[:, 1:2], m.spans[:, 2:3], ALU.add))
            nc.vector.tensor_copy(m.flag[:, :], m.spans[0:1, 0:1])


def if_general(m):
    settle(m)
    flag = m.nc.values_load(m.flag[0:1, 0:1], min_val=0, max_val=2)
    return branch(m, m.nc.If(flag > 0))


def general_sums(m, weighted=False):
    nc, ins = m.nc, m.ins
    nw = 3 if weighted else 1
    W = nw * DT
    at = [6 * AW + 2 * AW if weighted else 0]

    def reg(n):
        at[0] += n
        return m.part(at[0] - n, n)

    rel, src_f, src_rel, raw = reg(EG), reg(EG), reg(EG), reg(EG)
    hot = m.onehot[:, 0:2 * (P + W)].rearrange("p (u n) -> p u n", u=2)
    block_sums, acc, rows = reg(W), reg(3 * W).rearrange("p (f n) -> p f n", f=3), reg(D)
    if not weighted:
        hi, lo, back = reg(W // 2).bitcast(BF16), reg(W // 2).bitcast(BF16), reg(W)
    with phase(m, "loaded", "dve_step") as (block, loaded, dve_step):

        @block.sync
        def _(sp):
            sp.dma_start(raw.bitcast(I32), ins["dst"]).then_inc(loaded, 16)

        @block.vector
        def _(dve):
            nc.vector.tensor_copy(src_f, m.src[:, :])
            dve.wait_ge(loaded, 16)
            nc.vector.tensor_copy(rel, raw.bitcast(I32))

    with nc.Fori(0, 2) as h, nc.Fori(0, NDT) as j:
        with phase(m) as (block,):

            @block.vector
            def _(dve):
                nc.vector.tensor_copy(src_rel, src_f)
                nc.vector.memset(acc, 0.0)

        with nc.Fori(0, NT) as t:
            with phase(m, "made", "multiplied", "dve_step", "acc_ready", "block_ready", "rows_loaded", "stored") as \
                    (block, made, multiplied, dve_step, acc_ready, block_ready, rows_loaded, stored):

                @block.sync
                def _(sp):
                    if weighted:
                        sp.dma_start(rows[0:TP, :], m.table[ds(t * TP, TP), :]).then_inc(rows_loaded, 16)
                    else:
                        sp.wait_ge(block_ready, 2)
                        for of, to in ((hi, m.counts), (lo, m.counts_rest)):
                            sp.dma_start(to[ds(h, 1), ds(t, 1), :, ds(j * DT, DT)].rearrange("a b p n -> p (a b n)"),
                                         of[0:TP, :]).then_inc(stored, 16)
                        sp.wait_ge(stored, 32)

                @block.tensor
                def _(pe):
                    bank = m.banks[0][:, 0:W]
                    nc.tensor.matmul(bank, m.zeros[:, 0:P], m.zeros[:, 0:W], start=True, stop=False)
                    with pe.Fori(0, EG // 2) as i:
                        for u in range(2):
                            pe.wait_ge(made, i * 2 + u + 1)
                            nc.tensor.matmul(bank, hot[:, u, 0:P], hot[:, u, P:], start=False, stop=False,
                                             skip_group_check=True).then_inc(multiplied, 1)
                    nc.tensor.matmul(bank, m.zeros[:, 0:P], m.zeros[:, 0:W], start=False, stop=True)\
                        .then_inc(multiplied, 1)
                    pe.wait_ge(block_ready, 1)
                    if weighted:
                        pe.wait_ge(rows_loaded, 16)
                        for f in range(KD):
                            nc.tensor.matmul(m.banks[1 + f][:, 0:W], rows[0:TP, f * P:(f + 1) * P],
                                             block_sums[0:TP, :], start=True, stop=True)
                    nc.tensor.matmul(m.banks[3][:, 0:W], m.ones[0:TP, :], block_sums[0:TP, :], start=True,
                                     stop=True).then_inc(acc_ready, 1)

                @block.vector
                def _(dve):
                    dve.sem_inc(multiplied, 2)
                    with dve.Fori(0, EG // 2) as i:
                        for u in range(2):
                            c = ds(i * 2 + u, 1)
                            dve.wait_ge(multiplied, i * 2 + u + 1)
                            nc.vector.tensor_scalar(hot[:, u, 0:P], m.count[:, :], src_rel[:, c], None, ALU.is_equal)
                            if weighted:
                                for w, of in ((1, m.edge_abs), (2, m.edge_w)):
                                    nc.vector.tensor_scalar(hot[:, u, P + w * DT:P + (w + 1) * DT], m.count[:, 0:DT],
                                                            rel[:, c], of[:, c], ALU.is_equal, ALU.mult)
                            nc.vector.tensor_scalar(hot[:, u, P:P + DT], m.count[:, 0:DT], rel[:, c], None,
                                                    ALU.is_equal).then_inc(made, 1)
                    step = Steps(dve, dve_step)
                    dve.wait_ge(multiplied, EG + 3)
                    nc.vector.tensor_copy(block_sums, m.banks[0][:, 0:W]).then_inc(block_ready, 1)
                    nc.vector.tensor_scalar(src_rel, src_rel, -float(TP), None, ALU.add)
                    if not weighted:
                        dve.wait_ge(block_ready, 1)
                        step(nc.vector.tensor_copy(hi, block_sums))
                        step(nc.vector.tensor_copy(back, hi))
                        nc.vector.tensor_tensor(lo, block_sums, back, ALU.subtract).then_inc(block_ready, 1)
                    dve.wait_ge(acc_ready, 1)
                    for f in range(0 if weighted else 2, 3):
                        nc.vector.tensor_tensor(acc[:, f, :], acc[:, f, :], m.banks[1 + f][:, 0:W], ALU.add)

            settle(m)

        with phase(m) as (block,):

            @block.vector
            def _(dve):
                cols = ds(h * HALF + j * DT, DT)
                nc.vector.tensor_scalar(rel, rel, -float(DT), None, ALU.add)
                if weighted:
                    for w in range(3):
                        for f in range(KD):
                            nc.vector.tensor_copy(m.sums[:, 2 * w + f, cols], acc[:, f, w * DT:(w + 1) * DT])
                        if w:
                            nc.vector.tensor_copy(m.part(6 * AW, 2, AW)[:, w - 1, cols], acc[:, 2, w * DT:(w + 1) * DT])
                else:
                    nc.vector.tensor_copy(m.degree[:, cols], acc[:, 2, :])


def load_rows(m, rows, to):
    nc = m.nc
    stage = m.part(0, TU, D)
    with phase(m, "row_free", "transposed", *[f"row_loaded{u}" for u in range(TU)], "evacuated") as \
            (block, row_free, transposed, *row_loaded, evacuated):

        @block.sync
        def _(sp):
            with sp.Fori(0, NT // TU) as i:
                for u in range(TU):
                    sp.wait_ge(transposed, i * TU + u + 1)
                    sp.dma_start(stage[0:TP, u, :], rows[ds(i * (TU * TP) + u * TP, TP), :])\
                        .then_inc(row_loaded[u], 16)

        @block.gpsimd
        def _(pool):
            nc.gpsimd.memset(to[:, :, N:NP], 0.0)

        @block.tensor
        def _(pe):
            pe.sem_inc(transposed, TU)
            with pe.Fori(0, NT // TU) as i:
                for u in range(TU):
                    pe.wait_ge(row_loaded[u], i * 16 + 16)
                    pe.wait_ge(evacuated, i * TU + u + 1)
                    for k in range(KD):
                        last = nc.tensor.transpose(m.banks[u][:, k * TP:(k + 1) * TP],
                                                   stage[0:TP, u, k * P:(k + 1) * P], m.ident[0:TP, 0:TP])
                    last.then_inc(transposed, 1)

        @block.vector
        def _(dve):
            dve.sem_inc(evacuated, TU)
            with dve.Fori(0, NT // TU) as i:
                for u in range(TU):
                    dve.wait_ge(transposed, i * TU + u + 1 + TU)
                    nc.vector.tensor_copy(to[:, :, tile_at(i, u, TP, TU)],
                                          m.banks[u][:, 0:KD * TP].rearrange("p (k n) -> p k n", k=KD))\
                        .then_inc(evacuated, 1)


def store_rows(m, of, rows):
    nc = m.nc
    cols = m.part(0, TU, KD, TP)
    tile = m.part(TU * KD * TP, TU, D)
    with phase(m, "staged", "transposed", *[f"row_stored{u}" for u in range(TU)], "evacuated") as \
            (block, staged, transposed, *row_stored, evacuated):

        @block.scalar
        def _(act):
            with act.Fori(0, NT // TU) as i:
                for u in range(TU):
                    act.wait_ge(transposed, i * TU + u + 1)
                    nc.scalar.copy(cols[:, u, :, :], of[:, :, tile_at(i, u, TP, TU)]).then_inc(staged, 1)

        @block.tensor
        def _(pe):
            pe.sem_inc(transposed, TU)
            with pe.Fori(0, NT // TU) as i:
                for u in range(TU):
                    pe.wait_ge(staged, i * TU + u + 1)
                    pe.wait_ge(evacuated, i * TU + u + 1)
                    for k in range(KD):
                        last = nc.tensor.transpose(m.banks[u][0:TP, k * P:(k + 1) * P],
                                                   cols[:, u, k, :], m.ident[:, :])
                    last.then_inc(transposed, 1)

        @block.vector
        def _(dve):
            dve.sem_inc(evacuated, TU)
            with dve.Fori(0, NT // TU) as i:
                for u in range(TU):
                    dve.wait_ge(transposed, i * TU + u + 1 + TU)
                    dve.wait_ge(row_stored[u], i * 16 + 16)
                    nc.vector.tensor_copy(tile[0:TP, u, :], m.banks[u][0:TP, 0:D]).then_inc(evacuated, 1)

        @block.sync
        def _(sp):
            for u in range(TU):
                sp.sem_inc(row_stored[u], 16)
            with sp.Fori(0, NT // TU) as i:
                for u in range(TU):
                    sp.wait_ge(evacuated, i * TU + u + 1 + TU)
                    sp.dma_start(rows[ds(i * (TU * TP) + u * TP, TP), :], tile[0:TP, u, :])\
                        .then_inc(row_stored[u], 16)
            for u in range(TU):
                sp.wait_ge(row_stored[u], 16 * (NT // TU) + 16)


INVERSE, INVERSE_ROOT = 0, 1


def degree_row(m):
    return m.part(2 * AW, NP)


def invert_degrees(m):
    nc = m.nc
    ROWS = NDT * 4
    small = m.small[0:ROWS, 0:3 * (NP // ROWS)].rearrange("p (j n) -> p j n", j=3)
    of, inverse, root = small[:, 0, :], small[:, 1, :], small[:, 2, :]
    with phase(m, "degrees_out", "loaded", "dve_step", "rooted", "computed", "stored") as \
            (block, degrees_out, loaded, dve_step, rooted, computed, stored):

        @block.sync
        def _(sp):
            sp.dma_start(m.inverses[0:1, :], m.degree[0:1, 0:NP]).then_inc(degrees_out, 16)
            sp.wait_ge(degrees_out, 16)
            sp.dma_start(of, m.inverses[0].rearrange("(p n) -> p n", p=ROWS)).then_inc(loaded, 16)
            sp.wait_ge(computed, 1)
            for j, v in ((INVERSE, inverse), (INVERSE_ROOT, root)):
                sp.dma_start(m.inverses[j].rearrange("(p n) -> p n", p=ROWS), v).then_inc(stored, 16)
            sp.wait_ge(stored, 32)

        @block.scalar
        def _(act):
            act.wait_ge(dve_step, 1)
            nc.scalar.activation(root, root, ACT.Sqrt).then_inc(rooted, 1)

        @block.vector
        def _(dve):
            step = Steps(dve, dve_step)
            dve.wait_ge(loaded, 16)
            step(nc.vector.tensor_scalar(root, of, 1.0, None, ALU.add))
            step(nc.vector.tensor_scalar(inverse, of, 1.0, None, ALU.max))
            step(nc.vector.reciprocal(inverse, inverse))
            dve.wait_ge(rooted, 1)
            nc.vector.reciprocal(root, root).then_inc(computed, 1)


def layer_norm(m, of, to, gamma=None, beta=None, add_to=None, row=None):
    nc = m.nc
    LU = 4
    squares = m.part(0, LU, KD, CH)
    root = m.part(LU * KD * CH, LU, CH)
    pair = m.part(LU * (KD + 1) * CH, LU, CH)
    assert LU * (KD + 2) * CH <= 2 * AW
    with phase(m, "mean_ready", "centred", "squared", "var_ready", "root_ready", "normed", "scaled", "dve_step",
               "row_loaded", "paired", "squares_paired", "pool_claimed") as \
            (block, mean_ready, centred, squared, var_ready, root_ready, normed, scaled, dve_step,
             row_loaded, paired, squares_paired, pool_claimed):

        @block.sync
        def _(sp):
            if row is not None:
                sp.dma_start(degree_row(m), m.inverses[row].partition_broadcast(P)).then_inc(row_loaded, 16)
                sp.wait_ge(row_loaded, 16)

        @block.gpsimd
        def _(pool):
            with pool.Fori(0, NCH // LU) as i:
                for u in range(LU):
                    cols = tile_at(i, u, CH, LU)
                    pool.wait_ge(mean_ready, i * LU + u + 1)
                    pool.sem_inc(pool_claimed, 1)
                    nc.gpsimd.tensor_tensor(pair[:, u, :], of[:, 0, cols], of[:, 1, cols], ALU.add)\
                        .then_inc(paired, 1)
                for u in range(LU):
                    pool.wait_ge(squared, i * LU + u + 1)
                    pool.sem_inc(pool_claimed, 1)
                    nc.gpsimd.tensor_tensor(squares[:, u, 0, :], squares[:, u, 0, :], squares[:, u, 1, :], ALU.add)\
                        .then_inc(squares_paired, 1)

        @block.tensor
        def _(pe):
            pe.sem_inc(var_ready, LU)
            pe.sem_inc(mean_ready, LU)
            with pe.Fori(0, NCH // LU) as i:
                for u in range(LU):
                    pe.wait_ge(centred, i * LU + u + 1)
                    pe.wait_ge(paired, i * LU + u + 1)
                    nc.tensor.matmul(m.banks[u][:, 0:CH], m.mean_of[:, :], pair[:, u, :], start=True, stop=True)\
                        .then_inc(mean_ready, 1)
                for u in range(LU):
                    pe.wait_ge(squares_paired, i * LU + u + 1)
                    pe.wait_ge(root_ready, i * LU + u + 1)
                    nc.tensor.matmul(m.banks[LU + u][:, 0:CH], m.mean_of[:, :], squares[:, u, 0, :], start=True,
                                     stop=True).then_inc(var_ready, 1)

        @block.scalar
        def _(act):
            act.sem_inc(root_ready, LU)
            with act.Fori(0, NCH // LU) as i:
                for u in range(LU):
                    act.wait_ge(centred, i * LU + u + 1 + LU)
                    act.wait_ge(var_ready, i * LU + u + 1)
                    nc.scalar.activation(squares[:, u, :, :], to[:, :, tile_at(i, u, CH, LU)], ACT.Square)\
                        .then_inc(squared, 1)
                for u in range(LU):
                    act.wait_ge(var_ready, i * LU + u + 1 + LU)
                    act.wait_ge(normed, i * LU + u + 1)
                    nc.scalar.activation(root[:, u, :], m.banks[LU + u][:, 0:CH], ACT.Sqrt, bias=m.eps[:, 0:1])\
                        .then_inc(root_ready, 1)

        @block.vector
        def _(dve):
            dve.sem_inc(centred, LU)
            dve.sem_inc(normed, LU)
            with dve.Fori(0, NCH // LU) as i:
                for u in range(LU):
                    dve.wait_ge(mean_ready, i * LU + u + 1 + LU)
                    for k in range(KD):
                        cols = tile_at(i, u, CH, LU)
                        last = nc.vector.tensor_tensor(to[:, k, cols], of[:, k, cols], m.banks[u][:, 0:CH],
                                                       ALU.subtract)
                    last.then_inc(centred, 1)
                for u in range(LU):
                    cols = tile_at(i, u, CH, LU)
                    dve.wait_ge(root_ready, i * LU + u + 1 + LU)
                    nc.vector.reciprocal(root[:, u, :], root[:, u, :]).then_inc(dve_step, 1)
                    dve.wait_ge(dve_step, i * LU + u + 1)
                    dve.wait_ge(squared, i * LU + u + 1)
                    for k in range(KD):
                        last = nc.vector.tensor_tensor(to[:, k, cols], to[:, k, cols], root[:, u, :], ALU.mult)
                    last.then_inc(normed, 1)
                    if gamma:
                        dve.wait_ge(normed, i * LU + u + 1 + LU)
                        for k in range(KD):
                            last = nc.vector.tensor_scalar(to[:, k, cols], to[:, k, cols], m.vec(gamma, k),
                                                           m.vec(beta, k), ALU.mult, ALU.add)
                        last.then_inc(scaled, 1)
                    if add_to is not None:
                        dve.wait_ge(scaled, i * LU + u + 1)
                        for k in range(KD):
                            nc.vector.tensor_tensor(add_to[:, k, cols], add_to[:, k, cols], to[:, k, cols], ALU.add)


def turn_rows(m, of):
    nc = m.nc
    cols = m.part(0, TU, KD, TP)
    rows = row_tiles(m)
    with phase(m, "staged", "transposed", "evacuated") as (block, staged, transposed, evacuated):

        @block.scalar
        def _(act):
            with act.Fori(0, NT // TU) as i:
                for u in range(TU):
                    act.wait_ge(transposed, i * TU + u + 1)
                    nc.scalar.copy(cols[:, u, :, :], of[:, :, tile_at(i, u, TP, TU)]).then_inc(staged, 1)

        @block.tensor
        def _(pe):
            pe.sem_inc(transposed, TU)
            with pe.Fori(0, NT // TU) as i:
                for u in range(TU):
                    pe.wait_ge(staged, i * TU + u + 1)
                    pe.wait_ge(evacuated, i * TU + u + 1)
                    for k in range(KD):
                        last = nc.tensor.transpose(m.banks[u][0:TP, k * P:(k + 1) * P],
                                                   cols[:, u, k, :], m.ident[:, :])
                    last.then_inc(transposed, 1)

        @block.vector
        def _(dve):
            dve.sem_inc(evacuated, TU)
            with dve.Fori(0, NT // TU) as i:
                for u in range(TU):
                    dve.wait_ge(transposed, i * TU + u + 1 + TU)
                    nc.vector.tensor_copy(one_tile(rows, i, u), m.banks[u][0:TP, 0:D]).then_inc(evacuated, 1)


def row_tiles(m):
    return m.part(2 * AW + NP, NT, D)


def one_tile(rows, i, u):
    return rows[0:TP, ds(i * TU + u, 1), :].rearrange("p a d -> p (a d)")


SUM_ROOM = 2 * AW + NP + NT * D + TU * HALF // 2
SUM_SPLIT = TU * (HALF + PARTS * D)


def count_product(m, counts, first, with_self=False):
    nc = m.nc
    sums = m.sums
    rows = row_tiles(m)
    stream = m.part(SUM_ROOM - TU * HALF // 2, TU * HALF // 2).bitcast(BF16).rearrange("p (u n) -> p u n", u=TU)
    wide = m.split[:, 0:TU * HALF].rearrange("p (u n) -> p u n", u=TU)
    parts = m.split[:, TU * HALF:SUM_SPLIT].rearrange("p (u s d) -> p u s d", u=TU, s=PARTS)
    Q = HALF // CH
    CUT = HALF // 2
    with phase(m, *[f"counts_loaded{u}" for u in range(TU)], "high_ready", "act_ready", "dve_ready", "consumed",
               "half_ready", "taken") as \
            (block, *counts_loaded, high_ready, act_ready, dve_ready, consumed, half_ready, taken):

        @block.sync
        def _(sp):
            for h in range(2):
                with sp.Fori(0, NT // TU) as i:
                    for u in range(TU):
                        sp.wait_ge(act_ready, h * NT + i * TU + u + 1)
                        sp.wait_ge(dve_ready, h * NT + i * TU + u + 1)
                        sp.dma_start(stream[0:TP, u, :], counts[h][ds(i * TU + u, 1)].rearrange("a p n -> p (a n)"))\
                            .then_inc(counts_loaded[u], 16)

        @block.tensor
        def _(pe):
            pe.sem_inc(consumed, TU)
            for h in range(2):
                if h:
                    pe.wait_ge(taken, 2 * h)
                for bank in m.banks:
                    nc.tensor.matmul(bank[:, 0:CH], m.zeros[:, 0:P], m.zeros[:, 0:CH], start=True, stop=False)
                with pe.Fori(0, NT // TU) as i:
                    for u in range(TU):
                        pe.wait_ge(act_ready, h * NT + i * TU + u + 1 + TU)
                        pe.wait_ge(dve_ready, h * NT + i * TU + u + 1 + TU)
                        for part in range(PARTS):
                            for f in range(KD):
                                for q in range(Q):
                                    last = nc.tensor.matmul(m.banks[f * Q + q][:, 0:CH],
                                                            parts[0:TP, u, part, f * P:(f + 1) * P],
                                                            wide[0:TP, u, q * CH:(q + 1) * CH],
                                                            start=False, stop=False, skip_group_check=True)
                        last.then_inc(consumed, 1)
                for bank in m.banks:
                    last = nc.tensor.matmul(bank[:, 0:CH], m.zeros[:, 0:P], m.zeros[:, 0:CH], start=False, stop=True)
                last.then_inc(half_ready, 1)

        def take(h, f, plain):
            for q in range(Q):
                cols = slice((h * Q + q) * CH, (h * Q + q + 1) * CH)
                bank = m.banks[f * Q + q][:, 0:CH]
                if not first:
                    last = nc.vector.tensor_tensor(sums[:, f, cols], sums[:, f, cols], bank, ALU.add)
                elif with_self:
                    last = nc.vector.tensor_tensor(sums[:, f, cols], m.yT[:, f, cols], bank, ALU.add)
                else:
                    last = plain(sums[:, f, cols], bank)
            last.then_inc(taken, 1)

        plain_on_act = first and not with_self

        @block.scalar
        def _(act):
            act.sem_inc(act_ready, TU)
            for h in range(2):
                with act.Fori(0, NT // TU) as i:
                    for u in range(TU):
                        act.wait_ge(consumed, h * NT + i * TU + u + 1)
                        nc.scalar.copy(parts[0:TP, u, 0, :], one_tile(rows, i, u)).then_inc(high_ready, 1)
                        act.wait_ge(counts_loaded[u], (h * (NT // TU) + i + 1) * 16)
                        nc.scalar.copy(wide[0:TP, u, 0:CUT], stream[0:TP, u, 0:CUT]).then_inc(act_ready, 1)
                if plain_on_act:
                    act.wait_ge(half_ready, h + 1)
                    take(h, 0, nc.scalar.copy)

        @block.vector
        def _(dve):
            dve.sem_inc(dve_ready, TU)
            for h in range(2):
                with dve.Fori(0, NT // TU) as i:
                    for u in range(TU):
                        dve.wait_ge(consumed, h * NT + i * TU + u + 1)
                        dve.wait_ge(counts_loaded[u], (h * (NT // TU) + i + 1) * 16)
                        nc.vector.tensor_copy(wide[0:TP, u, CUT:], stream[0:TP, u, CUT:])
                        dve.wait_ge(high_ready, h * NT + i * TU + u + 1)
                        nc.vector.tensor_tensor(parts[0:TP, u, 1, :], one_tile(rows, i, u), parts[0:TP, u, 0, :]
                                                .bitcast(F32), ALU.subtract).then_inc(dve_ready, 1)
                dve.wait_ge(half_ready, h + 1)
                if not plain_on_act:
                    take(h, 0, None)
                take(h, 1, nc.vector.tensor_copy)


def neighbour_sums(m, with_self=False):
    turn_rows(m, m.yT)
    count_product(m, m.counts, True, with_self)
    with if_general(m):
        count_product(m, m.counts_rest, False)


def weighted_sums(m):
    nc = m.nc
    all_sums = m.part(0, 8, AW)
    hot = m.onehot[:, 0:SLOTS * 3 * WIN].rearrange("p (s w n) -> p s w n", s=SLOTS, w=3)
    W = 3 * WIN
    edge_cols = m.small[:, 0:2 * 3 * SLOTS].rearrange("p (h j n) -> p h j n", h=2, j=3)
    fetched = m.fetched
    rows = [m.gathered[:, k, :] if k < SLOTS else m.part(8 * AW, EU - SLOTS, D)[:, k - SLOTS, :] for k in range(EU)]
    product = lambda k: m.banks[k // AHEAD][:, k % AHEAD * 8 * WIN:(k % AHEAD + 1) * 8 * WIN]
    DONE = EU // AHEAD + 1
    with phase(m, "staged", "made", "multiplied", "added", "cleared", "slot_claimed", "edges_staged", "half_claimed") as \
            (block, staged, made, multiplied, added, cleared, slot_claimed, edges_staged, half_claimed):

        @block.scalar
        def _(act):
            nc.scalar.copy(m.part(4 * AW, 32, AW // 8), repeat_first(m.zeros[:, :], 32)).then_inc(cleared, 1)
            with act.Fori(0, EG // EU) as i:
                for h in range(2):
                    act.wait_ge(made, i * EU + h * SLOTS + 1)
                    nc.scalar.copy(m.base_cols[:, h, :], m.base[:, ds(i * EU + h * SLOTS, SLOTS)])
                    for j, of in enumerate((m.dst_rel, m.edge_abs, m.edge_w)):
                        last = nc.scalar.copy(edge_cols[:, h, j, :], of[:, ds(i * EU + (h + 1) * SLOTS, SLOTS)])
                    last.then_inc(edges_staged, 1)

        @block.gpsimd
        def _(pool):
            with pool.Fori(0, EG // EU) as i:
                for k in range(EU):
                    s = k % SLOTS
                    if s == 0:
                        pool.wait_ge(multiplied, i * (EU // AHEAD) + (k - SLOTS) // AHEAD + DONE)
                        pool.sem_inc(slot_claimed, 1)
                        nc.gpsimd.tensor_copy(m.src_cols[:, k // SLOTS, :], m.src[:, ds(i * EU + k, SLOTS)])\
                            .then_inc(staged, 1)
                        pool.wait_ge(staged, i * 2 + k // SLOTS + 1)
                        pool.sem_inc(slot_claimed, 1)
                    nc.gpsimd.indirect_dma_start(
                        rows[k], None, m.table,
                        bass.IndirectOffsetOnAxis(ap=m.src_cols[:, k // SLOTS, s:s + 1].bitcast(U32), axis=0),
                    ).then_inc(fetched[k], 16)

        @block.tensor
        def _(pe):
            pe.sem_inc(multiplied, DONE)
            with pe.Fori(0, EG // EU) as i:
                for k in range(EU):
                    s = k % SLOTS
                    if k % AHEAD == 0:
                        pe.wait_ge(made, i * EU + k + AHEAD)
                        pe.wait_ge(added, i * EU + k + AHEAD)
                    pe.wait_ge(fetched[k], i * 16 + 16)
                    for f in range(KD):
                        to = product(k)[:, 0:KD * W].rearrange("p (w f n) -> p f w n", w=3, f=KD)[:, f, :, :]
                        last = nc.tensor.matmul(to, rows[k][:, f * P:(f + 1) * P], hot[:, s, :, :],
                                                start=True, stop=True)
                    if k % AHEAD == AHEAD - 1:
                        to = m.banks[k // AHEAD][:, :].rearrange("p (k n) -> p k n", k=AHEAD)[:, :, KD * W:]
                        nc.tensor.matmul(to, m.ones[:, :], hot[:, s + 1 - AHEAD:s + 1, 1:3, :], start=True,
                                         stop=True).then_inc(multiplied, 1)

        @block.vector
        def _(dve):
            def make(o, rel, size, weight):
                nc.vector.tensor_scalar(hot[:, o, 0, :], m.count[:, 0:WIN], rel, None, ALU.is_equal)
                nc.vector.tensor_scalar(hot[:, o, 2, :], m.count[:, 0:WIN], rel, weight,
                                        ALU.is_equal, ALU.mult)
                nc.vector.tensor_scalar(hot[:, o, 1, :], m.count[:, 0:WIN], rel, size,
                                        ALU.is_equal, ALU.mult).then_inc(made, 1)

            for k in range(SLOTS):
                make(k, *(of[:, k:k + 1] for of in (m.dst_rel, m.edge_abs, m.edge_w)))
            nc.vector.memset(all_sums[:, 0:4, :], 0.0).then_inc(cleared, 1)
            dve.wait_ge(cleared, 2)
            dve.sem_inc(added, SLOTS)
            with dve.Fori(0, EG // EU) as i:
                for k in range(EU):
                    s, half = k % SLOTS, k // SLOTS
                    if s == 0:
                        dve.wait_ge(edges_staged, i * 2 + half + 1)
                        dve.sem_inc(half_claimed, 1)
                    at = dve.value_load(m.base_cols[0:1, half, s:s + 1], min_val=0, max_val=N - 1)
                    if k % AHEAD == 0:
                        dve.wait_ge(multiplied, i * (EU // AHEAD) + k // AHEAD + 1 + DONE)
                    dve.wait_ge(added, i * EU + k + SLOTS)
                    view = all_sums[:, :, ds(at, WIN)]
                    nc.vector.tensor_tensor(view, view, product(k).rearrange(
                        "p (w n) -> p w n", w=8), ALU.add).then_inc(added, 1)
                    make(s, *(edge_cols[:, half, j, s:s + 1] for j in range(3)))


def sage_update(m, w_l, w_r, b, last_layer):
    nc, ins = m.nc, m.ins
    w = m.part(m.REG, 2, KD, D)
    inverse = degree_row(m)
    mean = m.part(m.REG + 1024 + NP, 2, KD * CH)
    sums = m.sums
    with phase(m, "loaded", "averaged", "multiplied", "taken") as \
            (block, loaded, averaged, multiplied, taken):

        @block.sync
        def _(sp):
            for j, name in enumerate((w_l, w_r)):
                sp.dma_start(w[:, j, :, :], ins[name].rearrange("(k p) o -> p k o", p=P)).then_inc(loaded, 16)

        @block.tensor
        def _(pe):
            pe.sem_inc(multiplied, 2)
            pe.wait_ge(loaded, 32)
            with pe.Fori(0, NCH // 2) as i:
                for u in range(2):
                    pe.wait_ge(averaged, i * 2 + u + 1 + 2)
                    pe.wait_ge(taken, i * 2 + u + 1)
                    mu = mean[:, u, :].rearrange("p (k n) -> p k n", k=KD)
                    for f in range(KD):
                        cols = slice(f * P, (f + 1) * P)
                        for k in range(KD):
                            nc.tensor.matmul(m.banks[2 * u + f][:, 0:CH], w[:, 1, k, cols],
                                             m.yT[:, k, tile_at(i, u, CH, 2)], start=k == 0, stop=False)
                        for k in range(KD):
                            last = nc.tensor.matmul(m.banks[2 * u + f][:, 0:CH], w[:, 0, k, cols],
                                                    mu[:, k, :], start=False, stop=k == KD - 1)
                    last.then_inc(multiplied, 1)

        @block.vector
        def _(dve):
            dve.sem_inc(averaged, 2)

            def average(i, u):
                mu = mean[:, u, :].rearrange("p (k n) -> p k n", k=KD)
                cols = tile_at(i, u, CH, 2)
                for k in range(KD):
                    last = nc.vector.tensor_tensor(mu[:, k, :], sums[:, k, cols], inverse[:, cols], ALU.mult)
                last.then_inc(averaged, 1)

            with dve.Fori(0, NCH // 2) as i:
                for u in range(2):
                    dve.wait_ge(multiplied, i * 2 + u + 1)
                    average(i, u)
                if last_layer:
                    for u in range(2):
                        cols = tile_at(i, u, CH, 2)
                        dve.wait_ge(multiplied, i * 2 + u + 1 + 2)
                        for f in range(KD):
                            last = nc.vector.scalar_tensor_tensor(
                                m.xT[:, f, cols], m.banks[2 * u + f][:, 0:CH], m.vec(b, f), m.xT[:, f, cols],
                                ALU.add, ALU.add)
                        last.then_inc(taken, 1)

        @block.scalar
        def _(act):
            act.sem_inc(taken, 2)
            if not last_layer:
                with act.Fori(0, NCH // 2) as i:
                    for u in range(2):
                        act.wait_ge(multiplied, i * 2 + u + 1 + 2)
                        for f in range(KD):
                            last = nc.scalar.activation(m.yT[:, f, tile_at(i, u, CH, 2)],
                                                        m.banks[2 * u + f][:, 0:CH], ACT.Relu, bias=m.vec(b, f))
                        last.then_inc(taken, 1)


def sage(m, w1_l, w1_r, b1, w2_l, w2_r, b2):
    neighbour_sums(m)
    sage_update(m, w1_l, w1_r, b1, False)
    neighbour_sums(m)
    sage_update(m, w2_l, w2_r, b2, True)


def repeat_last(ap, n):
    return ap.unsqueeze(2).broadcast_to([*ap.shape, n])


def repeat_first(ap, n):
    return ap.unsqueeze(1).broadcast_to([ap.shape[0], n, ap.shape[1]])


def slice_attention(m):
    nc, ins = m.nc, m.ins
    at = [m.REG]

    def reg(*shape):
        v = m.part(at[0], *shape)
        at[0] += int(np.prod(shape))
        return v

    HP = HG // P
    wT = m.part(0, HP, NP)
    wx_t = reg(HP, D)
    wfx = reg(KD, HG)
    wo = reg(HP, D)
    pair = reg(4, P)
    wc = reg(KD, HG)
    bc = reg(HG)
    b_fx = reg(HG)
    b_slice = reg(G)
    inv_temp = reg(HEADS)
    mixed = reg(HP, D + 1)
    mixed_t = reg(KD, HG)
    share = reg(HG)
    tok = reg(HG)
    q_t, k_t, v_s = reg(HG), reg(HG), reg(HG)
    score = reg(HP, G)
    attn, attn_t, out_t = reg(HG), reg(HG), reg(HG)
    mo = reg(HP, D)
    probs = reg(TU, HG)
    assert at[0] <= 4 * AW + 16384
    zero = attn
    y_rows = m.gathered
    y_cols = m.onehot[:, 0:TU * KD * TP].rearrange("p (u k n) -> p u k n", u=TU, k=KD)
    top = m.small[:, 0:TU * HEADS].rearrange("p (u h) -> p u h", u=TU)
    tot = m.small[:, 64:64 + TU * HEADS].rearrange("p (u h) -> p u h", u=TU)
    tiny = m.small[:, 128:160]

    def four(ap):
        return ap.rearrange("p (j n) -> p j n", j=HP)

    def diagonal(ap, b):
        return four(ap)[b * G:(b + 1) * G, :, b * G:(b + 1) * G]

    with phase(m, "cleared", "loaded", "multiplied", "dve_step") as (block, cleared, loaded, multiplied, dve_step):

        @block.gpsimd
        def _(pool):
            nc.gpsimd.memset(attn, 0.0)
            nc.gpsimd.memset(tok, 0.0)
            nc.gpsimd.memset(wT[:, :, N:NP], 0.0)
            nc.gpsimd.memset(pair, 0.0).then_inc(cleared, 1)

        @block.sync
        def _(sp):
            def load(to, of):
                sp.dma_start(to, of).then_inc(loaded, 16)

            load(wx_t, ins["L0_ffn_W_x_t"].rearrange("(j p) f -> p j f", p=P))
            load(wfx, ins["L0_ffn_W_fx"].rearrange("(k p) o -> p k o", p=P))
            load(wo, ins["L0_ffn_W_out"].rearrange("(j p) o -> p j o", p=P))
            load(b_fx[0:1, :], ins["L0_ffn_b_fx"])
            load(b_slice[0:1, :], ins["L0_ffn_b_slice"])
            load(inv_temp, ins["L0_ffn_temperature"].partition_broadcast(P))
            sp.wait_ge(cleared, 1)
            for w, name in enumerate(("W_slice", "W_q", "W_k", "W_v")):
                for b in range(2):
                    load(pair[b * G:(b + 1) * G, w, b * G:(b + 1) * G], ins["L0_ffn_" + name])
            sp.wait_ge(loaded, 16 * 14)

        @block.tensor
        def _(pe):
            pe.wait_ge(loaded, 16 * 14)
            for j in range(HP):
                for k in range(KD):
                    nc.tensor.matmul(m.banks[k][:, j * P:(j + 1) * P], wx_t[:, j, k * P:(k + 1) * P], pair[:, 0, :],
                                     start=True, stop=True)
                last = nc.tensor.matmul(m.banks[2][0:1, j * P:(j + 1) * P], m.vec("L0_ffn_b_x", j), pair[:, 0, :],
                                        start=True, stop=True)
            last.then_inc(multiplied, 1)

        @block.vector
        def _(dve):
            step = Steps(dve, dve_step)
            dve.wait_ge(loaded, 16 * 14)
            step(nc.vector.tensor_scalar(inv_temp, inv_temp, 0.1, 5.0, ALU.max, ALU.min))
            step(nc.vector.reciprocal(inv_temp, inv_temp))
            dve.wait_ge(multiplied, 1)
            heads = lambda ap: ap.rearrange("p (h g) -> p h g", h=HEADS)
            for k in range(KD):
                nc.vector.tensor_tensor(heads(wc[:, k, :]), heads(m.banks[k][:, :]), repeat_last(inv_temp, G), ALU.mult)
            step(nc.vector.tensor_tensor(heads(bc[0:1, :]), heads(m.banks[2][0:1, :]),
                                         repeat_first(b_slice[0:1, :], HEADS), ALU.add))
            step(nc.vector.tensor_tensor(heads(bc[0:1, :]), heads(bc[0:1, :]), repeat_last(inv_temp[0:1, :], G),
                                         ALU.mult))

    LOGITS, ROWS, TURNED, NORM, MIXED = (0, 1), 2, (3, 4), 5, (6, 7)
    with phase(m, "staged", "y_turned", "y_taken", "logits_ready", "centred", "exped", "normed", "mixed_in",
               "w_turned", "w_taken", "maxed", "summed", "inverted") as \
            (block, staged, y_turned, y_taken, logits_ready, centred, exped, normed, mixed_in,
             w_turned, w_taken, maxed, summed, inverted):

        @block.scalar
        def _(act):
            act.sem_inc(y_taken, 1)
            act.sem_inc(w_taken, 2)

            def front(i, u):
                act.wait_ge(mixed_in, i * TU + u + 1)
                nc.scalar.copy(y_cols[:, u, :, :], m.yT[:, :, tile_at(i, u, TP, TU)]).then_inc(staged, 1)
                act.wait_ge(y_turned, i * TU + u + 1)
                nc.scalar.copy(y_rows[0:TP, u, :], m.banks[ROWS][0:TP, 0:D]).then_inc(y_taken, 1)

            def back(i, u):
                act.wait_ge(centred, i * TU + u + 1 + 1)
                nc.scalar.activation(probs[0:TP, u, :], probs[0:TP, u, :], ACT.Exp).then_inc(exped, 1)

            def last(i, u):
                act.wait_ge(w_turned, i * TU + u + 1)
                nc.scalar.copy(wT[:, :, tile_at(i, u, TP, TU)],
                               m.banks[TURNED[u % 2]][:, 0:HP * TP].rearrange("p (j n) -> p j n", j=HP))\
                    .then_inc(w_taken, 1)

            with act.Fori(0, NT // TU) as i:
                front(i, 0)
                for u in range(TU):
                    if u + 1 < TU:
                        front(i, u + 1)
                    back(i, u)
                    if u:
                        last(i, u - 1)
                last(i, TU - 1)

        @block.tensor
        def _(pe):
            pe.sem_inc(mixed_in, TU)
            for b in MIXED:
                nc.tensor.matmul(m.banks[b][:, :], zero[:, 0:P], zero, start=True, stop=False)
            nc.tensor.matmul(m.banks[NORM][:, 0:HP], zero[:, 0:P], zero[:, 0:HP], start=True, stop=False)

            def front(i, u):
                pe.wait_ge(staged, i * TU + u + 1)
                pe.wait_ge(y_taken, i * TU + u + 1)
                for k in range(KD):
                    last = nc.tensor.transpose(m.banks[ROWS][0:TP, k * P:(k + 1) * P], y_cols[:, u, k, :], m.ident[:, :])
                last.then_inc(y_turned, 1)
                pe.wait_ge(centred, i * TU + max(u - 1, 0) + 1)
                logits = m.banks[LOGITS[u % 2]][0:TP, :]
                for k in range(KD):
                    nc.tensor.matmul(logits, y_cols[:, u, k, :], wc[:, k, :], start=k == 0, stop=False)
                nc.tensor.matmul(logits, m.ones[0:1, 0:TP], bc[0:1, :], start=False, stop=True)\
                    .then_inc(logits_ready, 1)

            def back(i, u):
                pe.wait_ge(normed, i * TU + u + 1)
                pe.wait_ge(y_taken, i * TU + u + 1 + 1)
                pe.wait_ge(w_taken, i * TU + u + 1 + (u == 0))
                for j in range(HP):
                    w = probs[0:TP, u, j * P:(j + 1) * P]
                    nc.tensor.transpose(m.banks[TURNED[u % 2]][:, j * TP:(j + 1) * TP], w, m.ident[0:TP, 0:TP])\
                        .then_inc(w_turned, 1) if j == HP - 1 else \
                        nc.tensor.transpose(m.banks[TURNED[u % 2]][:, j * TP:(j + 1) * TP], w, m.ident[0:TP, 0:TP])
                for j in range(HP):
                    w = probs[0:TP, u, j * P:(j + 1) * P]
                    nc.tensor.matmul(m.banks[MIXED[j // 2]][:, (j % 2) * D:(j % 2 + 1) * D], w, y_rows[0:TP, u, :],
                                     start=False, stop=False, skip_group_check=True)
                    last = nc.tensor.matmul(m.banks[NORM][:, j:j + 1], w, m.ones[0:TP, 0:1], start=False, stop=False,
                                            skip_group_check=True)
                last.then_inc(mixed_in, 1)

            with pe.Fori(0, NT // TU) as i:
                front(i, 0)
                for u in range(TU):
                    if u + 1 < TU:
                        front(i, u + 1)
                    back(i, u)
            for b in MIXED:
                nc.tensor.matmul(m.banks[b][:, :], zero[:, 0:P], zero, start=False, stop=True)
            nc.tensor.matmul(m.banks[NORM][:, 0:HP], zero[:, 0:P], zero[:, 0:HP], start=False, stop=True)

        @block.vector
        def _(dve):
            heads = lambda ap: ap.rearrange("p (h g) -> p h g", h=HEADS)

            def centre(i, u):
                logits = heads(m.banks[LOGITS[u % 2]][0:TP, :])
                dve.wait_ge(logits_ready, i * TU + u + 1)
                nc.vector.tensor_reduce(top[0:TP, u, :], logits, AX, ALU.max).then_inc(maxed, 1)
                dve.wait_ge(maxed, i * TU + u + 1)
                dve.wait_ge(mixed_in, i * TU + u + 1)
                nc.vector.tensor_tensor(heads(probs[0:TP, u, :]), logits, repeat_last(top[0:TP, u, :], G),
                                        ALU.subtract).then_inc(centred, 1)

            def norm(i, u):
                p = heads(probs[0:TP, u, :])
                dve.wait_ge(exped, i * TU + u + 1)
                nc.vector.tensor_reduce(tot[0:TP, u, :], p, AX, ALU.add).then_inc(summed, 1)
                dve.wait_ge(summed, i * TU + u + 1)
                nc.vector.reciprocal(tot[0:TP, u, :], tot[0:TP, u, :]).then_inc(inverted, 1)
                dve.wait_ge(inverted, i * TU + u + 1)
                nc.vector.tensor_tensor(p, p, repeat_last(tot[0:TP, u, :], G), ALU.mult).then_inc(normed, 1)

            dve.sem_inc(centred, 1)
            with dve.Fori(0, NT // TU) as i:
                centre(i, 0)
                for u in range(TU):
                    norm(i, u)
                    if u + 1 < TU:
                        centre(i, u + 1)

    with phase(m, "multiplied", "taken", "dve_step", "exped") as (block, multiplied, taken, dve_step, exped):

        @block.tensor
        def _(pe):
            pe.wait_ge(taken, 1)
            for j in range(HP):
                for k in range(KD):
                    nc.tensor.transpose(m.banks[k][:, j * P:(j + 1) * P], mixed[:, j, k * P:(k + 1) * P], m.ident[:, :])
                last = nc.tensor.transpose(m.banks[2][0:1, j * P:(j + 1) * P], mixed[:, j, D:D + 1], m.ident[:, :])
            last.then_inc(multiplied, 1)
            pe.wait_ge(taken, 2)
            for j in range(HP):
                cols = slice(j * P, (j + 1) * P)
                for k in range(KD):
                    nc.tensor.matmul(m.banks[3][:, cols], wfx[:, k, cols], mixed_t[:, k, cols], start=k == 0, stop=False)
                last = nc.tensor.matmul(m.banks[3][:, cols], b_fx[0:1, cols], share[0:1, cols], start=False, stop=True)
            last.then_inc(multiplied, 1)
            pe.wait_ge(taken, 3)
            nc.tensor.matmul(m.banks[4][:, :], pair[:, 1, :], tok, start=True, stop=True)
            nc.tensor.matmul(m.banks[5][:, :], pair[:, 2, :], tok, start=True, stop=True)
            for j in range(HP):
                cols = slice(j * P, (j + 1) * P)
                last = nc.tensor.matmul(m.banks[6][:, cols], tok[:, cols], pair[:, 3, :], start=True, stop=True)
            last.then_inc(multiplied, 1)
            pe.wait_ge(taken, 4)
            for j in range(HP):
                cols = slice(j * P, (j + 1) * P)
                last = nc.tensor.matmul(m.banks[7][:, cols], q_t[:, cols], k_t[:, cols], start=True, stop=True)
            last.then_inc(multiplied, 1)
            pe.wait_ge(taken, 5)
            for j in range(HP):
                cols = slice(j * P, (j + 1) * P)
                last = nc.tensor.transpose(m.banks[0][:, cols], attn[:, cols], m.ident[:, :])
            last.then_inc(multiplied, 1)
            pe.wait_ge(taken, 6)
            for j in range(HP):
                cols = slice(j * P, (j + 1) * P)
                last = nc.tensor.matmul(m.banks[1][:, cols], v_s[:, cols], attn_t[:, cols], start=True, stop=True)
            last.then_inc(multiplied, 1)
            pe.wait_ge(taken, 7)
            for j in range(HP):
                last = nc.tensor.matmul(m.banks[2 + j // 2][:, (j % 2) * D:(j % 2 + 1) * D],
                                        out_t[:, j * P:(j + 1) * P], wo[:, j, :], start=True, stop=True)
            last.then_inc(multiplied, 1)

        @block.scalar
        def _(act):
            act.wait_ge(exped, 1)
            nc.scalar.activation(score, score, ACT.Exp).then_inc(exped, 1)

        @block.vector
        def _(dve):
            step = Steps(dve, dve_step)
            norm, inv = tiny[:, 0:HP], tiny[:, HP:2 * HP]
            step(nc.vector.tensor_copy(norm, m.banks[NORM][:, 0:HP]))
            step(nc.vector.tensor_scalar(inv, norm, 1e-5, None, ALU.add))
            step(nc.vector.reciprocal(inv, inv))
            for j in range(HP):
                nc.vector.tensor_tensor(mixed[:, j, D:D + 1], norm[:, j:j + 1], inv[:, j:j + 1], ALU.mult)
                last = nc.vector.tensor_scalar(mixed[:, j, 0:D], m.banks[MIXED[j // 2]][:, (j % 2) * D:(j % 2 + 1) * D],
                                               inv[:, j:j + 1], None, ALU.mult)
            last.then_inc(taken, 1)
            dve.wait_ge(multiplied, 1)
            for k in range(KD):
                nc.vector.tensor_copy(mixed_t[:, k, :], m.banks[k][:, :])
            nc.vector.tensor_copy(share[0:1, :], m.banks[2][0:1, :]).then_inc(taken, 1)
            dve.wait_ge(multiplied, 2)
            nc.vector.tensor_copy(diagonal(tok, 0), diagonal(m.banks[3][:, :], 0))
            nc.vector.tensor_copy(diagonal(tok, 1), diagonal(m.banks[3][:, :], 1)).then_inc(taken, 1)
            dve.wait_ge(multiplied, 3)
            nc.vector.tensor_copy(q_t, m.banks[4][:, :])
            nc.vector.tensor_copy(k_t, m.banks[5][:, :])
            nc.vector.tensor_copy(v_s, m.banks[6][:, :]).then_inc(taken, 1)
            dve.wait_ge(multiplied, 4)
            for b in range(2):
                last = nc.vector.tensor_scalar(score[b * G:(b + 1) * G, :, :], diagonal(m.banks[7][:, :], b),
                                               float(G) ** -0.5, None, ALU.mult)
            step(last)
            step(nc.vector.tensor_reduce(tiny[:, 8:8 + HP], score, AX, ALU.max))
            nc.vector.tensor_tensor(score, score, repeat_last(tiny[:, 8:8 + HP], G), ALU.subtract).then_inc(exped, 1)
            dve.wait_ge(exped, 2)
            step(nc.vector.tensor_reduce(tiny[:, 12:12 + HP], score, AX, ALU.add))
            step(nc.vector.reciprocal(tiny[:, 12:12 + HP], tiny[:, 12:12 + HP]))
            for b in range(2):
                rows = slice(b * G, (b + 1) * G)
                last = nc.vector.tensor_tensor(diagonal(attn, b), score[rows, :, :],
                                               repeat_last(tiny[rows, 12:12 + HP], G), ALU.mult)
            last.then_inc(taken, 1)
            dve.wait_ge(multiplied, 5)
            nc.vector.tensor_copy(attn_t, m.banks[0][:, :]).then_inc(taken, 1)
            dve.wait_ge(multiplied, 6)
            nc.vector.tensor_copy(out_t, m.banks[1][:, :]).then_inc(taken, 1)
            dve.wait_ge(multiplied, 7)
            for b in range(2):
                nc.vector.tensor_copy(mo[:, 2 * b:2 * b + 2, :],
                                      m.banks[2 + b][:, :].rearrange("p (j n) -> p j n", j=2))

    with phase(m, "multiplied", "taken") as (block, multiplied, taken):

        @block.tensor
        def _(pe):
            with pe.Fori(0, NCH // 2) as i:
                for u in range(2):
                    pe.wait_ge(taken, i * 2 + u + 1)
                    for f in range(KD):
                        for j in range(HP):
                            last = nc.tensor.matmul(m.banks[2 * u + f][:, 0:CH], mo[:, j, f * P:(f + 1) * P],
                                                    wT[:, j, tile_at(i, u, CH, 2)], start=j == 0, stop=j == HP - 1)
                    last.then_inc(multiplied, 1)

        @block.vector
        def _(dve):
            dve.sem_inc(taken, 2)
            with dve.Fori(0, NCH // 2) as i:
                for u in range(2):
                    cols = tile_at(i, u, CH, 2)
                    dve.wait_ge(multiplied, i * 2 + u + 1)
                    for f in range(KD):
                        last = nc.vector.scalar_tensor_tensor(m.xT[:, f, cols], m.banks[2 * u + f][:, 0:CH],
                                                              m.vec("L0_ffn_b_out", f), m.xT[:, f, cols],
                                                              ALU.add, ALU.add)
                    last.then_inc(taken, 1)


def gcn(m):
    nc, ins = m.nc, m.ins
    w = m.part(m.REG, KD, D)
    inv_root = degree_row(m)
    scaled = m.part(m.REG + 512, 2, KD, CH)
    with phase(m) as (block,):

        @block.vector
        def _(dve):
            for k in range(KD):
                nc.vector.tensor_tensor(m.yT[:, k, :], m.yT[:, k, :], inv_root, ALU.mult)

    for layer in (1, 2, 3):
        neighbour_sums(m, with_self=True)
        b = f"L1_gnn_b{layer}"
        with phase(m, "loaded", "multiplied", "taken", "scaled_back", "gelu_done") as \
                (block, loaded, multiplied, taken, scaled_back, gelu_done):

            @block.sync
            def _(sp):
                sp.dma_start(w, ins[f"L1_gnn_W{layer}"].rearrange("(k p) o -> p k o", p=P)).then_inc(loaded, 16)

            @block.tensor
            def _(pe):
                pe.wait_ge(loaded, 16)
                with pe.Fori(0, NCH // 2) as i:
                    for u in range(2):
                        pe.wait_ge(taken, i * 2 + u + 1)
                        for f in range(KD):
                            for k in range(KD):
                                last = nc.tensor.matmul(m.banks[2 * u + f][:, 0:CH], w[:, k, f * P:(f + 1) * P],
                                                        m.sums[:, k, tile_at(i, u, CH, 2)], start=k == 0,
                                                        stop=k == KD - 1)
                        last.then_inc(multiplied, 1)

            @block.vector
            def _(dve):
                dve.sem_inc(taken, 2)
                with dve.Fori(0, NCH // 2) as i:
                    for u in range(2):
                        cols = tile_at(i, u, CH, 2)
                        dve.wait_ge(multiplied, i * 2 + u + 1)
                        if layer < 3:
                            dve.wait_ge(gelu_done, i * 2 + u + 1)
                        for f in range(KD):
                            last = nc.vector.tensor_tensor(scaled[:, u, f, :], m.banks[2 * u + f][:, 0:CH],
                                                           inv_root[:, cols], ALU.mult)
                        last.then_inc(taken, 1)
                        if layer == 3:
                            dve.wait_ge(taken, i * 2 + u + 1 + 2)
                            for f in range(KD):
                                nc.vector.scalar_tensor_tensor(m.xT[:, f, cols], scaled[:, u, f, :], m.vec(b, f),
                                                               m.xT[:, f, cols], ALU.add, ALU.add)
                    if layer < 3:
                        for u in range(2):
                            cols = tile_at(i, u, CH, 2)
                            dve.wait_ge(gelu_done, i * 2 + u + 1 + 2)
                            for f in range(KD):
                                nc.vector.tensor_tensor(m.yT[:, f, cols], m.yT[:, f, cols], inv_root[:, cols], ALU.mult)

            @block.scalar
            def _(act):
                if layer < 3:
                    act.sem_inc(gelu_done, 2)
                    with act.Fori(0, NCH // 2) as i:
                        for u in range(2):
                            act.wait_ge(taken, i * 2 + u + 1 + 2)
                            for f in range(KD):
                                last = nc.scalar.activation(m.yT[:, f, tile_at(i, u, CH, 2)], scaled[:, u, f, :],
                                                            ACT.Gelu_apprx_tanh, bias=m.vec(b, f))
                            last.then_inc(gelu_done, 1)


def gates(m, w_r, b_r, top_two):
    nc, ins = m.nc, m.ins
    gate = m.part(0, NP)[0:NE, :]
    logit = m.part(NP, NP)[0:NE, :]
    stage = m.part(2 * NP, TU, TP)
    at = [2 * NP + TU * TP]

    def rows(*shape):
        v = m.part(at[0], *shape)[0:TP]
        at[0] += int(np.prod(shape))
        return v

    L, W, S1, S2, T, O = (rows(NT, NE) for _ in range(6))
    a, b, c = rows(NT), rows(NT), rows(NT)
    order = rows(NE)
    wr = m.small[:, 0:KD * NE].rearrange("p (k e) -> p k e", k=KD)
    br = m.small[0:NE, KD * NE:KD * NE + 1]
    with phase(m, "loaded", "ordered", "multiplied", "logits_taken") as (block, loaded, ordered, multiplied, logits_taken):

        @block.sync
        def _(sp):
            sp.dma_start(wr, ins[w_r].rearrange("(k p) e -> p k e", p=P)).then_inc(loaded, 16)
            sp.dma_start(br, ins[b_r]).then_inc(loaded, 16)

        @block.gpsimd
        def _(pool):
            order_i = rows(NE).bitcast(I32)
            nc.gpsimd.memset(gate[:, N:NP], 0.0)
            nc.gpsimd.iota(order_i, [[-1, NE]], base=NE, channel_multiplier=0).then_inc(ordered, 1)
            pool.wait_ge(ordered, 1)
            nc.gpsimd.tensor_copy(order, order_i)

        @block.tensor
        def _(pe):
            pe.wait_ge(loaded, 32)
            with pe.Fori(0, NCH // 2) as i:
                for u in range(2):
                    pe.wait_ge(logits_taken, i * 2 + u + 1)
                    for k in range(KD):
                        last = nc.tensor.matmul(m.banks[u][0:NE, 0:CH], wr[:, k, :], m.yT[:, k, tile_at(i, u, CH, 2)],
                                                start=k == 0, stop=k == KD - 1)
                    last.then_inc(multiplied, 1)

        @block.vector
        def _(dve):
            dve.wait_ge(loaded, 32)
            dve.sem_inc(logits_taken, 2)
            with dve.Fori(0, NCH // 2) as i:
                for u in range(2):
                    dve.wait_ge(multiplied, i * 2 + u + 1)
                    nc.vector.tensor_scalar(logit[:, tile_at(i, u, CH, 2)], m.banks[u][0:NE, 0:CH], br, None,
                                            ALU.add).then_inc(logits_taken, 1)

    def turn(of, to, back):
        with phase(m, "staged", "transposed", "taken", "bank_claimed") as (block, staged, transposed, taken, bank_claimed):

            @block.scalar
            def _(act):
                with act.Fori(0, NT // TU) as i:
                    for u in range(TU):
                        act.wait_ge(transposed, i * TU + u + 1)
                        if back:
                            nc.scalar.copy(stage[0:TP, u, 0:NE], of[:, ds(i * TU + u, 1), :]
                                           .rearrange("p a e -> p (a e)")).then_inc(staged, 1)
                        else:
                            nc.scalar.copy(stage[0:NE, u, :], of[:, tile_at(i, u, TP, TU)]).then_inc(staged, 1)

            @block.tensor
            def _(pe):
                pe.sem_inc(transposed, TU)
                with pe.Fori(0, NT // TU) as i:
                    for u in range(TU):
                        pe.wait_ge(staged, i * TU + u + 1)
                        pe.wait_ge(taken, i * TU + u + 1)
                        pe.sem_inc(bank_claimed, 1)
                        if back:
                            last = nc.tensor.transpose(m.banks[u][0:NE, 0:TP], stage[0:TP, u, 0:NE], m.ident[0:TP, 0:TP])
                        else:
                            last = nc.tensor.transpose(m.banks[u][0:TP, 0:NE], stage[0:NE, u, :], m.ident[0:NE, 0:NE])
                        last.then_inc(transposed, 1)

            @block.vector
            def _(dve):
                dve.sem_inc(taken, TU)
                with dve.Fori(0, NT // TU) as i:
                    for u in range(TU):
                        dve.wait_ge(transposed, i * TU + u + 1 + TU)
                        if back:
                            nc.vector.tensor_copy(to[:, tile_at(i, u, TP, TU)], m.banks[u][0:NE, 0:TP]).then_inc(taken, 1)
                        else:
                            nc.vector.tensor_copy(to[:, ds(i * TU + u, 1), :].rearrange("p a e -> p (a e)"),
                                                  m.banks[u][0:TP, 0:NE]).then_inc(taken, 1)

    turn(logit, L, False)

    with phase(m, "dve_step", "centred", "exped") as (block, dve_step, centred, exped):

        @block.scalar
        def _(act):
            act.wait_ge(centred, 1)
            v = b if top_two else W
            nc.scalar.activation(v, v, ACT.Exp).then_inc(exped, 1)

        @block.vector
        def _(dve):
            step = Steps(dve, dve_step)
            tt, wide = nc.vector.tensor_tensor, lambda v: repeat_last(v, NE)

            def first_largest(of, largest, mask):
                step(nc.vector.tensor_reduce(largest, of, AX, ALU.max))
                step(tt(T, of, wide(largest), ALU.is_equal))
                step(tt(T, T, repeat_first(order, NT), ALU.mult))
                step(nc.vector.tensor_reduce(c, T, AX, ALU.max))
                step(tt(mask, T, wide(c), ALU.is_equal))

            if top_two:
                first_largest(L, a, S1)
                step(nc.vector.scalar_tensor_tensor(O, S1, -1e30, L, ALU.mult, ALU.add))
                first_largest(O, b, S2)
                nc.vector.tensor_tensor(b, b, a, ALU.subtract).then_inc(centred, 1)
                dve.wait_ge(exped, 1)
                step(nc.vector.tensor_scalar(a, b, 1.0, None, ALU.add))
                step(nc.vector.reciprocal(a, a))
                step(tt(b, a, b, ALU.mult))
                step(tt(W, S1, wide(a), ALU.mult))
                step(tt(O, S2, wide(b), ALU.mult))
                step(tt(W, W, O, ALU.add))
            else:
                step(nc.vector.tensor_reduce(a, L, AX, ALU.max))
                tt(W, L, wide(a), ALU.subtract).then_inc(centred, 1)
                dve.wait_ge(exped, 1)
                step(nc.vector.tensor_reduce(b, W, AX, ALU.add))
                step(nc.vector.reciprocal(b, b))
                step(tt(W, W, wide(b), ALU.mult))

    turn(W, gate, True)

    with phase(m, "stored") as (block, stored):

        @block.sync
        def _(sp):
            sp.dma_start(m.gate_rows, gate).then_inc(stored, 16)
            sp.wait_ge(stored, 16)


class Layer:

    def __init__(self, name, inputs, outputs):
        self.name, self.K, self.H = name, inputs // P, outputs // P
        self.words = self.K * outputs


def experts_room(layers):
    return dict(words=KD * CH + sum(l.words for l in layers), split=PARTS * (KD * NP + 2 * sum(l.words for l in layers)
                                                  + 2 * CH * sum(l.H for l in layers[:-1])))


def experts(m, layers, activate, per_feature, out_bias):
    nc, ins = m.nc, m.ins
    L = len(layers)
    ITEMS = 2 * NCH
    last_h = layers[-1].H
    words = sum(l.words for l in layers)
    at = [0]

    def parts(*shape):
        v = m.split[:, at[0]:at[0] + int(np.prod(shape))]
        at[0] += int(np.prod(shape))
        names = "abcd"[:len(shape)]
        return v.rearrange(f"p ({' '.join(names)}) -> p {' '.join(names)}", **dict(zip(names, shape)))

    y = parts(PARTS, KD, NP)
    w = parts(2, PARTS, words)
    hidden = [parts(2, PARTS, l.H * CH) for l in layers[:-1]]
    weighed = m.part(0, KD, CH)
    raw = m.part(KD * CH, words)
    free, used = m.yT.rearrange("p k n -> p (k n)"), [0]

    def reuse(n):
        used[0] += n
        return free[:, used[0] - n:used[0]]

    whole = [reuse(l.H * CH) for l in layers[:-1]]
    gate = reuse(2 * CH).rearrange("p (u n) -> p u n", u=2)
    scalars = [[m.small[:, 128 + (s * 2 + j) * 16:][:, 0:2 * l.H] for j in range(len(per_feature[s]))]
               for s, l in enumerate(layers[:-1])]
    staged_per_turn = sum(len(v) for v in scalars)
    banks, first_bank = [], 0
    for l in layers[:-1]:
        banks.append([[m.banks[first_bank + h] for h in range(l.H)]] * 2)
        first_bank += l.H
    banks.append([[m.banks[first_bank + last_h * b + h] for h in range(last_h)] for b in range(2)])
    ready_before = [2 * l.H for l in layers[:-1]] + [ITEMS]

    def steps():
        for step in range(ITEMS + L - 1):
            for s in range(L):
                if 0 <= step - s < ITEMS:
                    yield s, step - s

    def flat(l, v):
        return v.rearrange("p (h n) -> p h n", h=l.H)

    names = [f"{n}{s}" for n in ("product_ready", "activated", "high_ready", "low_ready") for s in range(L)]
    with phase(m, *names, "y_high", "y_low", "scalars_staged", "out_taken", "weighed_ready", "raw_loaded", "raw_used", "raw_high", "weights_ready",
               "weights_claimed", "gate_loaded0", "gate_loaded1") as (block, *sems):
        ready, activated, high, low = (sems[j * L:(j + 1) * L] for j in range(4))
        (y_high, y_low, scalars_staged, out_taken, weighed_ready, raw_loaded, raw_used, raw_high, weights_ready, weights_claimed,
         *gate_loaded) = sems[4 * L:]

        @block.sync
        def _(sp):
            def load_weights(e):
                to = 0
                for l in layers:
                    sp.dma_start(raw[:, to:to + l.words].rearrange("p (k o) -> p k o", k=l.K),
                                 ins[l.name][ds(e, 1)].rearrange("e (k p) o -> p (e k) o", p=P)).then_inc(raw_loaded, 16)
                    to += l.words

            def turn(i, last):
                for u in range(2):
                    for c in range(NCH):
                        sp.wait_ge(out_taken, i * ITEMS + u * NCH + c + 1)
                        sp.dma_start(gate[:, c % 2, :], m.gate_rows[ds(i * 2 + u, 1), c * CH:(c + 1) * CH]
                                     .rearrange("e n -> (e n)").partition_broadcast(P)).then_inc(gate_loaded[c % 2], 16)
                        if c == 2 and not (last and u):
                            sp.wait_ge(raw_used, i * 2 + u + 1)
                            load_weights(i * 2 + u + 1)

            load_weights(0)
            sp.wait_ge(y_low, KD)
            with sp.Fori(0, NE // 2 - 1) as i:
                turn(i, False)
            turn(NE // 2 - 1, True)

        @block.gpsimd
        def _(pool):
            with pool.Fori(0, NE // 2) as i:
                for u in range(2):
                    pool.wait_ge(raw_loaded, (i * 2 + u + 1) * (16 * L))
                    pool.wait_ge(ready[-1], i * ITEMS + u * NCH + NCH)
                    pool.sem_inc(weights_claimed, 1)
                    nc.gpsimd.tensor_copy(w[:, u, 0, :], raw).then_inc(raw_high, 1)
                    pool.wait_ge(raw_high, i * 2 + u + 1)
                    pool.sem_inc(weights_claimed, 1)
                    nc.gpsimd.tensor_tensor(w[:, u, 1, :], raw, w[:, u, 0, :].bitcast(F32), ALU.subtract)\
                        .then_inc(weights_ready, 1)
                    pool.wait_ge(weights_ready, i * 2 + u + 1)
                    pool.sem_inc(raw_used, 1)

        @block.tensor
        def _(pe):
            for s in range(L):
                pe.sem_inc(ready[s], ready_before[s])
            pe.wait_ge(y_low, KD)
            with pe.Fori(0, NE // 2) as i:
                for s, n in steps():
                    l, u, c, g = layers[s], n // NCH, n % NCH, i * ITEMS + n
                    if s == 0 and c == 0:
                        pe.wait_ge(weights_ready, i * 2 + u + 1)
                    if s:
                        pe.wait_ge(low[s - 1], g + 1 + 1)
                    if s == L - 1:
                        pe.wait_ge(out_taken, g + 1)
                    base = sum(x.words for x in layers[:s])
                    for h in range(l.H):
                        if s < L - 1:
                            pe.wait_ge(activated[s], g * l.H + h + 1)
                        for j, (wp, xp) in enumerate(((0, 0), (0, 1), (1, 0))):
                            for k in range(l.K):
                                wk = base + k * l.H * P + h * P
                                x = y[:, xp, k, c * CH:(c + 1) * CH] if s == 0 else \
                                    hidden[s - 1][:, n % 2, xp, k * CH:(k + 1) * CH]
                                last = nc.tensor.matmul(banks[s][n % 2][h][:, 0:CH], w[:, u, wp, wk:wk + P], x,
                                                        start=j == 0 and k == 0, stop=j == 2 and k == l.K - 1)
                        if s < L - 1:
                            last.then_inc(ready[s], 1)
                    if s == L - 1:
                        last.then_inc(ready[s], 1)

        @block.scalar
        def _(act):
            for s in range(L - 1):
                act.sem_inc(activated[s], layers[s].H)
            for k in range(KD):
                nc.scalar.copy(y[:, 0, k, :], m.yT[:, k, :]).then_inc(y_high, 1)
            act.wait_ge(y_low, KD)
            with act.Fori(0, NE // 2) as i:
                for s, l in enumerate(layers[:-1]):
                    act.wait_ge(activated[s], i * (ITEMS * l.H) + l.H)
                    for to, of in zip(scalars[s], per_feature[s]):
                        nc.scalar.copy(to, of[:, ds(i * (2 * l.H), 2 * l.H)]).then_inc(scalars_staged, 1)
                act.wait_ge(scalars_staged, i * staged_per_turn + staged_per_turn)
                for s, n in steps():
                    if s == L - 1:
                        continue
                    l, u, g = layers[s], n // NCH, i * ITEMS + n
                    act.wait_ge(low[s], g + 1)
                    for h in range(l.H):
                        act.wait_ge(ready[s], g * l.H + h + 1 + ready_before[s])
                        activate(flat(l, whole[s])[:, h, :], banks[s][n % 2][h][:, 0:CH],
                                 [v[:, u * l.H + h:u * l.H + h + 1] for v in scalars[s]]).then_inc(activated[s], 1)
                    act.wait_ge(activated[s], g * l.H + 2 * l.H)
                    per = 1 if s + 1 == L - 1 else layers[s + 1].H
                    act.wait_ge(ready[s + 1], g * per + ready_before[s + 1] - per)
                    nc.scalar.copy(hidden[s][:, n % 2, 0, :], whole[s]).then_inc(high[s], 1)

        @block.vector
        def _(dve):
            for s in range(L - 1):
                dve.sem_inc(low[s], 1)
            dve.sem_inc(out_taken, 2)
            for k in range(KD):
                dve.wait_ge(y_high, k + 1)
                nc.vector.tensor_tensor(y[:, 1, k, :], m.yT[:, k, :], y[:, 0, k, :].bitcast(F32), ALU.subtract)\
                    .then_inc(y_low, 1)
            with dve.Fori(0, NE // 2) as i:
                for s, n in steps():
                    u, c, g = n // NCH, n % NCH, i * ITEMS + n
                    if s < L - 1:
                        dve.wait_ge(high[s], g + 1)
                        nc.vector.tensor_tensor(hidden[s][:, n % 2, 1, :], whole[s],
                                                hidden[s][:, n % 2, 0, :].bitcast(F32), ALU.subtract).then_inc(low[s], 1)
                        continue
                    cols = slice(c * CH, (c + 1) * CH)
                    dve.wait_ge(ready[s], g + 1 + ready_before[s])
                    dve.wait_ge(gate_loaded[c % 2], (i * NCH + n // 2 + 1) * 16)
                    dve.wait_ge(out_taken, g + 2)
                    for f in range(KD):
                        last = nc.vector.scalar_tensor_tensor(
                            weighed[:, f, :], banks[s][n % 2][f][:, 0:CH],
                            m.vec(out_bias)[:, ds(i * (2 * KD) + u * KD + f, 1)], gate[:, c % 2, :], ALU.add, ALU.mult)
                    last.then_inc(weighed_ready, 1)
                    dve.wait_ge(weighed_ready, g + 1)
                    nc.vector.tensor_tensor(m.xT[:, :, cols], m.xT[:, :, cols], weighed, ALU.add).then_inc(out_taken, 1)


TOP_TWO = (Layer("L1_ffn_W1", D, H1), Layer("L1_ffn_W2", H1, D))
DEEP = (Layer("L3_ffn_W1", D, D), Layer("L3_ffn_W2", D, D), Layer("L3_ffn_Wo", D, D))


def experts_top_two(m):

    def gelu(to, of, scalars):
        return m.nc.scalar.activation(to, of, ACT.Gelu, bias=scalars[0])

    experts(m, TOP_TWO, gelu, [[m.vec("L1_ffn_b1")]], "L1_ffn_b2")


def directional(m):
    nc, ins = m.nc, m.ins
    store_rows(m, m.yT, m.table)
    with if_general(m):
        general_sums(m, weighted=True)
    with branch(m, nc.Else()):
        weighted_sums(m)
    sums = m.sums
    wsum = m.part(6 * AW, 2, AW)
    w1 = m.part(8 * AW, 2 * KD, D)
    w2 = m.part(8 * AW + 2 * KD * D, 4 * KD, D)
    own = m.gathered[:, 0:4, :].rearrange("p a b -> p (a b)")[:, 0:KD * CH].rearrange("p (f n) -> p f n", f=KD)
    snorm = m.gathered[:, 4:8, :].rearrange("p a b -> p (a b)")[:, 0:2 * CH].rearrange("p (u n) -> p u n", u=2)
    inv = m.onehot[:, 0:3 * CH].rearrange("p (w n) -> p w n", w=3)
    OWN = (6, 7)
    with phase(m, "loaded", "snorm_loaded0", "snorm_loaded1", "edge_products", "own_taken", "joined", "absolute", "multiplied", "out_taken",
               "dve_step", "pool_claimed", "pool_weighed") as \
            (block, loaded, snorm_loaded0, snorm_loaded1, edge_products, own_taken, joined, absolute, multiplied, out_taken,
             dve_step, pool_claimed, pool_weighed):

        @block.gpsimd
        def _(pool):
            with pool.Fori(0, NCH) as c:
                cols = ds(c * CH, CH)
                pool.wait_ge(own_taken, c + 1)
                pool.sem_inc(pool_claimed, 1)
                for w, total in enumerate((m.degree[:, cols], wsum[:, 0, cols], wsum[:, 1, cols])):
                    last = nc.gpsimd.tensor_tensor(sums[:, 2 * w + 1, cols], own[:, 1, :], total, ALU.mult)
                last.then_inc(pool_weighed, 1)

        @block.sync
        def _(sp):
            sp.dma_start(w1, ins["L2_gnn_W1"].rearrange("(k p) o -> p k o", p=P)).then_inc(loaded, 16)
            sp.dma_start(w2, ins["L2_gnn_W2"].rearrange("(k p) o -> p k o", p=P)).then_inc(loaded, 16)
            with sp.Fori(0, NCH // 2) as i:
                for u in range(2):
                    sp.wait_ge(out_taken, i * 2 + u + 1)
                    sp.dma_start(snorm[:, u, :], ins["snorm"][ds(i * 2 * CH + u * CH, CH)].partition_broadcast(P))\
                        .then_inc((snorm_loaded0, snorm_loaded1)[u], 16)

        @block.tensor
        def _(pe):
            pe.wait_ge(loaded, 32)
            with pe.Fori(0, NCH) as c:
                cols = ds(c * CH, CH)
                pe.wait_ge(joined, c + 1)
                for w in range(3):
                    for f in range(KD):
                        for k in range(KD):
                            nc.tensor.matmul(m.banks[2 * w + f][:, 0:CH], w1[:, k, f * P:(f + 1) * P],
                                             sums[:, 2 * w + k, cols], start=k == 0, stop=k == KD - 1)
                pe.wait_ge(out_taken, c + 2)
                for f in range(KD):
                    for k in range(KD):
                        last = nc.tensor.matmul(m.banks[OWN[f]][:, 0:CH], w1[:, KD + k, f * P:(f + 1) * P],
                                                m.yT[:, k, cols], start=k == 0, stop=k == KD - 1)
                last.then_inc(edge_products, 1)
                pe.wait_ge(own_taken, c + 1)

                def join(blocks):
                    for f in range(KD):
                        for k in blocks:
                            rhs = m.yT[:, k, cols] if k < KD else sums[:, k - KD, cols]
                            last = nc.tensor.matmul(m.banks[OWN[f]][:, 0:CH], w2[:, k, f * P:(f + 1) * P], rhs,
                                                    start=k == 0, stop=k == 4 * KD - 1, skip_group_check=True)
                    return last

                join(range(KD))
                pe.wait_ge(absolute, c + 1)
                join(range(KD, 4 * KD)).then_inc(multiplied, 1)

        @block.scalar
        def _(act):
            with act.Fori(0, NCH) as c:
                cols = ds(c * CH, CH)
                act.wait_ge(edge_products, c + 1)
                act.wait_ge(joined, c + 1)
                for f in range(KD):
                    last = nc.scalar.activation(own[:, f, :], m.banks[OWN[f]][:, 0:CH], ACT.Identity,
                                                bias=m.vec("L2_gnn_b1", f))
                last.then_inc(own_taken, 1)
                act.wait_ge(joined, c + 2)
                for f in range(KD):
                    v = sums[:, 4 + f, cols]
                    last = nc.scalar.activation(v, v, ACT.Abs)
                last.then_inc(absolute, 1)

        @block.vector
        def _(dve):
            PER = 6
            dve.sem_inc(out_taken, 2)
            dve.sem_inc(joined, 1)
            with dve.Fori(0, NCH // 2) as i:
                for u in range(2):
                    c = i * 2 + u
                    cols = ds(i * 2 * CH + u * CH, CH)
                    n = [0]

                    def step(ins_):
                        ins_.then_inc(dve_step, 1)
                        n[0] += 1
                        dve.wait_ge(dve_step, c * PER + n[0])

                    totals = (m.degree[:, cols], wsum[:, 0, cols], wsum[:, 1, cols])
                    nc.vector.tensor_scalar(inv[:, 0, :], totals[0], 1.0, None, ALU.max)
                    step(nc.vector.tensor_scalar(inv[:, 1, :], totals[1], 1e-8, None, ALU.add))
                    step(nc.vector.reciprocal(inv[:, 0:2, :], inv[:, 0:2, :]))
                    dve.wait_ge(own_taken, c + 1)
                    for w in range(3):
                        last = nc.vector.tensor_tensor(sums[:, 2 * w, cols], own[:, 0, :], totals[w], ALU.mult)
                    step(last)
                    for f in range(KD):
                        if f:
                            dve.wait_ge(pool_weighed, c + 1)
                        for w in range(3):
                            v = sums[:, 2 * w + f, cols]
                            last = nc.vector.tensor_tensor(v, v, m.banks[2 * w + f][:, 0:CH], ALU.add)
                    step(last)
                    for f in range(KD):
                        for w in range(3):
                            v = sums[:, 2 * w + f, cols]
                            last = nc.vector.tensor_tensor(v, v, inv[:, min(w, 1), :], ALU.mult)
                    step(last)
                    for f in range(KD):
                        v = sums[:, 4 + f, cols]
                        last = nc.vector.tensor_tensor(v, v, m.yT[:, f, cols], ALU.subtract)
                    last.then_inc(joined, 1)
                    dve.wait_ge(multiplied, c + 1)
                    for f in range(KD):
                        last = nc.vector.tensor_scalar(sums[:, f, cols], m.banks[OWN[f]][:, 0:CH], m.vec("L2_gnn_b2", f),
                                                       None, ALU.add)
                    step(last)
                    dve.wait_ge((snorm_loaded0, snorm_loaded1)[u], i * 16 + 16)
                    for f in range(KD):
                        last = nc.vector.tensor_tensor(sums[:, f, cols], sums[:, f, cols], snorm[:, u, :], ALU.mult)
                    last.then_inc(out_taken, 1)
                    assert n[0] == PER

    stat = m.small
    sq = m.part(2 * AW, KD, NP)
    with phase(m, "centred", "squared", "rooted", "scaled_ready", "relu_done", "dve_step") as \
            (block, centred, squared, rooted, scaled_ready, relu_done, dve_step):

        @block.scalar
        def _(act):
            act.wait_ge(centred, 1)
            for f in range(KD):
                last = nc.scalar.activation(sq[:, f, 0:N], sums[:, f, 0:N], ACT.Square, accum_out=stat[:, 4 + f:5 + f])
            last.then_inc(squared, 1)
            act.wait_ge(scaled_ready, 1)
            nc.scalar.activation(stat[:, 4:6], stat[:, 4:6], ACT.Sqrt, bias=m.eps[:, 0:1]).then_inc(rooted, 1)
            act.wait_ge(scaled_ready, 2)
            for f in range(KD):
                nc.scalar.activation(sums[:, f, 0:NP], sums[:, f, 0:NP], ACT.Relu, bias=m.vec("L2_gnn_beta", f),
                                     scale=stat[:, 6 + f:7 + f]).then_inc(relu_done, 1)

        @block.vector
        def _(dve):
            step = Steps(dve, dve_step)
            for f in range(KD):
                last = nc.vector.tensor_reduce(stat[:, f:f + 1], sums[:, f, 0:N], AX, ALU.add)
            step(last)
            step(nc.vector.tensor_scalar(stat[:, 0:2], stat[:, 0:2], 1.0 / N, None, ALU.mult))
            for f in range(KD):
                last = nc.vector.tensor_scalar(sums[:, f, 0:NP], sums[:, f, 0:NP], stat[:, f:f + 1], None, ALU.subtract)
            last.then_inc(centred, 1)
            dve.wait_ge(squared, 1)
            nc.vector.tensor_scalar(stat[:, 4:6], stat[:, 4:6], 1.0 / N, None, ALU.mult).then_inc(scaled_ready, 1)
            dve.wait_ge(rooted, 1)
            step(nc.vector.reciprocal(stat[:, 4:6], stat[:, 4:6]))
            nc.vector.tensor_tensor(stat[:, 6:8], stat[:, 4:6], m.vec("L2_gnn_gamma"), ALU.mult).then_inc(scaled_ready, 1)
            for f in range(KD):
                step(nc.vector.tensor_tensor(m.xT[:, f, :], m.xT[:, f, :], m.yT[:, f, :], ALU.add))
                dve.wait_ge(relu_done, f + 1)
                nc.vector.tensor_tensor(m.xT[:, f, 0:N], m.xT[:, f, 0:N], sums[:, f, 0:N], ALU.add)


def experts_for_all(m):
    nc, ins = m.nc, m.ins
    HT = H1 // P
    CAP = float(ceil(N * 1.25 / NE))
    w1 = m.part(0, 2, KD * H1).rearrange("p e (k h) -> p e k h", k=KD)
    w2 = m.part(2048, 2, HT * D).rearrange("p e (h o) -> p e h o", h=HT)
    wr = m.part(4096, KD, NE)
    b1 = m.part(4112, 2, HT)
    b2 = m.part(4120, 2, KD)
    bias = m.part(4124, KD)
    hidden = m.part(4200, 2, HT, CH)
    words = KD * H1
    w_parts = [m.split[:, l * 4 * words:(l + 1) * 4 * words].rearrange("p (e s n) -> p e s n", e=2, s=PARTS)
               for l in range(2)]
    at = 8 * words
    y_parts = m.split[:, at:at + 4 * KD * CH].rearrange("p (u s k n) -> p u s k n", u=2, s=PARTS, k=KD)
    at += 4 * KD * CH
    h_parts = m.split[:, at:at + 4 * HT * CH].rearrange("p (e s h n) -> p e s h n", e=2, s=PARTS, h=HT)
    mean = m.small[:, 0:KD]
    row = lambda j: m.small[0:1, 16 + NE * j:16 + NE * (j + 1)]
    br, logit, weight, scale, picked, masked, order, t8 = (row(j) for j in range(8))
    one = lambda j: m.small[0:1, 100 + j:101 + j]
    chosen = m.small[0:1, 120:122].bitcast(I32)
    order_i = m.small[0:1, 130:138].bitcast(I32)
    both = m.small[:, 140:142]
    with phase(m, "loaded", "ordered", "averaged", "multiplied", "centred", "exped", "dve_step", "chosen_ready",
               "w_loaded", "gates_ready", "gates_spread") as \
            (block, loaded, ordered, averaged, multiplied, centred, exped, dve_step, chosen_ready,
             w_loaded, gates_ready, gates_spread):

        @block.sync
        def _(sp):
            sp.dma_start(wr, ins["L2_ffn_Wr"].rearrange("(k p) e -> p k e", p=P)).then_inc(loaded, 16)
            sp.dma_start(br, ins["L2_ffn_br"]).then_inc(loaded, 16)
            for j in range(2):
                sp.wait_ge(chosen_ready, j + 1)
                e = sp.value_load(chosen[0:1, j:j + 1], min_val=0, max_val=NE - 1)
                one_of = lambda name: ins[name][ds(e, 1)]
                sp.dma_start(w1[:, j, :, :], one_of("L2_ffn_W1").rearrange("e (k p) h -> p (e k) h", p=P)).then_inc(w_loaded, 16)
                sp.dma_start(w2[:, j, :, :], one_of("L2_ffn_W2").rearrange("e (h p) o -> p (e h) o", p=P)).then_inc(w_loaded, 16)
                sp.dma_start(b1[:, j, :], one_of("L2_ffn_b1").rearrange("e p h -> p (e h)")).then_inc(w_loaded, 16)
                sp.dma_start(b2[:, j, :], one_of("L2_ffn_b2").rearrange("e p f -> p (e f)")).then_inc(w_loaded, 16)
            sp.wait_ge(w_loaded, 16 * 8)

        @block.gpsimd
        def _(pool):
            nc.gpsimd.iota(order_i, [[-1, NE]], base=NE, channel_multiplier=0).then_inc(ordered, 1)
            pool.wait_ge(ordered, 1)
            nc.gpsimd.tensor_copy(order, order_i).then_inc(ordered, 1)

        @block.tensor
        def _(pe):
            pe.wait_ge(loaded, 32)
            pe.wait_ge(averaged, 1)
            for k in range(KD):
                last = nc.tensor.matmul(m.banks[0][0:1, 0:NE], mean[:, k:k + 1], wr[:, k, :], start=k == 0,
                                        stop=k == KD - 1)
            last.then_inc(multiplied, 1)
            pe.wait_ge(gates_ready, 1)
            nc.tensor.matmul(m.banks[1][:, 0:2], m.ones[0:1, :], m.small[0:1, 108:110], start=True, stop=True)\
                .then_inc(gates_spread, 1)

        @block.scalar
        def _(act):
            for n, v in enumerate((weight, weight, one(3))):
                act.wait_ge(centred, n + 1)
                nc.scalar.activation(v, v, ACT.Exp).then_inc(exped, 1)

        @block.vector
        def _(dve):
            step = Steps(dve, dve_step)
            for k in range(KD):
                last = nc.vector.tensor_reduce(mean[:, k:k + 1], m.yT[:, k, 0:N], AX, ALU.add)
            step(last)
            nc.vector.tensor_scalar(mean, mean, 1.0 / N, None, ALU.mult).then_inc(averaged, 1)
            dve.wait_ge(multiplied, 1)
            step(nc.vector.tensor_tensor(logit, m.banks[0][0:1, 0:NE], br, ALU.add))

            def softmax(of, n):
                step(nc.vector.tensor_reduce(one(0), of, AX, ALU.max))
                nc.vector.tensor_scalar(weight, of, one(0), None, ALU.subtract).then_inc(centred, 1)
                dve.wait_ge(exped, n)
                step(nc.vector.tensor_reduce(one(1), weight, AX, ALU.add))
                step(nc.vector.reciprocal(one(1), one(1)))
                step(nc.vector.tensor_scalar(weight, weight, one(1), None, ALU.mult))

            softmax(logit, 1)
            step(nc.vector.tensor_scalar(scale, weight, float(N), 1e-30, ALU.mult, ALU.max))
            step(nc.vector.reciprocal(scale, scale))
            step(nc.vector.tensor_scalar(scale, scale, CAP, 1.0, ALU.mult, ALU.min))
            step(nc.vector.tensor_tensor(scale, scale, weight, ALU.mult))
            softmax(scale, 2)
            dve.wait_ge(ordered, 2)
            for j, of in enumerate((weight, masked)):
                step(nc.vector.tensor_reduce(one(4 + j), of, AX, ALU.max))
                step(nc.vector.tensor_scalar(t8, of, one(4 + j), None, ALU.is_equal))
                step(nc.vector.tensor_tensor(t8, t8, order, ALU.mult))
                step(nc.vector.tensor_reduce(one(6), t8, AX, ALU.max))
                step(nc.vector.tensor_scalar(picked, t8, one(6), None, ALU.is_equal))
                step(nc.vector.tensor_scalar(one(6), one(6), -1.0, float(NE), ALU.mult, ALU.add))
                nc.vector.tensor_copy(chosen[0:1, j:j + 1], one(6)).then_inc(chosen_ready, 1)
                if j == 0:
                    step(nc.vector.scalar_tensor_tensor(masked, picked, -1e30, weight, ALU.mult, ALU.add))
            nc.vector.tensor_tensor(one(3), one(5), one(4), ALU.subtract).then_inc(centred, 1)
            dve.wait_ge(exped, 3)
            step(nc.vector.tensor_scalar(one(2), one(3), 1.0, None, ALU.add))
            step(nc.vector.reciprocal(one(8), one(2)))
            nc.vector.tensor_tensor(one(9), one(8), one(3), ALU.mult).then_inc(gates_ready, 1)
            dve.wait_ge(gates_spread, 1)
            step(nc.vector.tensor_copy(both, m.banks[1][:, 0:2]))
            dve.wait_ge(w_loaded, 16 * 8)
            for j in range(2):
                g = both[:, j:j + 1]
                nc.vector.tensor_scalar(w2[:, j, :, :], w2[:, j, :, :], g, None, ALU.mult)
                last = nc.vector.tensor_scalar(b2[:, j, :], b2[:, j, :], g, None, ALU.mult)
            step(last)
            nc.vector.tensor_tensor(bias, b2[:, 0, :], b2[:, 1, :], ALU.add)

    OUT = (4, 5)
    products = ((0, 0), (0, 1), (1, 0))
    with phase(m, "w_high", "w_low", "y_high", "y_low", "hidden_ready", "gelu_done", "high_ready", "low_ready",
               "out_ready", "added") as \
            (block, w_high, w_low, y_high, y_low, hidden_ready, gelu_done, high_ready, low_ready, out_ready, added):

        @block.tensor
        def _(pe):
            pe.sem_inc(out_ready, 2)
            pe.wait_ge(w_low, 4)
            with pe.Fori(0, NCH // 2) as i:
                for v in range(2):

                    def up(e):
                        for h in range(HT):
                            pe.wait_ge(gelu_done, ((i * 2 + v) * 2 + e) * HT + h + 1)
                            for j, (wp, yp) in enumerate(products):
                                for k in range(KD):
                                    last = nc.tensor.matmul(
                                        m.banks[h][:, 0:CH], w_parts[0][:, e, wp, k * H1 + h * P:k * H1 + (h + 1) * P],
                                        y_parts[:, v, yp, k, :], start=j == 0 and k == 0, stop=j == 2 and k == KD - 1)
                            last.then_inc(hidden_ready, 1)

                    def down(e):
                        pe.wait_ge(low_ready, (i * 2 + v) * 2 + e + 1 + 2)
                        for f in range(KD):
                            for j, (wp, hp) in enumerate(products):
                                for h in range(HT):
                                    last = nc.tensor.matmul(
                                        m.banks[OUT[f]][:, 0:CH], w_parts[1][:, e, wp, h * D + f * P:h * D + (f + 1) * P],
                                        h_parts[:, e, hp, h, :], start=e == 0 and j == 0 and h == 0,
                                        stop=e == 1 and j == 2 and h == HT - 1, skip_group_check=True)
                        return last

                    pe.wait_ge(y_low, i * 2 + v + 1)
                    up(0)
                    up(1)
                    pe.wait_ge(added, i * 2 + v + 2)
                    down(0)
                    down(1).then_inc(out_ready, 1)

        @block.scalar
        def _(act):
            for l, w in enumerate((w1, w2)):
                for e in range(2):
                    nc.scalar.copy(w_parts[l][:, e, 0, :], w[:, e, :, :].rearrange("p a b -> p (a b)")).then_inc(w_high, 1)
            act.sem_inc(gelu_done, HT)
            with act.Fori(0, NCH // 2) as i:
                for v in range(2):
                    c = i * 2 + v
                    act.wait_ge(out_ready, c + 1)
                    nc.scalar.copy(y_parts[:, v, 0, :, :], m.yT[:, :, tile_at(i, v, CH, 2)]).then_inc(y_high, 1)
                    for e in range(2):
                        act.wait_ge(low_ready, c * 2 + e + 1)
                        for h in range(HT):
                            act.wait_ge(hidden_ready, (c * 2 + e) * HT + h + 1)
                            nc.scalar.activation(hidden[:, e, h, :], m.banks[h][:, 0:CH], ACT.Gelu,
                                                 bias=b1[:, e, h:h + 1]).then_inc(gelu_done, 1)
                        act.wait_ge(gelu_done, (c * 2 + e) * HT + 2 * HT)
                        nc.scalar.copy(h_parts[:, e, 0, :, :], hidden[:, e, :, :]).then_inc(high_ready, 1)

        @block.vector
        def _(dve):
            for l, w in enumerate((w1, w2)):
                for e in range(2):
                    dve.wait_ge(w_high, l * 2 + e + 1)
                    nc.vector.tensor_tensor(w_parts[l][:, e, 1, :], w[:, e, :, :].rearrange("p a b -> p (a b)"),
                                            w_parts[l][:, e, 0, :].bitcast(F32), ALU.subtract).then_inc(w_low, 1)
            dve.sem_inc(low_ready, 2)
            dve.sem_inc(added, 2)

            def split(i, n):
                c, v = i * 2 + n, n % 2
                dve.wait_ge(y_high, c + 1)
                nc.vector.tensor_tensor(y_parts[:, v, 1, :, :], m.yT[:, :, ds(i * (2 * CH) + n * CH, CH)],
                                        y_parts[:, v, 0, :, :].bitcast(F32), ALU.subtract).then_inc(y_low, 1)
                if n:
                    add(i, n - 1)
                for e in range(2):
                    dve.wait_ge(high_ready, c * 2 + e + 1)
                    nc.vector.tensor_tensor(h_parts[:, e, 1, :, :], hidden[:, e, :, :],
                                            h_parts[:, e, 0, :, :].bitcast(F32), ALU.subtract).then_inc(low_ready, 1)

            def add(i, n):
                c, cols = i * 2 + n, ds(i * (2 * CH) + n * CH, CH)
                dve.wait_ge(y_low, c + 1)
                dve.wait_ge(out_ready, c + 3)
                for f in range(KD):
                    last = nc.vector.scalar_tensor_tensor(m.yT[:, f, cols], m.banks[OUT[f]][:, 0:CH], bias[:, f:f + 1],
                                                          m.yT[:, f, cols], ALU.add, ALU.add)
                last.then_inc(added, 1)

            split(0, 0)
            with dve.Fori(0, NCH // 2 - 1) as i:
                split(i, 1)
                split(i, 2)
            split(NCH // 2 - 1, 1)
            add(NCH // 2 - 1, 1)

    layer_norm(m, m.yT, m.yT, "L2_ffn_gamma", "L2_ffn_beta", add_to=m.xT)


def experts_deep(m):
    nc = m.nc
    scale = m.small[:, 32:64].rearrange("p (l n) -> p l n", l=2)
    bias = m.small[:, 64:96].rearrange("p (l n) -> p l n", l=2)
    with phase(m, "rooted", "dve_step") as (block, rooted, dve_step):

        @block.scalar
        def _(act):
            for l, n in enumerate("12"):
                last = nc.scalar.activation(scale[:, l, :], m.vec("L3_ffn_v" + n), ACT.Sqrt, bias=m.eps[:, 1:2])
            last.then_inc(rooted, 1)

        @block.vector
        def _(dve):
            step = Steps(dve, dve_step)
            dve.wait_ge(rooted, 1)
            step(nc.vector.reciprocal(scale, scale))
            for l, n in enumerate("12"):
                nc.vector.tensor_tensor(bias[:, l, :], m.vec("L3_ffn_b" + n), m.vec("L3_ffn_m" + n), ALU.subtract)
                last = nc.vector.tensor_tensor(scale[:, l, :], scale[:, l, :], m.vec("L3_ffn_g" + n), ALU.mult)
            step(last)
            step(nc.vector.tensor_tensor(bias, bias, scale, ALU.mult))
            for l, n in enumerate("12"):
                nc.vector.tensor_tensor(bias[:, l, :], bias[:, l, :], m.vec("L3_ffn_be" + n), ALU.add)

    def norm_relu(to, of, scalars):
        return m.nc.scalar.activation(to, of, ACT.Relu, bias=scalars[0], scale=scalars[1])

    experts(m, DEEP, norm_relu, [[bias[:, s, :], scale[:, s, :]] for s in range(2)], "L3_ffn_bo")


def program(nc, ins, out, stop=8):
    with ExitStack() as stack:
        m = Machine(nc, stack, ins, out)
        with nc.sbuf_tensor("source_tiles", [P, 2, EG + 2 * AHEAD], F32) as tiles:
            lo, key = tiles[:, 0, :], tiles[:, 1, :]
            with m.room(10 * EG + KEYS):
                setup(m, lo, key)
            with nc.sbuf_tensor("counts_in_sbuf", [P, NT, AW], BF16) as counts, \
                    nc.sbuf_tensor("edge_one_hots", [P, 2 * AHEAD * (P + KEYS)], BF16) as hot:
                build_counts(m, counts, lo, key, hot)
        with m.room():
            with if_general(m):
                general_sums(m)
            invert_degrees(m)
        m.place_activations()
        with m.room():
            load_rows(m, ins["x"], m.xT)
        summing, other = dict(words=SUM_ROOM, split=SUM_SPLIT), {}
        sublayers = [
            [(summing, lambda: sage(m, "L0_gnn_W1_l", "L0_gnn_W1_r", "L0_gnn_b1", "L0_gnn_W2_l", "L0_gnn_W2_r",
                                    "L0_gnn_b2"))],
            [(other, lambda: slice_attention(m))],
            [(summing, lambda: gcn(m))],
            [(other, lambda: (layer_norm(m, m.yT, m.yT, "L1_ffn_gamma", "L1_ffn_beta"),
                              gates(m, "L1_ffn_Wr", "L1_ffn_br", top_two=True))),
             (experts_room(TOP_TWO), lambda: experts_top_two(m))],
            [(other, lambda: directional(m))],
            [(dict(words=8192, split=8 * KD * H1 + 4 * CH * (KD + H1 // P)), lambda: experts_for_all(m))],
            [(summing, lambda: sage(m, "L3_gnn_w1_l", "L3_gnn_w1_r", "L3_gnn_b1", "L3_gnn_w2_l", "L3_gnn_w2_r",
                                    "L3_gnn_b2"))],
            [(other, lambda: gates(m, "L3_ffn_Wr", "L3_ffn_br", top_two=False)),
             (experts_room(DEEP), lambda: experts_deep(m))],
        ]
        rows = {0: INVERSE, 2: INVERSE_ROOT, 6: INVERSE}
        for number, steps in enumerate(sublayers[:stop]):
            for j, (room, step) in enumerate(steps):
                with m.room(**room):
                    if j == 0:
                        layer_norm(m, m.xT, m.yT, row=rows.get(number))
                    step()
        with m.room():
            store_rows(m, m.xT, out)




def kernel(**inputs):
    import concourse.bacc as bacc
    from concourse.bass_utils import run_bass_kernel_spmd as run

    a = {k: np.asarray(v) for k, v in inputs.items()}

    def by_group(v, pad):
        full = np.full(P * EG, pad, v.dtype)
        full[:E] = v
        return np.ascontiguousarray(full.reshape(EG, P).T)

    ins = {
        "x": a["x"],
        "src": by_group(a["src"], 0),
        "dst": by_group(a["dst"], PAD_DST),
        "edge_w": by_group(a["edge_attr_2"][:, 0], 0),
        "snorm": np.pad(a["node_vec1"][:, 0], (0, NP - N)),
    }
    for name in ("w1_l", "w1_r", "w2_l", "w2_r"):
        ins[f"L3_gnn_{name}"] = a[f"L3_gnn_{name}"].T
    for name in ("L1_ffn_br", "L3_ffn_br"):
        ins[name] = a[name][:, None]
    ins["L2_ffn_br"] = a["L2_ffn_br"][None]
    for name in ("L2_ffn_b1", "L2_ffn_b2"):
        ins[name] = a[name].reshape(NE, -1, P).transpose(0, 2, 1)
    ins["L0_ffn_W_x_t"] = a["L0_ffn_W_x"].T
    ins["L0_ffn_b_fx"] = a["L0_ffn_b_fx"][None]
    ins["L0_ffn_b_slice"] = a["L0_ffn_b_slice"][None]
    ins["L0_ffn_temperature"] = a["L0_ffn_temperature"].reshape(HEADS)
    for name in ("L0_gnn_W1_l", "L0_gnn_W1_r", "L0_gnn_W2_l", "L0_gnn_W2_r", "L0_ffn_W_fx", "L0_ffn_W_out",
                 "L0_ffn_W_slice", "L0_ffn_W_q", "L0_ffn_W_k", "L0_ffn_W_v", "L1_gnn_W1", "L1_gnn_W2", "L1_gnn_W3",
                 "L1_ffn_Wr", "L1_ffn_W1", "L1_ffn_W2", "L2_gnn_W1", "L2_gnn_W2", "L2_ffn_Wr",
                 "L2_ffn_W1", "L2_ffn_W2", "L3_ffn_Wr", "L3_ffn_W1", "L3_ffn_W2", "L3_ffn_Wo"):
        ins[name] = a[name]
    ins["vecs"] = np.concatenate([a[n].reshape(-1, P).T for n in VECS], axis=1)
    nc = bacc.Bacc("TRN2", target_bir_lowering=False, num_devices=1)
    arrays, aps = {}, {}
    for name, v in ins.items():
        arrays[f"in_{name}"] = np.ascontiguousarray(v)
        aps[name] = nc.dram_tensor(f"in_{name}", v.shape, mybir.dt.from_np(v.dtype), kind="ExternalInput").ap()
    out = nc.dram_tensor("out", (N, D), F32, kind="ExternalOutput").ap()
    program(nc, aps, out)
    return run(nc, [arrays], core_ids=[0]).results[0]["out"]
```
